# Optimizing a Trainium2 kernel written in Bass

```python
import numpy as np
import jax
import jax.numpy as jnp

def _softmax(x, axis=-1):
    return jax.nn.softmax(x, axis=axis)

def _gelu(x):
    return jax.nn.gelu(x, approximate=True)

def _silu(x):
    return jax.nn.silu(x)

def _sigmoid(x):
    return jax.nn.sigmoid(x)

def _layernorm(x, axis=-1, eps=1e-05):
    m = jnp.mean(x, axis=axis, keepdims=True)
    v = jnp.var(x, axis=axis, keepdims=True)
    return (x - m) / jnp.sqrt(v + eps)

def _scatter_add(tgt, idx, src, axis=0):
    return tgt.at[idx].add(src)

def _segment_sum(src, seg, n):
    return jax.ops.segment_sum(src, seg, n)
kernel_name = 'mk_perceiver_d4_seqx_r8_a679fa'

def setup_inputs(seed: int=0):
    np.random.seed(seed)
    _w = jnp.asarray

    def _rec_inputs():
        import jax
        import jax.numpy as jnp
        _rk = jax.random.key(seed)
        x = -0.0002928 + 1 * jax.random.normal(jax.random.fold_in(_rk, 1), (128, 32, 128), jnp.float32)
        _lenS = 32 - jax.random.randint(jax.random.fold_in(_rk, 7), (128,), 0, max(1, 32 // 4) + 1, jnp.int32)
        _lenS2 = 257 - jax.random.randint(jax.random.fold_in(_rk, 8), (128,), 0, max(1, 257 // 4) + 1, jnp.int32)
        _ctx_1024P = jax.random.normal(jax.random.fold_in(_rk, 11), (128, 16, 128), jnp.float32)
        _ctx_1024c = jax.random.dirichlet(jax.random.fold_in(_rk, 511), 0.3 * jnp.ones((16,), jnp.float32), (128, 257))
        _ctx_1024t = jnp.einsum('bsk,bkd->bsd', _ctx_1024c, _ctx_1024P)
        _ctx_1024t = _ctx_1024t * jax.lax.rsqrt(jnp.mean(jnp.square(_ctx_1024t)) + 1e-12) * 0.953939
        ctx_1024 = 4.13588e-05 + 0.999923 * (_ctx_1024t + 0.3 * jax.random.normal(jax.random.fold_in(_rk, 611), (128, 257, 128), jnp.float32))
        _validS = jnp.arange(32)[None, :] < _lenS[:, None]
        _validS2 = jnp.arange(257)[None, :] < _lenS2[:, None]
        _causal = jnp.tril(jnp.ones((32, 32), dtype=bool))
        mask_1x1xSxS2_ik0 = jnp.where(jnp.broadcast_to(_validS2[0:1, None, None, :], (1, 1, 32, 257)), 0, 1).astype(jnp.int32)
        return (x, ctx_1024, mask_1x1xSxS2_ik0)
    x, ctx_1024, mask_1x1xSxS2_ik0 = _rec_inputs()

    def _L0_xattn_setup():
        import jax, jax.numpy as jnp
        import numpy as np
        HIDDEN = 128
        NUM_HEADS = 16
        HEAD_DIM = HIDDEN // NUM_HEADS
        key = jax.random.key(seed)
        k1, k2, k3, k4, k5, k6 = jax.random.split(key, 6)
        B, SQ, SKV = (4, 128, 256)
        s = HIDDEN ** (-0.5)
        return {'xq': jax.random.normal(k1, (B, SQ, HIDDEN), jnp.float32), 'xkv': jax.random.normal(k2, (B, SKV, HIDDEN), jnp.float32), 'Wq': jax.random.normal(k3, (HIDDEN, HIDDEN), jnp.float32) * s, 'Wkv': jax.random.normal(k4, (2 * HIDDEN, HIDDEN), jnp.float32) * s, 'Wout': jax.random.normal(k5, (HIDDEN, HIDDEN), jnp.float32) * s, 'bout': jax.random.normal(k6, (HIDDEN,), jnp.float32) * 0.01}
    _L0_xattn_all = _L0_xattn_setup()
    _L0_xattn_in = {k: v for k, v in _L0_xattn_all.items() if k in ('Wq', 'Wkv', 'Wout', 'bout')}
    del _L0_xattn_all

    def _L0_attn_setup():
        import jax, jax.numpy as jnp
        import numpy as np
        DIM = 128
        DEPTH = 6
        HEADS = 8
        FF_MULT = 4
        LN_EPS = 1e-05
        LEAKY_SLOPE = 0.01

        def _layernorm(x, w, b):
            m = jnp.mean(x, axis=-1, keepdims=True)
            v = jnp.mean(jnp.square(x - m), axis=-1, keepdims=True)
            return (x - m) * jax.lax.rsqrt(v + LN_EPS) * w + b

        def _linear_attn(q, k, v):
            q = jax.nn.softmax(q, axis=-1)
            k = jax.nn.softmax(k, axis=-2)
            context = jnp.einsum('bhnd,bhne->bhde', k, v)
            return jnp.einsum('bhnd,bhde->bhne', q, context)
        key = jax.random.key(seed)
        ks = jax.random.split(key, 12)
        b, t = (2, 512)
        s = 0.02
        return {'x': jax.random.normal(ks[0], (b, t, DIM), dtype=jnp.float32), 'ln1_w': jnp.ones((DEPTH, DIM), jnp.float32), 'ln1_b': jnp.zeros((DEPTH, DIM), jnp.float32), 'wq': jax.random.normal(ks[1], (DEPTH, DIM, DIM), jnp.float32) * s, 'wk': jax.random.normal(ks[2], (DEPTH, DIM, DIM), jnp.float32) * s, 'wv': jax.random.normal(ks[3], (DEPTH, DIM, DIM), jnp.float32) * s, 'wo': jax.random.normal(ks[4], (DEPTH, DIM, DIM), jnp.float32) * s, 'bo': jnp.zeros((DEPTH, DIM), jnp.float32), 'ln2_w': jnp.ones((DEPTH, DIM), jnp.float32), 'ln2_b': jnp.zeros((DEPTH, DIM), jnp.float32), 'w1': jax.random.normal(ks[5], (DEPTH, DIM, FF_MULT * DIM), jnp.float32) * s, 'w2': jax.random.normal(ks[6], (DEPTH, FF_MULT * DIM, DIM), jnp.float32) * s}
    _L0_attn_all = _L0_attn_setup()
    _L0_attn_in = {k: v for k, v in _L0_attn_all.items() if k in ('ln1_w', 'ln1_b', 'wq', 'wk', 'wv', 'wo', 'bo', 'ln2_w', 'ln2_b', 'w1', 'w2')}
    del _L0_attn_all

    def _L0_ffn_setup():
        import jax, jax.numpy as jnp
        import numpy as np
        LN_EPS = 1e-05

        def _swiglu(h, w_gate_up, w_down):
            gu = h @ w_gate_up.T
            gate, up = jnp.split(gu, 2, axis=-1)
            return jax.nn.silu(gate) * up @ w_down.T
        key = jax.random.key(seed)
        ks = jax.random.split(key, 6)
        d_model, d_ff, E = (128, 512, 8)
        shared_d_ff = d_ff // 4
        routed_d_ff = d_ff - shared_d_ff
        B, S = (4, 256)
        x = jax.random.normal(ks[0], (B, S, d_model), dtype=jnp.float32)
        ln_gamma = jnp.ones((d_model,), jnp.float32)
        ln_beta = jnp.zeros((d_model,), jnp.float32)
        router_w = jax.random.normal(ks[1], (E, d_model), jnp.float32) * 0.02
        gate_up_w = jax.random.normal(ks[2], (E, 2 * routed_d_ff, d_model), jnp.float32) * (1.0 / np.sqrt(d_model))
        down_w = jax.random.normal(ks[3], (E, d_model, routed_d_ff), jnp.float32) * (1.0 / np.sqrt(routed_d_ff))
        shared_gate_up_w = jax.random.normal(ks[4], (2 * shared_d_ff, d_model), jnp.float32) * (1.0 / np.sqrt(d_model))
        shared_down_w = jax.random.normal(ks[5], (d_model, shared_d_ff), jnp.float32) * (1.0 / np.sqrt(shared_d_ff))
        return dict(x=x, ln_gamma=ln_gamma, ln_beta=ln_beta, router_w=router_w, gate_up_w=gate_up_w, down_w=down_w, shared_gate_up_w=shared_gate_up_w, shared_down_w=shared_down_w)
    _L0_ffn_all = _L0_ffn_setup()
    _L0_ffn_in = {k: v for k, v in _L0_ffn_all.items() if k in ('ln_gamma', 'ln_beta', 'router_w', 'gate_up_w', 'down_w', 'shared_gate_up_w', 'shared_down_w')}
    del _L0_ffn_all

    def _L1_xattn_setup():
        import jax, jax.numpy as jnp
        import numpy as np
        N_EMBD = 128
        N_HEADS = 16
        HEAD_DIM = N_EMBD // N_HEADS
        key = jax.random.key(seed)
        ks = jax.random.split(key, 12)
        B, T, S, C = (2, 256, 256, N_EMBD)
        std = 1.0 / np.sqrt(C)
        inp = {'x': jax.random.normal(ks[0], (B, T, C), dtype=jnp.float32), 'context': jax.random.normal(ks[1], (B, S, C), dtype=jnp.float32), 'q_w': jax.random.uniform(ks[2], (C, C), minval=-std, maxval=std, dtype=jnp.float32), 'q_b': jax.random.uniform(ks[3], (C,), minval=-std, maxval=std, dtype=jnp.float32), 'k_w': jax.random.uniform(ks[4], (C, C), minval=-std, maxval=std, dtype=jnp.float32), 'k_b': jax.random.uniform(ks[5], (C,), minval=-std, maxval=std, dtype=jnp.float32), 'v_w': jax.random.uniform(ks[6], (C, C), minval=-std, maxval=std, dtype=jnp.float32), 'v_b': jax.random.uniform(ks[7], (C,), minval=-std, maxval=std, dtype=jnp.float32), 'o_w': jax.random.uniform(ks[8], (C, C), minval=-std, maxval=std, dtype=jnp.float32), 'o_b': jax.random.uniform(ks[9], (C,), minval=-std, maxval=std, dtype=jnp.float32)}
        return inp
    _L1_xattn_all = _L1_xattn_setup()
    _L1_xattn_in = {k: v for k, v in _L1_xattn_all.items() if k in ('q_w', 'q_b', 'k_w', 'k_b', 'v_w', 'v_b', 'o_w', 'o_b')}
    del _L1_xattn_all

    def _L1_attn_setup():
        import jax, jax.numpy as jnp
        import numpy as np
        EMBED_DIM = 128
        NUM_HEADS = 16
        BLOCK_SIZE = 128
        GLOBAL_EVERY = 24

        def make_block_sparse_mask(seq_len):
            bi = jnp.arange(seq_len) // BLOCK_SIZE
            is_global = bi % GLOBAL_EVERY == 0
            allowed = (bi[:, None] == bi[None, :]) | is_global[:, None] | is_global[None, :]
            return jnp.where(allowed, 0.0, -jnp.inf).astype(jnp.float32)
        key = jax.random.key(seed)
        k_x, k_w, k_wo = jax.random.split(key, 3)
        B, L, D = (1, 512, EMBED_DIM)
        x = jax.random.normal(k_x, (B, L, D), dtype=jnp.float32)
        w_qkv = jax.random.normal(k_w, (3 * D, D), dtype=jnp.float32) * 0.02
        b_qkv = jnp.zeros((3 * D,), dtype=jnp.float32)
        w_out = jax.random.normal(k_wo, (D, D), dtype=jnp.float32) * 0.02
        b_out = jnp.zeros((D,), dtype=jnp.float32)
        return {'x': x, 'w_qkv': w_qkv, 'b_qkv': b_qkv, 'w_out': w_out, 'b_out': b_out}
    _L1_attn_all = _L1_attn_setup()
    _L1_attn_in = {k: v for k, v in _L1_attn_all.items() if k in ('w_qkv', 'b_qkv', 'w_out', 'b_out')}
    del _L1_attn_all

    def _L1_ffn_setup():
        import jax, jax.numpy as jnp
        import numpy as np
        import math
        N_EXP = 8
        TOP_K = 2
        CAPACITY_FACTOR = 1.25

        def _capacity(num_tokens):
            cap = math.floor(TOP_K * CAPACITY_FACTOR * num_tokens / N_EXP)
            cap += cap % 2
            return int(cap)
        key = jax.random.key(seed)
        k1, k2, k3, k4 = jax.random.split(key, 4)
        B, C, d = (4, 128, 128)
        x = jax.random.normal(k1, (B, C, d), dtype=jnp.float32)
        w_g = jax.random.normal(k2, (d, N_EXP), dtype=jnp.float32) * 0.02
        c_fc = jax.random.normal(k3, (N_EXP, d, 4 * d), dtype=jnp.float32) * 0.02
        c_proj = jax.random.normal(k4, (N_EXP, 4 * d, d), dtype=jnp.float32) * 0.02
        return {'x': x, 'w_g': w_g, 'c_fc': c_fc, 'c_proj': c_proj}
    _L1_ffn_all = _L1_ffn_setup()
    _L1_ffn_in = {k: v for k, v in _L1_ffn_all.items() if k in ('w_g', 'c_fc', 'c_proj')}
    del _L1_ffn_all

    def _L2_xattn_setup():
        import jax, jax.numpy as jnp
        import numpy as np
        B, S, D, H = (2, 256, 128, 16)
        HD = D // H
        key = jax.random.key(seed)
        k1, k2, k3, k4, k5, k6, k7 = jax.random.split(key, 7)
        queries = jax.random.normal(k1, (B, S, D), dtype=jnp.float32)
        keys = jax.random.normal(k2, (B, S, D), dtype=jnp.float32)
        values = jax.random.normal(k3, (B, S, D), dtype=jnp.float32)
        scale = 0.02
        Wq = jax.random.normal(k4, (H, D, HD), dtype=jnp.float32) * scale
        Wk = jax.random.normal(k5, (H, D, HD), dtype=jnp.float32) * scale
        Wv = jax.random.normal(k6, (H, D, HD), dtype=jnp.float32) * scale
        Wo = jax.random.normal(k7, (D, D), dtype=jnp.float32) * scale
        return {'queries': queries, 'keys': keys, 'values': values, 'Wq': Wq, 'Wk': Wk, 'Wv': Wv, 'Wo': Wo}
    _L2_xattn_all = _L2_xattn_setup()
    _L2_xattn_in = {k: v for k, v in _L2_xattn_all.items() if k in ('Wq', 'Wk', 'Wv', 'Wo')}
    del _L2_xattn_all

    def _L2_attn_setup():
        import math
        import jax, jax.numpy as jnp
        import numpy as np
        HEADS = 8
        SCALE_BASE = 512.0
        GN_EPS = 1e-05

        def _gammas(heads):
            return 1.0 - np.exp(np.linspace(math.log(1.0 / 32.0), math.log(1.0 / 512.0), heads))

        def _xpos(x, downscale):
            N, S, d = x.shape
            half = d // 2
            scale = (jnp.arange(0, d, 2, dtype=jnp.float32) + 0.4 * d) / (1.4 * d)
            pos = jnp.arange(S, dtype=jnp.float32)
            sc = scale[None, :] ** (pos / SCALE_BASE)[:, None]
            inv_freq = 1.0 / 10000.0 ** (jnp.arange(half, dtype=jnp.float32) / half)
            sinusoid = pos[:, None] * inv_freq[None, :]
            sin, cos = (jnp.sin(sinusoid), jnp.cos(sinusoid))
            if downscale:
                sc = 1.0 / sc
            sin_s = jnp.repeat(sin * sc, 2, axis=-1)
            cos_s = jnp.repeat(cos * sc, 2, axis=-1)
            x1, x2 = (x[..., ::2], x[..., 1::2])
            rot = jnp.stack((-x2, x1), axis=-1).reshape(x.shape)
            return x * cos_s + rot * sin_s
        key = jax.random.key(seed)
        ks = jax.random.split(key, 6)
        B, S, H = (2, 256, 128)
        h = HEADS
        d = H // h
        X = jax.random.normal(ks[0], (B, S, H), dtype=jnp.float32)
        W_Q = jax.random.normal(ks[1], (h, d, d), dtype=jnp.float32) / d
        W_K = jax.random.normal(ks[2], (h, d, d), dtype=jnp.float32) / d
        W_V = jax.random.normal(ks[3], (h, d, d), dtype=jnp.float32) / d
        W_G = jax.random.normal(ks[4], (H, H), dtype=jnp.float32) / H
        W_O = jax.random.normal(ks[5], (H, H), dtype=jnp.float32) / H
        gn_weight = jnp.ones((H,), dtype=jnp.float32)
        gn_bias = jnp.zeros((H,), dtype=jnp.float32)
        return {'X': X, 'W_Q': W_Q, 'W_K': W_K, 'W_V': W_V, 'W_G': W_G, 'W_O': W_O, 'gn_weight': gn_weight, 'gn_bias': gn_bias}
    _L2_attn_all = _L2_attn_setup()
    _L2_attn_in = {k: v for k, v in _L2_attn_all.items() if k in ('W_Q', 'W_K', 'W_V', 'W_G', 'W_O', 'gn_weight', 'gn_bias')}
    del _L2_attn_all

    def _L2_ffn_setup():
        import jax, jax.numpy as jnp
        import numpy as np
        EPS = 1e-08

        def _ste(x, q):
            return x + jax.lax.stop_gradient(q - x)

        def quant_act_uint8(x):
            s = jax.lax.stop_gradient(jnp.maximum(jnp.max(x), EPS)) / 255.0
            q = jnp.clip(jnp.round(x / s), 0.0, 255.0) * s
            return (_ste(x, q), s)

        def quant_weight_int8_perchannel(w):
            s = jax.lax.stop_gradient(jnp.maximum(jnp.max(jnp.abs(w), axis=1, keepdims=True), EPS)) / 127.0
            q = jnp.clip(jnp.round(w / s), -128.0, 127.0) * s
            return (_ste(w, q), s[:, 0])

        def quant_bias_int32(b, s_in, s_w):
            s = jax.lax.stop_gradient(s_in * s_w)
            q = jnp.round(b / s) * s
            return _ste(b, q)

        def quant_linear(x, w, b):
            xq, s_in = quant_act_uint8(x)
            wq, s_w = quant_weight_int8_perchannel(w)
            bq = quant_bias_int32(b, s_in, s_w)
            return jnp.einsum('btd,fd->btf', xq, wq) + bq
        key = jax.random.key(seed)
        k1, k2, k3, k4, k5 = jax.random.split(key, 5)
        B, S, D, F = (4, 256, 128, 512)
        return {'x': jax.random.normal(k1, (B, S, D), dtype=jnp.float32), 'w1': jax.random.normal(k2, (F, D), dtype=jnp.float32) * (1.0 / np.sqrt(D)), 'b1': jax.random.normal(k3, (F,), dtype=jnp.float32) * 0.01, 'w2': jax.random.normal(k4, (D, F), dtype=jnp.float32) * (1.0 / np.sqrt(F)), 'b2': jax.random.normal(k5, (D,), dtype=jnp.float32) * 0.01}
    _L2_ffn_all = _L2_ffn_setup()
    _L2_ffn_in = {k: v for k, v in _L2_ffn_all.items() if k in ('w1', 'b1', 'w2', 'b2')}
    del _L2_ffn_all

    def _L3_xattn_setup():
        import jax, jax.numpy as jnp
        import numpy as np
        import math
        B, S, D, H = (2, 256, 128, 16)
        DK = D // H

        def _split_heads(x):
            b, s, _ = x.shape
            return x.reshape(b, s, H, DK).transpose(0, 2, 1, 3)
        key = jax.random.key(seed)
        ks = jax.random.split(key, 12)
        std = 1.0 / math.sqrt(D)
        inp = {'q': jax.random.normal(ks[0], (B, S, D), jnp.float32), 'k': jax.random.normal(ks[1], (B, S, D), jnp.float32), 'v': jax.random.normal(ks[2], (B, S, D), jnp.float32), 'mask': jnp.tril(jnp.ones((S, S), jnp.int32))[None, None, :, :], 'wq': jax.random.normal(ks[3], (D, D), jnp.float32) * std, 'bq': jax.random.normal(ks[4], (D,), jnp.float32) * std, 'wk': jax.random.normal(ks[5], (D, D), jnp.float32) * std, 'bk': jax.random.normal(ks[6], (D,), jnp.float32) * std, 'wv': jax.random.normal(ks[7], (D, D), jnp.float32) * std, 'bv': jax.random.normal(ks[8], (D,), jnp.float32) * std, 'wo': jax.random.normal(ks[9], (D, D), jnp.float32) * std, 'bo': jax.random.normal(ks[10], (D,), jnp.float32) * std}
        return inp
    _L3_xattn_all = _L3_xattn_setup()
    _L3_xattn_in = {k: v for k, v in _L3_xattn_all.items() if k in ('wq', 'bq', 'wk', 'bk', 'wv', 'bv', 'wo', 'bo')}
    del _L3_xattn_all

    def _L3_attn_setup():
        import jax, jax.numpy as jnp
        import numpy as np
        B, S, D, H, I, A = (2, 256, 128, 16, 512, 2)
        HD = D // H

        def _gen_param(sub, Wl, W, Bp):
            p = jnp.einsum('a...,a->...', sub, Wl[0])
            return jnp.tanh(p) * W + Bp

        def _student_linear(x, sub_w, Wl_w, W_w, B_w, sub_b, Wl_b, W_b, B_b):
            w = _gen_param(sub_w, Wl_w, W_w, B_w)
            b = _gen_param(sub_b, Wl_b, W_b, B_b)
            return x @ w.T + b

        def _layernorm(x, g, b, eps=1e-05):
            m = jnp.mean(x, axis=-1, keepdims=True)
            v = jnp.mean((x - m) ** 2, axis=-1, keepdims=True)
            return (x - m) * jax.lax.rsqrt(v + eps) * g + b

        def _gelu_new(x):
            c = 0.7978845608028654
            return 0.5 * x * (1.0 + jnp.tanh(c * (x + 0.044715 * x ** 3)))

        def _block(hs, ln1_g, ln1_b, ln2_g, ln2_b, *p):
            ca, cp, cf, cm = (p[0:8], p[8:16], p[16:24], p[24:32])
            b_, s_, d_ = hs.shape
            h = _layernorm(hs, ln1_g, ln1_b)
            qkv = _student_linear(h, *ca)
            q, k, v = jnp.split(qkv, 3, axis=-1)
            split = lambda t: t.reshape(b_, s_, H, HD).transpose(0, 2, 1, 3)
            q, k, v = (split(q), split(k), split(v))
            scores = jnp.einsum('bhqd,bhkd->bhqk', q, k) / float(HD) ** 0.5
            causal = jnp.tril(jnp.ones((s_, s_), dtype=bool))
            scores = jnp.where(causal, scores, jnp.asarray(-10000.0, scores.dtype))
            attn = jax.nn.softmax(scores, axis=-1)
            o = jnp.einsum('bhqk,bhkd->bhqd', attn, v)
            o = o.transpose(0, 2, 1, 3).reshape(b_, s_, d_)
            o = _student_linear(o, *cp)
            hs = hs + o
            h2 = _layernorm(hs, ln2_g, ln2_b)
            m = _student_linear(h2, *cf)
            m = _gelu_new(m)
            m = _student_linear(m, *cm)
            return hs + m
        key = jax.random.key(seed)
        ks = iter(jax.random.split(key, 32))

        def lin(out_f, in_f):
            return {'sub_w': jax.random.normal(next(ks), (A, out_f, in_f), jnp.float32) * 0.02, 'Wl_w': jax.random.normal(next(ks), (1, A), jnp.float32) * 0.5, 'W_w': jnp.ones((out_f, in_f), jnp.float32), 'B_w': jnp.zeros((out_f, in_f), jnp.float32), 'sub_b': jax.random.normal(next(ks), (A, out_f), jnp.float32) * 0.02, 'Wl_b': jax.random.normal(next(ks), (1, A), jnp.float32) * 0.5, 'W_b': jnp.ones((out_f,), jnp.float32), 'B_b': jnp.zeros((out_f,), jnp.float32)}
        inp = {'hs': jax.random.normal(next(ks), (B, S, D), jnp.float32)}
        for name, (o, i) in (('ca', (3 * D, D)), ('cp', (D, D)), ('cf', (I, D)), ('cm', (D, I))):
            for k2, v in lin(o, i).items():
                inp[name + '_' + k2] = v
        inp['ln1_g'] = jnp.ones((D,), jnp.float32)
        inp['ln1_b'] = jnp.zeros((D,), jnp.float32)
        inp['ln2_g'] = jnp.ones((D,), jnp.float32)
        inp['ln2_b'] = jnp.zeros((D,), jnp.float32)
        return inp
    _L3_attn_all = _L3_attn_setup()
    _L3_attn_in = {k: v for k, v in _L3_attn_all.items() if k in ('ln1_g', 'ln1_b', 'ln2_g', 'ln2_b', 'ca_sub_w', 'ca_Wl_w', 'ca_W_w', 'ca_B_w', 'ca_sub_b', 'ca_Wl_b', 'ca_W_b', 'ca_B_b', 'cp_sub_w', 'cp_Wl_w', 'cp_W_w', 'cp_B_w', 'cp_sub_b', 'cp_Wl_b', 'cp_W_b', 'cp_B_b', 'cf_sub_w', 'cf_Wl_w', 'cf_W_w', 'cf_B_w', 'cf_sub_b', 'cf_Wl_b', 'cf_W_b', 'cf_B_b', 'cm_sub_w', 'cm_Wl_w', 'cm_W_w', 'cm_B_w', 'cm_sub_b', 'cm_Wl_b', 'cm_W_b', 'cm_B_b')}
    del _L3_attn_all

    def _L3_ffn_setup():
        import jax, jax.numpy as jnp
        import numpy as np
        DIM = 128
        NQ = 16
        NKV = 4
        HD = DIM // NQ
        HID = 256
        E = 8
        B, S = (1, 128)
        EPS = 1e-06

        def rmsnorm(x, w):
            ms = jnp.mean(x * x, axis=-1, keepdims=True)
            return w * (x * jax.lax.rsqrt(ms + EPS))

        def rope_tables(seq_len, head_dim):
            inv_freq = 1.0 / 10000.0 ** (jnp.arange(0, head_dim, 2, dtype=jnp.float32) / head_dim)
            t = jnp.arange(seq_len, dtype=jnp.float32)
            freqs = jnp.einsum('i,j->ij', t, inv_freq)
            return (jnp.cos(freqs), jnp.sin(freqs))

        def apply_rope(x, cos, sin):
            c = cos[None, :, None, :]
            s = sin[None, :, None, :]
            half = x.shape[-1] // 2
            x1, x2 = (x[..., :half], x[..., half:])
            return jnp.concatenate([x1 * c - x2 * s, x1 * s + x2 * c], axis=-1)

        def _forward(x, ln1_w, ln2_w, Wq, bq, Wk, bk, Wv, bv, qn_w, kn_w, Wg, bg, Wo, bo, Wr, br, W1, b1, W2, b2):
            batch, seq, _ = x.shape
            cos, sin = rope_tables(seq, HD)
            h = rmsnorm(x, ln1_w)
            q = (h @ Wq + bq).reshape(batch, seq, NQ, HD)
            k = (h @ Wk + bk).reshape(batch, seq, NKV, HD)
            v = (h @ Wv + bv).reshape(batch, seq, NKV, HD)
            q = rmsnorm(apply_rope(q, cos, sin), qn_w)
            k = rmsnorm(apply_rope(k, cos, sin), kn_w)
            rep = NQ // NKV
            k = jnp.repeat(k, rep, axis=2)
            v = jnp.repeat(v, rep, axis=2)
            scores = jnp.einsum('bthd,bshd->bhts', q, k) / np.sqrt(HD)
            causal = jnp.tril(jnp.ones((seq, seq), dtype=bool))
            scores = jnp.where(causal[None, None], scores, -jnp.inf)
            attn = jax.nn.softmax(scores, axis=-1)
            out = jnp.einsum('bhts,bshd->bthd', attn, v)
            gate = jax.nn.sigmoid(out @ Wg + bg)
            out = (out * gate).reshape(batch, seq, DIM)
            x = x + out @ Wo + bo
            h2 = rmsnorm(x, ln2_w)
            logits = h2 @ Wr + br
            top1 = jnp.argmax(logits, axis=-1).reshape(-1)
            xt = h2.reshape(-1, DIM)
            u = jnp.einsum('td,edf->tef', xt, W1) + b1
            u1, u2 = (u[..., :HID], u[..., HID:])
            act = u1 * jax.nn.sigmoid(u2)
            y_all = jnp.einsum('teh,ehd->ted', act, W2) + b2
            y = jnp.take_along_axis(y_all, top1[:, None, None], axis=1)[:, 0, :]
            return x + y.reshape(batch, seq, DIM)
        key = jax.random.key(seed)
        ks = jax.random.split(key, 20)
        sc = lambda fan_in: 1.0 / np.sqrt(fan_in)
        d = {}
        d['x'] = jax.random.normal(ks[0], (B, S, DIM), dtype=jnp.float32)
        d['ln1_w'] = jnp.ones((DIM,), jnp.float32)
        d['ln2_w'] = jnp.ones((DIM,), jnp.float32)
        d['Wq'] = jax.random.normal(ks[1], (DIM, DIM), jnp.float32) * sc(DIM)
        d['bq'] = jnp.zeros((DIM,), jnp.float32)
        d['Wk'] = jax.random.normal(ks[2], (DIM, HD * NKV), jnp.float32) * sc(DIM)
        d['bk'] = jnp.zeros((HD * NKV,), jnp.float32)
        d['Wv'] = jax.random.normal(ks[3], (DIM, HD * NKV), jnp.float32) * sc(DIM)
        d['bv'] = jnp.zeros((HD * NKV,), jnp.float32)
        d['qn_w'] = jnp.ones((HD,), jnp.float32)
        d['kn_w'] = jnp.ones((HD,), jnp.float32)
        d['Wg'] = jax.random.normal(ks[4], (HD, HD), jnp.float32) * sc(HD)
        d['bg'] = jnp.zeros((HD,), jnp.float32)
        d['Wo'] = jax.random.normal(ks[5], (DIM, DIM), jnp.float32) * sc(DIM)
        d['bo'] = jnp.zeros((DIM,), jnp.float32)
        d['Wr'] = jax.random.normal(ks[6], (DIM, E), jnp.float32) * sc(DIM)
        d['br'] = jnp.zeros((E,), jnp.float32)
        d['W1'] = jax.random.normal(ks[7], (E, DIM, 2 * HID), jnp.float32) * sc(DIM)
        d['b1'] = jnp.zeros((E, 2 * HID), jnp.float32)
        d['W2'] = jax.random.normal(ks[8], (E, HID, DIM), jnp.float32) * sc(HID)
        d['b2'] = jnp.zeros((E, DIM), jnp.float32)
        return d
    _L3_ffn_all = _L3_ffn_setup()
    _L3_ffn_in = {k: v for k, v in _L3_ffn_all.items() if k in ('ln1_w', 'ln2_w', 'Wq', 'bq', 'Wk', 'bk', 'Wv', 'bv', 'qn_w', 'kn_w', 'Wg', 'bg', 'Wo', 'bo', 'Wr', 'br', 'W1', 'b1', 'W2', 'b2')}
    del _L3_ffn_all
    return {'x': x, 'ctx_1024': ctx_1024, 'mask_1x1xSxS2_ik0': mask_1x1xSxS2_ik0, 'L0_xattn_Wq': _L0_xattn_in['Wq'], 'L0_xattn_Wkv': _L0_xattn_in['Wkv'], 'L0_xattn_Wout': _L0_xattn_in['Wout'], 'L0_xattn_bout': _L0_xattn_in['bout'], 'L0_attn_ln1_w': _L0_attn_in['ln1_w'], 'L0_attn_ln1_b': _L0_attn_in['ln1_b'], 'L0_attn_wq': _L0_attn_in['wq'], 'L0_attn_wk': _L0_attn_in['wk'], 'L0_attn_wv': _L0_attn_in['wv'], 'L0_attn_wo': _L0_attn_in['wo'], 'L0_attn_bo': _L0_attn_in['bo'], 'L0_attn_ln2_w': _L0_attn_in['ln2_w'], 'L0_attn_ln2_b': _L0_attn_in['ln2_b'], 'L0_attn_w1': _L0_attn_in['w1'], 'L0_attn_w2': _L0_attn_in['w2'], 'L0_ffn_ln_gamma': _L0_ffn_in['ln_gamma'], 'L0_ffn_ln_beta': _L0_ffn_in['ln_beta'], 'L0_ffn_router_w': _L0_ffn_in['router_w'], 'L0_ffn_gate_up_w': _L0_ffn_in['gate_up_w'], 'L0_ffn_down_w': _L0_ffn_in['down_w'], 'L0_ffn_shared_gate_up_w': _L0_ffn_in['shared_gate_up_w'], 'L0_ffn_shared_down_w': _L0_ffn_in['shared_down_w'], 'L1_xattn_q_w': _L1_xattn_in['q_w'], 'L1_xattn_q_b': _L1_xattn_in['q_b'], 'L1_xattn_k_w': _L1_xattn_in['k_w'], 'L1_xattn_k_b': _L1_xattn_in['k_b'], 'L1_xattn_v_w': _L1_xattn_in['v_w'], 'L1_xattn_v_b': _L1_xattn_in['v_b'], 'L1_xattn_o_w': _L1_xattn_in['o_w'], 'L1_xattn_o_b': _L1_xattn_in['o_b'], 'L1_attn_w_qkv': _L1_attn_in['w_qkv'], 'L1_attn_b_qkv': _L1_attn_in['b_qkv'], 'L1_attn_w_out': _L1_attn_in['w_out'], 'L1_attn_b_out': _L1_attn_in['b_out'], 'L1_ffn_w_g': _L1_ffn_in['w_g'], 'L1_ffn_c_fc': _L1_ffn_in['c_fc'], 'L1_ffn_c_proj': _L1_ffn_in['c_proj'], 'L2_xattn_Wq': _L2_xattn_in['Wq'], 'L2_xattn_Wk': _L2_xattn_in['Wk'], 'L2_xattn_Wv': _L2_xattn_in['Wv'], 'L2_xattn_Wo': _L2_xattn_in['Wo'], 'L2_attn_W_Q': _L2_attn_in['W_Q'], 'L2_attn_W_K': _L2_attn_in['W_K'], 'L2_attn_W_V': _L2_attn_in['W_V'], 'L2_attn_W_G': _L2_attn_in['W_G'], 'L2_attn_W_O': _L2_attn_in['W_O'], 'L2_attn_gn_weight': _L2_attn_in['gn_weight'], 'L2_attn_gn_bias': _L2_attn_in['gn_bias'], 'L2_ffn_w1': _L2_ffn_in['w1'], 'L2_ffn_b1': _L2_ffn_in['b1'], 'L2_ffn_w2': _L2_ffn_in['w2'], 'L2_ffn_b2': _L2_ffn_in['b2'], 'L3_xattn_wq': _L3_xattn_in['wq'], 'L3_xattn_bq': _L3_xattn_in['bq'], 'L3_xattn_wk': _L3_xattn_in['wk'], 'L3_xattn_bk': _L3_xattn_in['bk'], 'L3_xattn_wv': _L3_xattn_in['wv'], 'L3_xattn_bv': _L3_xattn_in['bv'], 'L3_xattn_wo': _L3_xattn_in['wo'], 'L3_xattn_bo': _L3_xattn_in['bo'], 'L3_attn_ln1_g': _L3_attn_in['ln1_g'], 'L3_attn_ln1_b': _L3_attn_in['ln1_b'], 'L3_attn_ln2_g': _L3_attn_in['ln2_g'], 'L3_attn_ln2_b': _L3_attn_in['ln2_b'], 'L3_attn_ca_sub_w': _L3_attn_in['ca_sub_w'], 'L3_attn_ca_Wl_w': _L3_attn_in['ca_Wl_w'], 'L3_attn_ca_W_w': _L3_attn_in['ca_W_w'], 'L3_attn_ca_B_w': _L3_attn_in['ca_B_w'], 'L3_attn_ca_sub_b': _L3_attn_in['ca_sub_b'], 'L3_attn_ca_Wl_b': _L3_attn_in['ca_Wl_b'], 'L3_attn_ca_W_b': _L3_attn_in['ca_W_b'], 'L3_attn_ca_B_b': _L3_attn_in['ca_B_b'], 'L3_attn_cp_sub_w': _L3_attn_in['cp_sub_w'], 'L3_attn_cp_Wl_w': _L3_attn_in['cp_Wl_w'], 'L3_attn_cp_W_w': _L3_attn_in['cp_W_w'], 'L3_attn_cp_B_w': _L3_attn_in['cp_B_w'], 'L3_attn_cp_sub_b': _L3_attn_in['cp_sub_b'], 'L3_attn_cp_Wl_b': _L3_attn_in['cp_Wl_b'], 'L3_attn_cp_W_b': _L3_attn_in['cp_W_b'], 'L3_attn_cp_B_b': _L3_attn_in['cp_B_b'], 'L3_attn_cf_sub_w': _L3_attn_in['cf_sub_w'], 'L3_attn_cf_Wl_w': _L3_attn_in['cf_Wl_w'], 'L3_attn_cf_W_w': _L3_attn_in['cf_W_w'], 'L3_attn_cf_B_w': _L3_attn_in['cf_B_w'], 'L3_attn_cf_sub_b': _L3_attn_in['cf_sub_b'], 'L3_attn_cf_Wl_b': _L3_attn_in['cf_Wl_b'], 'L3_attn_cf_W_b': _L3_attn_in['cf_W_b'], 'L3_attn_cf_B_b': _L3_attn_in['cf_B_b'], 'L3_attn_cm_sub_w': _L3_attn_in['cm_sub_w'], 'L3_attn_cm_Wl_w': _L3_attn_in['cm_Wl_w'], 'L3_attn_cm_W_w': _L3_attn_in['cm_W_w'], 'L3_attn_cm_B_w': _L3_attn_in['cm_B_w'], 'L3_attn_cm_sub_b': _L3_attn_in['cm_sub_b'], 'L3_attn_cm_Wl_b': _L3_attn_in['cm_Wl_b'], 'L3_attn_cm_W_b': _L3_attn_in['cm_W_b'], 'L3_attn_cm_B_b': _L3_attn_in['cm_B_b'], 'L3_ffn_ln1_w': _L3_ffn_in['ln1_w'], 'L3_ffn_ln2_w': _L3_ffn_in['ln2_w'], 'L3_ffn_Wq': _L3_ffn_in['Wq'], 'L3_ffn_bq': _L3_ffn_in['bq'], 'L3_ffn_Wk': _L3_ffn_in['Wk'], 'L3_ffn_bk': _L3_ffn_in['bk'], 'L3_ffn_Wv': _L3_ffn_in['Wv'], 'L3_ffn_bv': _L3_ffn_in['bv'], 'L3_ffn_qn_w': _L3_ffn_in['qn_w'], 'L3_ffn_kn_w': _L3_ffn_in['kn_w'], 'L3_ffn_Wg': _L3_ffn_in['Wg'], 'L3_ffn_bg': _L3_ffn_in['bg'], 'L3_ffn_Wo': _L3_ffn_in['Wo'], 'L3_ffn_bo': _L3_ffn_in['bo'], 'L3_ffn_Wr': _L3_ffn_in['Wr'], 'L3_ffn_br': _L3_ffn_in['br'], 'L3_ffn_W1': _L3_ffn_in['W1'], 'L3_ffn_b1': _L3_ffn_in['b1'], 'L3_ffn_W2': _L3_ffn_in['W2'], 'L3_ffn_b2': _L3_ffn_in['b2']}

def reference(x, ctx_1024, mask_1x1xSxS2_ik0, L0_xattn_Wq, L0_xattn_Wkv, L0_xattn_Wout, L0_xattn_bout, L0_attn_ln1_w, L0_attn_ln1_b, L0_attn_wq, L0_attn_wk, L0_attn_wv, L0_attn_wo, L0_attn_bo, L0_attn_ln2_w, L0_attn_ln2_b, L0_attn_w1, L0_attn_w2, L0_ffn_ln_gamma, L0_ffn_ln_beta, L0_ffn_router_w, L0_ffn_gate_up_w, L0_ffn_down_w, L0_ffn_shared_gate_up_w, L0_ffn_shared_down_w, L1_xattn_q_w, L1_xattn_q_b, L1_xattn_k_w, L1_xattn_k_b, L1_xattn_v_w, L1_xattn_v_b, L1_xattn_o_w, L1_xattn_o_b, L1_attn_w_qkv, L1_attn_b_qkv, L1_attn_w_out, L1_attn_b_out, L1_ffn_w_g, L1_ffn_c_fc, L1_ffn_c_proj, L2_xattn_Wq, L2_xattn_Wk, L2_xattn_Wv, L2_xattn_Wo, L2_attn_W_Q, L2_attn_W_K, L2_attn_W_V, L2_attn_W_G, L2_attn_W_O, L2_attn_gn_weight, L2_attn_gn_bias, L2_ffn_w1, L2_ffn_b1, L2_ffn_w2, L2_ffn_b2, L3_xattn_wq, L3_xattn_bq, L3_xattn_wk, L3_xattn_bk, L3_xattn_wv, L3_xattn_bv, L3_xattn_wo, L3_xattn_bo, L3_attn_ln1_g, L3_attn_ln1_b, L3_attn_ln2_g, L3_attn_ln2_b, L3_attn_ca_sub_w, L3_attn_ca_Wl_w, L3_attn_ca_W_w, L3_attn_ca_B_w, L3_attn_ca_sub_b, L3_attn_ca_Wl_b, L3_attn_ca_W_b, L3_attn_ca_B_b, L3_attn_cp_sub_w, L3_attn_cp_Wl_w, L3_attn_cp_W_w, L3_attn_cp_B_w, L3_attn_cp_sub_b, L3_attn_cp_Wl_b, L3_attn_cp_W_b, L3_attn_cp_B_b, L3_attn_cf_sub_w, L3_attn_cf_Wl_w, L3_attn_cf_W_w, L3_attn_cf_B_w, L3_attn_cf_sub_b, L3_attn_cf_Wl_b, L3_attn_cf_W_b, L3_attn_cf_B_b, L3_attn_cm_sub_w, L3_attn_cm_Wl_w, L3_attn_cm_W_w, L3_attn_cm_B_w, L3_attn_cm_sub_b, L3_attn_cm_Wl_b, L3_attn_cm_W_b, L3_attn_cm_B_b, L3_ffn_ln1_w, L3_ffn_ln2_w, L3_ffn_Wq, L3_ffn_bq, L3_ffn_Wk, L3_ffn_bk, L3_ffn_Wv, L3_ffn_bv, L3_ffn_qn_w, L3_ffn_kn_w, L3_ffn_Wg, L3_ffn_bg, L3_ffn_Wo, L3_ffn_bo, L3_ffn_Wr, L3_ffn_br, L3_ffn_W1, L3_ffn_b1, L3_ffn_W2, L3_ffn_b2):
    import jax
    import jax.numpy as jnp

    def _L0_xattn_ref(xq, xkv, Wq, Wkv, Wout, bout):
        import jax, jax.numpy as jnp
        import numpy as np
        HIDDEN = 128
        NUM_HEADS = 16
        HEAD_DIM = HIDDEN // NUM_HEADS
        B, SQ, H = xq.shape
        SKV = xkv.shape[1]
        scale = HEAD_DIM ** (-0.5)
        q = (xq @ Wq.T).reshape(B, SQ, NUM_HEADS, HEAD_DIM)
        kv = (xkv @ Wkv.T).reshape(B, SKV, 2, NUM_HEADS, HEAD_DIM)
        k, v = (kv[:, :, 0], kv[:, :, 1])
        att = jax.nn.softmax(jnp.einsum('bxhd,byhd->bhxy', q, k) * scale, axis=-1)
        x = jnp.einsum('bhxy,byhd->bxhd', att, v).reshape(B, SQ, H)
        return x @ Wout.T + bout

    def _L0_attn_ref(x, ln1_w, ln1_b, wq, wk, wv, wo, bo, ln2_w, ln2_b, w1, w2):
        import jax, jax.numpy as jnp
        import numpy as np
        DIM = 128
        DEPTH = 6
        HEADS = 8
        FF_MULT = 4
        LN_EPS = 1e-05
        LEAKY_SLOPE = 0.01

        def _layernorm(x, w, b):
            m = jnp.mean(x, axis=-1, keepdims=True)
            v = jnp.mean(jnp.square(x - m), axis=-1, keepdims=True)
            return (x - m) * jax.lax.rsqrt(v + LN_EPS) * w + b

        def _linear_attn(q, k, v):
            q = jax.nn.softmax(q, axis=-1)
            k = jax.nn.softmax(k, axis=-2)
            context = jnp.einsum('bhnd,bhne->bhde', k, v)
            return jnp.einsum('bhnd,bhde->bhne', q, context)
        b, t, e = x.shape
        h, dh = (HEADS, e // HEADS)
        for i in range(DEPTH):
            xn = _layernorm(x, ln1_w[i], ln1_b[i])
            q = (xn @ wq[i]).reshape(b, t, h, dh).transpose(0, 2, 1, 3)
            k = (xn @ wk[i]).reshape(b, t, h, dh).transpose(0, 2, 1, 3)
            v = (xn @ wv[i]).reshape(b, t, h, dh).transpose(0, 2, 1, 3)
            attn = _linear_attn(q, k, v)
            attn = attn.transpose(0, 2, 1, 3).reshape(b, t, e)
            x = attn @ wo[i] + bo[i] + x
            xn = _layernorm(x, ln2_w[i], ln2_b[i])
            hdn = xn @ w1[i]
            hdn = jnp.where(hdn >= 0, hdn, LEAKY_SLOPE * hdn)
            x = hdn @ w2[i] + x
        return x

    def _L0_ffn_ref(x, ln_gamma, ln_beta, router_w, gate_up_w, down_w, shared_gate_up_w, shared_down_w):
        import jax, jax.numpy as jnp
        import numpy as np
        LN_EPS = 1e-05

        def _swiglu(h, w_gate_up, w_down):
            gu = h @ w_gate_up.T
            gate, up = jnp.split(gu, 2, axis=-1)
            return jax.nn.silu(gate) * up @ w_down.T
        B, S, D = x.shape
        E = router_w.shape[0]
        top_k = 2
        xt = x.reshape(-1, D)
        mu = jnp.mean(xt, axis=-1, keepdims=True)
        var = jnp.mean(jnp.square(xt - mu), axis=-1, keepdims=True)
        normed = (xt - mu) * jax.lax.rsqrt(var + LN_EPS) * ln_gamma + ln_beta
        logits = normed.astype(jnp.float32) @ router_w.T
        probs = jax.nn.softmax(logits, axis=-1)
        top_v, top_i = jax.lax.top_k(probs, top_k)
        gates = jax.nn.softmax(top_v, axis=-1)
        comb = jnp.sum(jax.nn.one_hot(top_i, E, dtype=gates.dtype) * gates[..., None], axis=1)
        out = jnp.zeros_like(normed)
        for e in range(E):
            y = _swiglu(normed, gate_up_w[e], down_w[e])
            out = out + comb[:, e, None] * y
        out = out + _swiglu(normed, shared_gate_up_w, shared_down_w)
        return out.reshape(B, S, D)

    def _L1_xattn_ref(x, context, q_w, q_b, k_w, k_b, v_w, v_b, o_w, o_b):
        import jax, jax.numpy as jnp
        import numpy as np
        N_EMBD = 128
        N_HEADS = 16
        HEAD_DIM = N_EMBD // N_HEADS
        B, T, C = x.shape
        S = context.shape[1]
        H, D = (N_HEADS, HEAD_DIM)
        q = (x @ q_w + q_b).reshape(B, T, H, D).transpose(0, 2, 1, 3)
        k = (context @ k_w + k_b).reshape(B, S, H, D).transpose(0, 2, 1, 3)
        v = (context @ v_w + v_b).reshape(B, S, H, D).transpose(0, 2, 1, 3)
        att = jnp.einsum('bhtd,bhsd->bhts', q, k) / jnp.sqrt(jnp.float32(D))
        causal = jnp.tril(jnp.ones((T, S), dtype=bool))
        att = jnp.where(causal[None, None, :, :], att, -jnp.inf)
        att = jax.nn.softmax(att, axis=-1)
        y = jnp.einsum('bhts,bhsd->bhtd', att, v)
        y = y.transpose(0, 2, 1, 3).reshape(B, T, C)
        return y @ o_w + o_b

    def _L1_attn_ref(x, w_qkv, b_qkv, w_out, b_out):
        import jax, jax.numpy as jnp
        import numpy as np
        EMBED_DIM = 128
        NUM_HEADS = 16
        BLOCK_SIZE = 128
        GLOBAL_EVERY = 24

        def make_block_sparse_mask(seq_len):
            bi = jnp.arange(seq_len) // BLOCK_SIZE
            is_global = bi % GLOBAL_EVERY == 0
            allowed = (bi[:, None] == bi[None, :]) | is_global[:, None] | is_global[None, :]
            return jnp.where(allowed, 0.0, -jnp.inf).astype(jnp.float32)
        B, L, D = x.shape
        H = NUM_HEADS
        hd = D // H
        mask = make_block_sparse_mask(L)
        qkv = x @ w_qkv.T + b_qkv
        q, k, v = jnp.split(qkv, 3, axis=-1)
        q = q.reshape(B, L, H, hd).transpose(0, 2, 1, 3)
        k = k.reshape(B, L, H, hd).transpose(0, 2, 1, 3)
        v = v.reshape(B, L, H, hd).transpose(0, 2, 1, 3)
        scale = 1.0 / jnp.sqrt(jnp.asarray(hd, dtype=x.dtype))
        scores = jnp.einsum('bhqd,bhkd->bhqk', q * scale, k) + mask
        attn = jax.nn.softmax(scores, axis=-1)
        out = jnp.einsum('bhqk,bhkd->bhqd', attn, v)
        out = out.transpose(0, 2, 1, 3).reshape(B, L, D)
        return out @ w_out.T + b_out

    def _L1_ffn_ref(x, w_g, c_fc, c_proj):
        import jax, jax.numpy as jnp
        import numpy as np
        import math
        N_EXP = 8
        TOP_K = 2
        CAPACITY_FACTOR = 1.25

        def _capacity(num_tokens):
            cap = math.floor(TOP_K * CAPACITY_FACTOR * num_tokens / N_EXP)
            cap += cap % 2
            return int(cap)
        B, C, d = x.shape
        T = B * C
        cap = _capacity(T)
        xt = x.reshape(T, d)
        logits = xt @ w_g
        top_v, top_i = jax.lax.top_k(logits, TOP_K)
        full = jnp.full_like(logits, -jnp.inf)
        full = full.at[jnp.arange(T)[:, None], top_i].set(top_v)
        probs = jax.nn.softmax(full, axis=-1)
        exp_mask = jax.nn.one_hot(top_i, N_EXP, dtype=jnp.int32)
        exp_mask = jnp.transpose(exp_mask, (1, 0, 2))
        exp_rank = jnp.cumsum(exp_mask.reshape(TOP_K * T, N_EXP), axis=0) - 1
        exp_rank = exp_rank.reshape(TOP_K, T, N_EXP)
        exp_mask = exp_mask * (exp_rank < cap).astype(jnp.int32)
        exp_rank = jnp.sum(exp_mask * exp_rank, axis=-1)
        exp_weights = exp_mask.astype(x.dtype) * probs[None]
        rank_oh = jax.nn.one_hot(exp_rank, cap, dtype=x.dtype)
        cb_weight = jnp.einsum('kte,ktc->tec', exp_weights, rank_oh)
        sec_mask = (cb_weight != 0).astype(x.dtype)
        exp_batches = jnp.einsum('tec,td->ecd', sec_mask, xt)
        h = jax.nn.gelu(jnp.einsum('ecd,edf->ecf', exp_batches, c_fc), approximate=False)
        exp_out = jnp.einsum('ecf,efd->ecd', h, c_proj)
        out = cb_weight.reshape(T, N_EXP * cap) @ exp_out.reshape(N_EXP * cap, d)
        return out.reshape(B, C, d)

    def _L2_xattn_ref(queries, keys, values, Wq, Wk, Wv, Wo):
        import jax, jax.numpy as jnp
        import numpy as np
        B, S, D, H = (2, 256, 128, 16)
        HD = D // H
        q = jnp.einsum('bsd,hde->bhse', queries, Wq)
        k = jnp.einsum('bsd,hde->bhse', keys, Wk)
        v = jnp.einsum('bsd,hde->bhse', values, Wv)
        inv_sqrt_hd = 1.0 / jnp.sqrt(jnp.asarray(HD, dtype=q.dtype))
        scores = jnp.einsum('bhse,bhte->bhst', q, k) * inv_sqrt_hd
        attn = jax.nn.softmax(scores, axis=-1)
        out = jnp.einsum('bhst,bhte->bhse', attn, v)
        out = out.transpose(0, 2, 1, 3).reshape(out.shape[0], out.shape[2], -1)
        return jnp.einsum('bsd,ed->bse', out, Wo)

    def _L2_attn_ref(X, W_Q, W_K, W_V, W_G, W_O, gn_weight, gn_bias):
        import math
        import jax, jax.numpy as jnp
        import numpy as np
        HEADS = 8
        SCALE_BASE = 512.0
        GN_EPS = 1e-05

        def _gammas(heads):
            return 1.0 - np.exp(np.linspace(math.log(1.0 / 32.0), math.log(1.0 / 512.0), heads))

        def _xpos(x, downscale):
            N, S, d = x.shape
            half = d // 2
            scale = (jnp.arange(0, d, 2, dtype=jnp.float32) + 0.4 * d) / (1.4 * d)
            pos = jnp.arange(S, dtype=jnp.float32)
            sc = scale[None, :] ** (pos / SCALE_BASE)[:, None]
            inv_freq = 1.0 / 10000.0 ** (jnp.arange(half, dtype=jnp.float32) / half)
            sinusoid = pos[:, None] * inv_freq[None, :]
            sin, cos = (jnp.sin(sinusoid), jnp.cos(sinusoid))
            if downscale:
                sc = 1.0 / sc
            sin_s = jnp.repeat(sin * sc, 2, axis=-1)
            cos_s = jnp.repeat(cos * sc, 2, axis=-1)
            x1, x2 = (x[..., ::2], x[..., 1::2])
            rot = jnp.stack((-x2, x1), axis=-1).reshape(x.shape)
            return x * cos_s + rot * sin_s
        B, S, H = X.shape
        h = HEADS
        d = H // h
        gammas = jnp.asarray(_gammas(h), dtype=X.dtype)
        Xh = X.reshape(B, S, h, d)
        Q = jnp.einsum('bshd,hde->bhse', Xh, W_Q)
        K = jnp.einsum('bshd,hde->bhse', Xh, W_K)
        V = jnp.einsum('bshd,hde->bhse', Xh, W_V)
        Q = _xpos(Q.reshape(B * h, S, d), downscale=False).reshape(B, h, S, d)
        K = _xpos(K.reshape(B * h, S, d), downscale=True).reshape(B, h, S, d)
        n = jnp.arange(S)
        diff = n[:, None] - n[None, :]
        causal = diff >= 0
        D = gammas[:, None, None] ** jnp.where(causal, diff, 0).astype(X.dtype) * causal[None].astype(X.dtype)
        att = jnp.einsum('bhsd,bhtd->bhst', Q, K) * D[None]
        Y = jnp.einsum('bhst,bhtd->bshd', att, V).reshape(B, S, H)
        Yg = Y.reshape(B * S, h, d)
        mu = Yg.mean(axis=-1, keepdims=True)
        var = Yg.var(axis=-1, keepdims=True)
        Yn = ((Yg - mu) / jnp.sqrt(var + GN_EPS)).reshape(B * S, H)
        Yn = (Yn * gn_weight + gn_bias).reshape(B, S, H)
        G = X @ W_G
        return G * jax.nn.sigmoid(G) * Yn @ W_O

    def _L2_ffn_ref(x, w1, b1, w2, b2):
        import jax, jax.numpy as jnp
        import numpy as np
        EPS = 1e-08

        def _ste(x, q):
            return x + jax.lax.stop_gradient(q - x)

        def quant_act_uint8(x):
            s = jax.lax.stop_gradient(jnp.maximum(jnp.max(x), EPS)) / 255.0
            q = jnp.clip(jnp.round(x / s), 0.0, 255.0) * s
            return (_ste(x, q), s)

        def quant_weight_int8_perchannel(w):
            s = jax.lax.stop_gradient(jnp.maximum(jnp.max(jnp.abs(w), axis=1, keepdims=True), EPS)) / 127.0
            q = jnp.clip(jnp.round(w / s), -128.0, 127.0) * s
            return (_ste(w, q), s[:, 0])

        def quant_bias_int32(b, s_in, s_w):
            s = jax.lax.stop_gradient(s_in * s_w)
            q = jnp.round(b / s) * s
            return _ste(b, q)

        def quant_linear(x, w, b):
            xq, s_in = quant_act_uint8(x)
            wq, s_w = quant_weight_int8_perchannel(w)
            bq = quant_bias_int32(b, s_in, s_w)
            return jnp.einsum('btd,fd->btf', xq, wq) + bq
        h = jax.nn.relu(quant_linear(x, w1, b1))
        return quant_linear(h, w2, b2)

    def _L3_xattn_ref(q, k, v, mask, wq, bq, wk, bk, wv, bv, wo, bo):
        import jax, jax.numpy as jnp
        import numpy as np
        import math
        B, S, D, H = (2, 256, 128, 16)
        DK = D // H

        def _split_heads(x):
            b, s, _ = x.shape
            return x.reshape(b, s, H, DK).transpose(0, 2, 1, 3)
        query = _split_heads(q @ wq.T + bq)
        key_h = _split_heads(k @ wk.T + bk)
        value = _split_heads(v @ wv.T + bv)
        scale = 1.0 / math.sqrt(DK)
        scores = jnp.einsum('bhqd,bhkd->bhqk', query, key_h) * scale
        scores = jnp.where(mask == 0, jnp.float32(-1000000000.0), scores)
        attn = jax.nn.softmax(scores, axis=-1)
        x = jnp.einsum('bhqk,bhkd->bhqd', attn, value)
        x = x.transpose(0, 2, 1, 3).reshape(q.shape[0], -1, H * DK)
        return x @ wo.T + bo

    def _L3_attn_ref(hs, ln1_g, ln1_b, ln2_g, ln2_b, ca_sub_w, ca_Wl_w, ca_W_w, ca_B_w, ca_sub_b, ca_Wl_b, ca_W_b, ca_B_b, cp_sub_w, cp_Wl_w, cp_W_w, cp_B_w, cp_sub_b, cp_Wl_b, cp_W_b, cp_B_b, cf_sub_w, cf_Wl_w, cf_W_w, cf_B_w, cf_sub_b, cf_Wl_b, cf_W_b, cf_B_b, cm_sub_w, cm_Wl_w, cm_W_w, cm_B_w, cm_sub_b, cm_Wl_b, cm_W_b, cm_B_b):
        import jax, jax.numpy as jnp
        import numpy as np
        B, S, D, H, I, A = (2, 256, 128, 16, 512, 2)
        HD = D // H

        def _gen_param(sub, Wl, W, Bp):
            p = jnp.einsum('a...,a->...', sub, Wl[0])
            return jnp.tanh(p) * W + Bp

        def _student_linear(x, sub_w, Wl_w, W_w, B_w, sub_b, Wl_b, W_b, B_b):
            w = _gen_param(sub_w, Wl_w, W_w, B_w)
            b = _gen_param(sub_b, Wl_b, W_b, B_b)
            return x @ w.T + b

        def _layernorm(x, g, b, eps=1e-05):
            m = jnp.mean(x, axis=-1, keepdims=True)
            v = jnp.mean((x - m) ** 2, axis=-1, keepdims=True)
            return (x - m) * jax.lax.rsqrt(v + eps) * g + b

        def _gelu_new(x):
            c = 0.7978845608028654
            return 0.5 * x * (1.0 + jnp.tanh(c * (x + 0.044715 * x ** 3)))

        def _block(hs, ln1_g, ln1_b, ln2_g, ln2_b, *p):
            ca, cp, cf, cm = (p[0:8], p[8:16], p[16:24], p[24:32])
            b_, s_, d_ = hs.shape
            h = _layernorm(hs, ln1_g, ln1_b)
            qkv = _student_linear(h, *ca)
            q, k, v = jnp.split(qkv, 3, axis=-1)
            split = lambda t: t.reshape(b_, s_, H, HD).transpose(0, 2, 1, 3)
            q, k, v = (split(q), split(k), split(v))
            scores = jnp.einsum('bhqd,bhkd->bhqk', q, k) / float(HD) ** 0.5
            causal = jnp.tril(jnp.ones((s_, s_), dtype=bool))
            scores = jnp.where(causal, scores, jnp.asarray(-10000.0, scores.dtype))
            attn = jax.nn.softmax(scores, axis=-1)
            o = jnp.einsum('bhqk,bhkd->bhqd', attn, v)
            o = o.transpose(0, 2, 1, 3).reshape(b_, s_, d_)
            o = _student_linear(o, *cp)
            hs = hs + o
            h2 = _layernorm(hs, ln2_g, ln2_b)
            m = _student_linear(h2, *cf)
            m = _gelu_new(m)
            m = _student_linear(m, *cm)
            return hs + m
        return _block(hs, ln1_g, ln1_b, ln2_g, ln2_b, ca_sub_w, ca_Wl_w, ca_W_w, ca_B_w, ca_sub_b, ca_Wl_b, ca_W_b, ca_B_b, cp_sub_w, cp_Wl_w, cp_W_w, cp_B_w, cp_sub_b, cp_Wl_b, cp_W_b, cp_B_b, cf_sub_w, cf_Wl_w, cf_W_w, cf_B_w, cf_sub_b, cf_Wl_b, cf_W_b, cf_B_b, cm_sub_w, cm_Wl_w, cm_W_w, cm_B_w, cm_sub_b, cm_Wl_b, cm_W_b, cm_B_b)

    def _L3_ffn_ref(x, ln1_w, ln2_w, Wq, bq, Wk, bk, Wv, bv, qn_w, kn_w, Wg, bg, Wo, bo, Wr, br, W1, b1, W2, b2):
        import jax, jax.numpy as jnp
        import numpy as np
        DIM = 128
        NQ = 16
        NKV = 4
        HD = DIM // NQ
        HID = 256
        E = 8
        B, S = (1, 128)
        EPS = 1e-06

        def rmsnorm(x, w):
            ms = jnp.mean(x * x, axis=-1, keepdims=True)
            return w * (x * jax.lax.rsqrt(ms + EPS))

        def rope_tables(seq_len, head_dim):
            inv_freq = 1.0 / 10000.0 ** (jnp.arange(0, head_dim, 2, dtype=jnp.float32) / head_dim)
            t = jnp.arange(seq_len, dtype=jnp.float32)
            freqs = jnp.einsum('i,j->ij', t, inv_freq)
            return (jnp.cos(freqs), jnp.sin(freqs))

        def apply_rope(x, cos, sin):
            c = cos[None, :, None, :]
            s = sin[None, :, None, :]
            half = x.shape[-1] // 2
            x1, x2 = (x[..., :half], x[..., half:])
            return jnp.concatenate([x1 * c - x2 * s, x1 * s + x2 * c], axis=-1)

        def _forward(x, ln1_w, ln2_w, Wq, bq, Wk, bk, Wv, bv, qn_w, kn_w, Wg, bg, Wo, bo, Wr, br, W1, b1, W2, b2):
            batch, seq, _ = x.shape
            cos, sin = rope_tables(seq, HD)
            h = rmsnorm(x, ln1_w)
            q = (h @ Wq + bq).reshape(batch, seq, NQ, HD)
            k = (h @ Wk + bk).reshape(batch, seq, NKV, HD)
            v = (h @ Wv + bv).reshape(batch, seq, NKV, HD)
            q = rmsnorm(apply_rope(q, cos, sin), qn_w)
            k = rmsnorm(apply_rope(k, cos, sin), kn_w)
            rep = NQ // NKV
            k = jnp.repeat(k, rep, axis=2)
            v = jnp.repeat(v, rep, axis=2)
            scores = jnp.einsum('bthd,bshd->bhts', q, k) / np.sqrt(HD)
            causal = jnp.tril(jnp.ones((seq, seq), dtype=bool))
            scores = jnp.where(causal[None, None], scores, -jnp.inf)
            attn = jax.nn.softmax(scores, axis=-1)
            out = jnp.einsum('bhts,bshd->bthd', attn, v)
            gate = jax.nn.sigmoid(out @ Wg + bg)
            out = (out * gate).reshape(batch, seq, DIM)
            x = x + out @ Wo + bo
            h2 = rmsnorm(x, ln2_w)
            logits = h2 @ Wr + br
            top1 = jnp.argmax(logits, axis=-1).reshape(-1)
            xt = h2.reshape(-1, DIM)
            u = jnp.einsum('td,edf->tef', xt, W1) + b1
            u1, u2 = (u[..., :HID], u[..., HID:])
            act = u1 * jax.nn.sigmoid(u2)
            y_all = jnp.einsum('teh,ehd->ted', act, W2) + b2
            y = jnp.take_along_axis(y_all, top1[:, None, None], axis=1)[:, 0, :]
            return x + y.reshape(batch, seq, DIM)
        return _forward(x, ln1_w, ln2_w, Wq, bq, Wk, bk, Wv, bv, qn_w, kn_w, Wg, bg, Wo, bo, Wr, br, W1, b1, W2, b2)
    x = x + _L0_xattn_ref(_layernorm(x, axis=-1), ctx_1024, L0_xattn_Wq, L0_xattn_Wkv, L0_xattn_Wout, L0_xattn_bout)
    x = x + _L0_attn_ref(_layernorm(x, axis=-1), L0_attn_ln1_w, L0_attn_ln1_b, L0_attn_wq, L0_attn_wk, L0_attn_wv, L0_attn_wo, L0_attn_bo, L0_attn_ln2_w, L0_attn_ln2_b, L0_attn_w1, L0_attn_w2)
    x = x + _L0_ffn_ref(_layernorm(x, axis=-1), L0_ffn_ln_gamma, L0_ffn_ln_beta, L0_ffn_router_w, L0_ffn_gate_up_w, L0_ffn_down_w, L0_ffn_shared_gate_up_w, L0_ffn_shared_down_w)
    x = x + _L1_xattn_ref(_layernorm(x, axis=-1), ctx_1024, L1_xattn_q_w, L1_xattn_q_b, L1_xattn_k_w, L1_xattn_k_b, L1_xattn_v_w, L1_xattn_v_b, L1_xattn_o_w, L1_xattn_o_b)
    x = x + _L1_attn_ref(_layernorm(x, axis=-1), L1_attn_w_qkv, L1_attn_b_qkv, L1_attn_w_out, L1_attn_b_out)
    x = x + _L1_ffn_ref(_layernorm(x, axis=-1), L1_ffn_w_g, L1_ffn_c_fc, L1_ffn_c_proj)
    x = x + _L2_xattn_ref(_layernorm(x, axis=-1), ctx_1024, ctx_1024, L2_xattn_Wq, L2_xattn_Wk, L2_xattn_Wv, L2_xattn_Wo)
    x = x + _L2_attn_ref(_layernorm(x, axis=-1), L2_attn_W_Q, L2_attn_W_K, L2_attn_W_V, L2_attn_W_G, L2_attn_W_O, L2_attn_gn_weight, L2_attn_gn_bias)
    x = x + _L2_ffn_ref(_layernorm(x, axis=-1), L2_ffn_w1, L2_ffn_b1, L2_ffn_w2, L2_ffn_b2)
    x = x + _L3_xattn_ref(_layernorm(x, axis=-1), ctx_1024, ctx_1024, mask_1x1xSxS2_ik0, L3_xattn_wq, L3_xattn_bq, L3_xattn_wk, L3_xattn_bk, L3_xattn_wv, L3_xattn_bv, L3_xattn_wo, L3_xattn_bo)
    x = x + _L3_attn_ref(_layernorm(x, axis=-1), L3_attn_ln1_g, L3_attn_ln1_b, L3_attn_ln2_g, L3_attn_ln2_b, L3_attn_ca_sub_w, L3_attn_ca_Wl_w, L3_attn_ca_W_w, L3_attn_ca_B_w, L3_attn_ca_sub_b, L3_attn_ca_Wl_b, L3_attn_ca_W_b, L3_attn_ca_B_b, L3_attn_cp_sub_w, L3_attn_cp_Wl_w, L3_attn_cp_W_w, L3_attn_cp_B_w, L3_attn_cp_sub_b, L3_attn_cp_Wl_b, L3_attn_cp_W_b, L3_attn_cp_B_b, L3_attn_cf_sub_w, L3_attn_cf_Wl_w, L3_attn_cf_W_w, L3_attn_cf_B_w, L3_attn_cf_sub_b, L3_attn_cf_Wl_b, L3_attn_cf_W_b, L3_attn_cf_B_b, L3_attn_cm_sub_w, L3_attn_cm_Wl_w, L3_attn_cm_W_w, L3_attn_cm_B_w, L3_attn_cm_sub_b, L3_attn_cm_Wl_b, L3_attn_cm_W_b, L3_attn_cm_B_b)
    x = x + _L3_ffn_ref(_layernorm(x, axis=-1), L3_ffn_ln1_w, L3_ffn_ln2_w, L3_ffn_Wq, L3_ffn_bq, L3_ffn_Wk, L3_ffn_bk, L3_ffn_Wv, L3_ffn_bv, L3_ffn_qn_w, L3_ffn_kn_w, L3_ffn_Wg, L3_ffn_bg, L3_ffn_Wo, L3_ffn_bo, L3_ffn_Wr, L3_ffn_br, L3_ffn_W1, L3_ffn_b1, L3_ffn_W2, L3_ffn_b2)
    return x

_drawn_inputs = setup_inputs


def setup_inputs(seed=0):
    import zlib

    import numpy as np

    out = dict(_drawn_inputs(seed))
    spreads = {'L0_attn_ln1_w': (1.0, 0.6),
     'L0_attn_ln1_b': (0.0, 0.333),
     'L0_attn_bo': (0.0, 0.1),
     'L0_attn_ln2_w': (1.0, 0.2),
     'L0_attn_ln2_b': (0.0, 0.1),
     'L0_ffn_ln_gamma': (1.0, 0.2),
     'L0_ffn_ln_beta': (0.0, 0.1),
     'L1_attn_b_qkv': (0.0, 0.393),
     'L1_attn_b_out': (0.0, 0.1),
     'L2_attn_gn_weight': (1.0, 0.6),
     'L2_attn_gn_bias': (0.0, 0.8),
     'L3_attn_ln1_g': (1.0, 0.2),
     'L3_attn_ln1_b': (0.0, 0.1),
     'L3_attn_ln2_g': (1.0, 0.2),
     'L3_attn_ln2_b': (0.0, 0.1),
     'L3_attn_ca_W_w': (1.0, 0.6),
     'L3_attn_ca_B_w': (0.0, 0.1),
     'L3_attn_ca_W_b': (1.0, 0.6),
     'L3_attn_ca_B_b': (0.0, 0.1),
     'L3_attn_cp_W_w': (1.0, 0.6),
     'L3_attn_cp_B_w': (0.0, 0.1),
     'L3_attn_cp_W_b': (1.0, 0.6),
     'L3_attn_cp_B_b': (0.0, 0.1),
     'L3_attn_cf_W_w': (1.0, 0.6),
     'L3_attn_cf_B_w': (0.0, 0.1),
     'L3_attn_cf_W_b': (1.0, 0.6),
     'L3_attn_cf_B_b': (0.0, 0.1),
     'L3_attn_cm_W_w': (1.0, 0.581),
     'L3_attn_cm_B_w': (0.0, 0.1),
     'L3_attn_cm_W_b': (1.0, 0.6),
     'L3_attn_cm_B_b': (0.0, 0.1),
     'L3_ffn_ln1_w': (1.0, 0.2),
     'L3_ffn_ln2_w': (1.0, 0.2),
     'L3_ffn_bq': (0.0, 0.544),
     'L3_ffn_bk': (0.0, 0.8),
     'L3_ffn_bv': (0.0, 0.279),
     'L3_ffn_qn_w': (1.0, 0.6),
     'L3_ffn_kn_w': (1.0, 0.6),
     'L3_ffn_bg': (0.0, 0.434),
     'L3_ffn_bo': (0.0, 0.1),
     'L3_ffn_br': (0.0, 0.1),
     'L3_ffn_b1': (0.0, 0.719),
     'L3_ffn_b2': (0.0, 0.41)}
    factors = {'L0_attn_wq': 8.0,
     'L0_attn_wk': 8.0,
     'L1_xattn_q_w': 3.17,
     'L1_xattn_q_b': 8.0,
     'L1_xattn_k_w': 2.99,
     'L1_xattn_k_b': 8.0,
     'L1_xattn_v_b': 2.986,
     'L1_attn_w_qkv': 3.165,
     'L1_ffn_w_g': 2.93,
     'L2_xattn_Wq': 8.0,
     'L2_xattn_Wk': 8.0,
     'L2_xattn_Wv': 3.13,
     'L2_xattn_Wo': 3.387,
     'L2_attn_W_Q': 8.0,
     'L2_attn_W_K': 8.0,
     'L2_attn_W_V': 8.0,
     'L2_attn_W_G': 8.0,
     'L2_attn_W_O': 8.0,
     'L2_ffn_b1': 7.837,
     'L2_ffn_b2': 6.431,
     'L3_xattn_bq': 3.358,
     'L3_xattn_bk': 8.0,
     'L3_attn_ca_Wl_w': 8.0,
     'L3_attn_ca_sub_b': 5.367,
     'L3_attn_ca_Wl_b': 3.823,
     'L3_attn_cp_sub_b': 4.263,
     'L3_attn_cp_Wl_b': 8.0,
     'L3_attn_cf_Wl_w': 3.933,
     'L3_attn_cf_sub_b': 8.0,
     'L3_attn_cf_Wl_b': 8.0,
     'L3_attn_cm_sub_b': 7.873,
     'L3_attn_cm_Wl_b': 8.0}
    for name, (base, spread) in spreads.items():
        noise = np.random.default_rng([zlib.crc32(name.encode()), seed]).standard_normal(out[name].shape)
        drawn = base * np.exp(spread * noise) if base else spread * noise
        out[name] = jnp.asarray(drawn.astype(out[name].dtype))
    for name, factor in factors.items():
        out[name] = (out[name] * factor).astype(out[name].dtype)
    return out
```

```python
from contextlib import ExitStack

import numpy as np

import concourse.bass as bass
from concourse import mybir

ALU = mybir.AluOpType
ACT = mybir.ActivationFunctionType
AX = mybir.AxisListType
F32 = mybir.dt.float32
BF16 = mybir.dt.bfloat16

P = 128
S = 32
B = 128
TOK = B * S
TILES = TOK // P
BPT = P // S
TPC = 4
CHUNK = TPC * P
CHUNKS = TILES // TPC
SK = 257
SUBLAYERS = range(1, 13)


def constants():
    c = {}
    ch = np.arange(P)
    c["ident"] = np.eye(P)
    c["heads16"] = (ch[:, None] // 8 == np.arange(16)[None]).astype(float)
    c["heads8"] = (ch[:, None] // 16 == np.arange(8)[None]).astype(float)
    row = np.arange(P)
    c["own8"] = (row[:, None] // S == np.arange(32)[None] // 8).astype(float)
    c["own16"] = (row[:, None] // S == np.arange(64)[None] // 16).astype(float)
    c["fold"] = (row[:, None] % S == np.arange(S)[None]).astype(float)
    c["causal"] = (np.arange(S)[None] <= row[:, None] % S).astype(float)
    c["causal_neg"] = (c["causal"] - 1.0) * 1e30
    c["causal_fill"] = (c["causal"] - 1.0) * 1e4 * 8 ** 0.5
    c["same8"] = (ch[:, None] // 8 == ch[None] // 8).astype(float)
    c["same16"] = (ch[:, None] // 16 == ch[None] // 16).astype(float)
    pos = np.arange(S, dtype=np.float32)
    d = 16
    scale = (np.arange(0, d, 2, dtype=np.float32) + np.float32(0.4 * d)) / np.float32(1.4 * d)
    sc = scale[None] ** (pos / np.float32(512.0))[:, None]
    inv = (1.0 / np.float32(10000.0) ** (np.arange(d // 2, dtype=np.float32) / np.float32(d // 2)))
    ang = pos[:, None] * inv[None].astype(np.float32)
    pair = (ch % 16) // 2
    sign = np.where(ch % 2 == 0, -1.0, 1.0)[:, None]
    c["xcos_q"] = (np.cos(ang) * sc).T[pair]
    c["xsin_q"] = (np.sin(ang) * sc).T[pair] * sign
    c["xcos_k"] = (np.cos(ang) / sc).T[pair]
    c["xsin_k"] = (np.sin(ang) / sc).T[pair] * sign
    inv = (1.0 / np.float32(10000.0) ** (np.arange(0, 8, 2, dtype=np.float32) / np.float32(8)))
    ang = pos[:, None] * inv[None].astype(np.float32)
    sign = np.where(ch % 8 < 4, -1.0, 1.0)[:, None]
    c["rcos"] = np.cos(ang).T[ch % 4]
    c["rsin"] = np.sin(ang).T[ch % 4] * sign
    gam = 1.0 - np.exp(np.linspace(np.log(1.0 / 32.0), np.log(1.0 / 512.0), 8))
    gam = gam.astype(np.float32).astype(float)
    diff = (row[:, None] % S) - np.arange(S)[None]
    for g in range(2):
        ga = gam[4 * g + row // S][:, None]
        c[f"decay{g}"] = np.where(diff >= 0, ga ** np.maximum(diff, 0), 0.0)
    c["ones"] = np.ones((P, P))
    c["mhalf"] = np.full((P, TPC), -0.5)
    c["eps5"] = np.full((P, TPC), 1e-5)
    c["eps6"] = np.full((P, TPC), 1e-6)
    c["group_of"] = np.zeros((P, P))
    c["group_of"][0:4] = np.arange(4)[:, None] == np.arange(P)[None] // 32
    c["magic"] = np.full((P, 1), -12582912.0)
    c["experts"] = np.tile(8.0 - np.arange(8.0), (P, 1))
    c["upto"] = (np.arange(P)[:, None] <= np.arange(P)[None]).astype(float)
    return {k: np.asarray(v, np.float32) for k, v in c.items()}


CONSTANTS = constants()
CONST_AT = {}
_at = 0
for _name, _value in CONSTANTS.items():
    CONST_AT[_name] = (_at, _value.shape[1])
    _at += _value.shape[1]
CONST_WIDTH = _at


class Core:

    def __init__(self, nc, packs, x_sb, const_sb):
        self.nc, self.packs, self.X, self.const_sb = nc, packs, x_sb, const_sb

    def const2(self, first, second):
        (at, width), (at2, width2) = CONST_AT[first], CONST_AT[second]
        assert at2 == at + width
        return self.const_sb[:, at:at2 + width2]

    def const(self, name):
        at, width = CONST_AT[name]
        return self.const_sb[:, at:at + width]


class Link:

    def __init__(self, eng, sem, done):
        self.eng, self.sem, self.done, self.count = eng, sem, done, 0

    def __call__(self, instruction):
        self.count += 1
        instruction.then_inc(self.sem, 1)
        self.eng.wait_ge(self.sem, self.done + self.count)


class Scope(ExitStack):

    def __init__(self, core, name):
        super().__init__()
        self.core, self.nc, self.name, self.sems = core, core.nc, name, []

    def sb(self, name, shape, dt=F32):
        return self.enter_context(self.nc.sbuf_tensor(f"{self.name}_{name}", shape, dt))

    def banks(self):
        return self.enter_context(self.nc.psum_tensor(f"{self.name}_psum", [P, 8, 512], F32))

    def sem(self, name):
        sem = self.enter_context(self.nc.semaphore(f"{self.name}_{name}"))
        self.sems.append(sem)
        return sem

    def weights(self, source):
        if not isinstance(source, str):
            return source, lambda eng: None, lambda eng: None
        s_w = self.sem("weights")
        dram, at = self.core.packs[source]
        tile = self.sb("weights", list(dram.shape))

        def fetch(eng):
            eng.dma_start(tile[:], dram).then_inc(s_w, 16)

        return (lambda name: tile[:, at[name][0]:at[name][0] + at[name][1]]), lambda eng: eng.wait_ge(s_w, 16), fetch

    def open_block(self):
        self.block_guard = self.nc.Block()
        return self.block_guard.__enter__()

    def close_block(self):
        self.block_guard.__exit__(None, None, None)
        with self.nc.Block() as block:
            @block.gpsimd
            def _(pool):
                for sem in self.sems:
                    pool.sem_clear(sem)


def gate(eng, sem, value, passed):
    eng.wait_ge(sem, value)
    eng.sem_inc(passed, 1)


def spread(ap, reps, axis):
    shape = list(ap.shape)
    shape.insert(axis, reps)
    return ap.unsqueeze(axis).to_broadcast(shape)


class Norm:

    def __init__(self, sc, name, eps, rms=False):
        self.eps, self.rms = sc.core.const(eps), rms
        self.mhalf = sc.core.const("mhalf")
        self.stats = sc.sb(name + "_stats", [P, 2, TPC, 6])
        self.moments = sc.sb(name + "_moments", [P, 2, TPC, 2])
        self.square = sc.sb(name + "_square", [P, 2, TPC]) if rms else None
        self.rstd = sc.sb(name + "_rstd", [P, 2, 2, TPC])
        self.s_stats = sc.sem(name + "_stats")
        self.s_moments = sc.sem(name + "_moments")
        self.s_square = sc.sem(name + "_square")
        self.s_var = sc.sem(name + "_var")
        self.s_rstd = sc.sem(name + "_rstd")
        self.passed_dve = sc.sem(name + "_passed_dve")

    def dve_stats(self, dve, tile_of, c, u):
        for k in range(TPC):
            last = dve.bn_stats(self.stats[:, u, k], tile_of(k))
        last.then_inc(self.s_stats, 1)
        gate(dve, self.s_stats, c + 1, self.passed_dve)
        for k in range(TPC):
            last = dve.bn_aggr(self.moments[:, u, k], self.stats[:, u, k])
        last.then_inc(self.s_moments, 1)
        if self.rms:
            mean, var = self.moments[:, u, :, 0], self.moments[:, u, :, 1]
            dve.wait_ge(self.s_moments, c + 1)
            dve.tensor_tensor(self.square[:, u], mean, mean, ALU.mult).then_inc(self.s_square, 1)
            dve.wait_ge(self.s_square, 2 * c + 1)
            dve.tensor_tensor(self.square[:, u], self.square[:, u], var, ALU.add).then_inc(self.s_square, 1)

    def pool_rstd(self, pool, c, u):
        pool.wait_ge(*((self.s_square, 2 * c + 2) if self.rms else (self.s_moments, c + 1)))
        var = self.square[:, u] if self.rms else self.moments[:, u, :, 1]
        pool.tensor_tensor(self.rstd[:, u, 0], var, self.eps, ALU.add).then_inc(self.s_var, 1)
        pool.wait_ge(self.s_var, c + 1)
        pool.tensor_tensor(self.rstd[:, u, 1], self.rstd[:, u, 0], self.mhalf, ALU.pow).then_inc(self.s_rstd, 1)

    def dve_apply(self, dve, out_of, tile_of, c, u, s_out):
        dve.wait_ge(self.s_rstd, c + 1)
        for k in range(TPC):
            if self.rms:
                last = dve.tensor_scalar(out_of(k), tile_of(k), self.rstd[:, u, 1, k:k + 1], None, ALU.mult)
            else:
                last = dve.tensor_scalar(out_of(k), tile_of(k), self.moments[:, u, k, 0:1],
                                         self.rstd[:, u, 1, k:k + 1], ALU.subtract, ALU.mult)
        last.then_inc(s_out, 1)



def small_attention(core, name, weights, heads, scale, context=None, mask=None, second=None,
                    keep=None, rotate=None, qk_norm=False, post=None, softmax=True):
    nc, X = core.nc, core.X
    dh = P // heads
    G = heads // 4
    GW = 4 * dh
    GB = G * BPT
    own, head_of, ident = core.const(f"own{dh}"), core.const(f"heads{heads}"), core.const("ident")
    dest = keep if keep is not None else X
    PAIRS = CHUNKS // 2
    with Scope(core, name) as sc:
        psum = sc.banks()
        w, arrived, fetch = sc.weights(weights)
        norm = Norm(sc, "ln", "eps5")
        norm2 = Norm(sc, "ln2", second[0], rms=second[1]) if second else None
        Y = sc.sb("normed", [P, 2, TPC, P])
        Y2 = sc.sb("normed2", [P, 2, TPC, P]) if second else Y
        hT = sc.sb("hT", [P, 2, CHUNK])
        cT = sc.sb("cT", [P, 2, CHUNK]) if context is not None else hT
        qT = sc.sb("qT", [P, 2, CHUNK])
        kT = sc.sb("kT", [P, 2, CHUNK])
        q_heads = sc.sb("q_heads", [P, 4, BPT, heads, S])
        v_own = core.hT_all[:].rearrange("p (t b c) -> p t b c", b=BPT, c=P)
        E = sc.sb("E", [P, 4, GB, S])
        ET = sc.sb("ET", [P, 4, G, P])
        top = sc.sb("top", [P, 4, GB])
        total = sc.sb("total", [P, 8, 2, GB])
        O = sc.sb("O", [P, 4, GB, GW])
        O_own = sc.sb("O_own", [P, 4, BPT, P])
        aT = sc.sb("aT", [P, 2, 4, CHUNK])
        rot = sc.sb("rot", [P, 2, 4, CHUNK]) if rotate else None
        scratch = sc.sb("scratch", [P, 2, 2, CHUNK]) if qk_norm or post else None
        s_zero, s_ctx = sc.sem("zero"), [sc.sem("ctx0"), sc.sem("ctx1")]
        s_norm, s_norm2, s_turn, s_hT = sc.sem("norm"), sc.sem("norm2"), sc.sem("turn"), sc.sem("hT")
        s_proj, s_q, s_k, s_v = sc.sem("proj"), sc.sem("q"), sc.sem("k"), sc.sem("v")
        s_heads, s_score, s_mask = sc.sem("heads"), sc.sem("score"), sc.sem("mask")
        s_top, s_sub, s_exp, s_sum = sc.sem("top"), sc.sem("sub"), sc.sem("exp"), sc.sem("sum")
        s_recip, s_eT, s_ET, s_pv = sc.sem("recip"), sc.sem("eT"), sc.sem("ET"), sc.sem("pv")
        s_scaled, s_own, s_fold, s_aT = sc.sem("scaled"), sc.sem("own"), sc.sem("fold"), sc.sem("aT")
        s_out, s_done, s_post = sc.sem("out"), sc.sem("done"), sc.sem("post")
        passed_dve, passed_pool = sc.sem("passed_dve"), sc.sem("passed_pool")
        s_link, s_kept = sc.sem("link"), sc.sem("kept")
        if rotate:
            s_rot, s_swap_k, s_bias_rot = sc.sem("rot"), sc.sem("swap_k"), sc.sem("bias_rot")
            s_rot_link = sc.sem("rot_link")
        if qk_norm:
            s_square, s_ms, s_ms_sb = sc.sem("square"), sc.sem("ms"), sc.sem("ms_sb")
            s_power, s_unit = sc.sem("power"), sc.sem("unit")
        if post:
            s_gate, s_sig = sc.sem("gate"), sc.sem("sig")
        if post == "group_norm":
            s_mean, s_centred, s_dev = sc.sem("mean"), sc.sem("centred"), sc.sem("dev")
            s_var, s_var_sb = sc.sem("var"), sc.sem("var_sb")
        bg_neg = sc.sb("bg_neg", [P, 1]) if post == "gate" else None
        bias_rot = sc.sb("bias_rot", [P, 2 * S]) if rotate else None
        s_q_final = s_unit if qk_norm else s_q
        q_count = 2 if qk_norm else 1
        post_steps = {"group_norm": 4, "gate": 2, None: 0}[post]
        bank_of = lambda at: psum[:, at, 0:G * P]
        block = sc.open_block()

        @block.sync
        def _(sp):
            fetch(sp)
            if context is not None:
                for u in range(2):
                    sp.dma_start(cT[:, u], context[:, u * CHUNK:(u + 1) * CHUNK]).then_inc(s_ctx[u], 16)
                with sp.Fori(1, PAIRS) as i:
                    for u in range(2):
                        sp.wait_ge(s_proj, i * 2 - 1 + u)
                        sp.dma_start(cT[:, u], context[:, bass.ds((i * 2 + u) * CHUNK, CHUNK)]).then_inc(s_ctx[u], 16)

        @block.gpsimd
        def _(pool):
            pool.memset(v_own, 0.0).then_inc(s_zero, 1)
            if rotate:
                arrived(pool)
                pool.wait_ge(s_bias_rot, 1)
            with pool.Fori(0, PAIRS) as i:
                for u in range(2):
                    norm.pool_rstd(pool, i * 2 + u, u)
                if second:
                    for u in range(2):
                        norm2.pool_rstd(pool, i * 2 + u, u)
                if rotate:
                    link = Link(pool, s_rot_link, i * 4)
                    for u in range(2):
                        for a, dst, s_dst in ((0, qT, s_q), (1, kT, s_k)):
                            pool.wait_ge(s_rot, (i * 2 + u) * 4 + 2 * a + 2)
                            r = rot[:, u, 2 * a].rearrange("p (b s) -> p b s", s=S)
                            link(pool.tensor_tensor(r, r, spread(bias_rot[:, a * S:(a + 1) * S], CHUNK // S, 1), ALU.add))
                            pool.tensor_tensor(dst[:, u], rot[:, u, 2 * a], rot[:, u, 2 * a + 1],
                                               ALU.add).then_inc(s_dst, 1)
                for n in range(8):
                    u, t = divmod(n, TPC)
                    pool.wait_ge(s_q_final, (i * 2 + u) * q_count + 1)
                    if n >= 4:
                        pool.wait_ge(s_score, i * 8 + n - 3)
                    pool.tensor_tensor(q_heads[:, n % 4],
                                       spread(qT[:, u, t * P:(t + 1) * P].rearrange("p (b s) -> p b s", s=S), heads, 2),
                                       spread(spread(head_of, BPT, 1), S, 3), ALU.mult).then_inc(s_heads, 1)

        @block.tensor
        def _(pe):
            arrived(pe)
            with pe.Fori(0, PAIRS) as i:
                for u in range(2):
                    pe.wait_ge(s_norm2 if second else s_norm, i * 2 + u + 1)
                    for k in range(TPC):
                        last = pe.transpose(psum[:, 4 * u, k * P:(k + 1) * P], Y2[:, u, k], ident)
                    last.then_inc(s_turn, 1)
                for u in range(2):
                    pe.wait_ge(s_hT, i * 2 + u + 1)
                    if context is not None:
                        pe.wait_ge(s_ctx[u], i * 16 + 16)
                    pe.matmul(psum[:, 4 * u + 1], w("wq"), hT[:, u], start=True, stop=True)
                    pe.matmul(psum[:, 4 * u + 2], w("wk"), cT[:, u], start=True, stop=True)
                    if rotate:
                        pe.matmul(psum[:, 4 * u], w("wq_swap"), hT[:, u], start=True, stop=True)
                    for k in range(TPC):
                        last = pe.matmul(psum[:, 4 * u + 3, k * P:(k + 1) * P], cT[:, u, k * P:(k + 1) * P],
                                         w("wv"), start=True, stop=True)
                    last.then_inc(s_proj, 1)
                if rotate:
                    for u in range(2):
                        pe.wait_ge(s_rot, (i * 2 + u) * 4 + 1)
                        pe.matmul(psum[:, 4 * u + 1], w("wk_swap"), hT[:, u], start=True, stop=True).then_inc(s_swap_k, 1)
                if qk_norm:
                    for u in range(2):
                        for a in range(2):
                            pe.wait_ge(s_square, (i * 2 + u) * 2 + a + 1)
                            pe.matmul(psum[:, 4 * u + 2 * a], core.const("same8"), scratch[:, u, a],
                                      start=True, stop=True).then_inc(s_ms, 1)

                def scores(n):
                    u, t = divmod(n, TPC)
                    if n == 0:
                        pe.wait_ge(s_v, i * 2 + 2)
                        pe.wait_ge(s_k, i * 2 + 2)
                        pe.wait_ge(s_q_final, (i * 2 + 2) * q_count)
                    pe.wait_ge(s_heads, i * 8 + n + 1)
                    if n >= 2:
                        pe.wait_ge(s_mask if mask else s_sub, i * 8 + n - 1)
                    bank = bank_of(n % 2).rearrange("p (g b k) -> p g b k", b=BPT, k=S)
                    for b in range(BPT):
                        for g in range(G):
                            last = pe.matmul(bank[:, g, b], q_heads[:, n % 4, b, 4 * g:4 * g + 4].rearrange("p h s -> p (h s)"),
                                             kT[:, u, t * P + b * S:t * P + (b + 1) * S], start=True, stop=True)
                    last.then_inc(s_score, 1)

                def turn(n):
                    pe.wait_ge(s_exp if softmax else s_mask, i * 8 + n + 1)
                    if n >= 2:
                        pe.wait_ge(s_ET, i * 8 + n - 1)
                    for g in range(G):
                        last = pe.transpose(psum[:, 2 + n % 2, g * P:(g + 1) * P],
                                            E[:, n % 4, g * BPT:(g + 1) * BPT].rearrange("p b k -> p (b k)"), ident)
                    last.then_inc(s_eT, 1)

                def values(n):
                    pe.wait_ge(s_ET, i * 8 + n + 1)
                    if n >= 2:
                        pe.wait_ge(s_scaled, i * 8 + n - 1)
                    bank = psum[:, 4 + n % 2].rearrange("p (g b c) -> p g b c", b=BPT, c=GW)
                    for g in range(G):
                        last = pe.matmul(bank[:, g], ET[:, n % 4, g], v_own[:, n, :, g * GW:(g + 1) * GW],
                                         start=True, stop=True)
                    last.then_inc(s_pv, 1)

                def fold(n):
                    u, t = divmod(n, TPC)
                    pe.wait_ge(s_own if softmax else s_scaled, i * 8 + n + 1)
                    for b in range(BPT):
                        last = pe.matmul(psum[:, 6 + u, t * P + b * S:t * P + (b + 1) * S],
                                         O_own[:, n % 4, b], core.const("fold"), start=True, stop=True)
                    last.then_inc(s_fold, 1)

                for step in range(8 + 6):
                    if step < 8:
                        scores(step)
                    if 0 <= step - 2 < 8:
                        turn(step - 2)
                    if 0 <= step - 4 < 8:
                        values(step - 4)
                    if 0 <= step - 6 < 8:
                        fold(step - 6)
                if post == "group_norm":
                    for u in range(2):
                        pe.wait_ge(s_aT, i * 2 + u + 1)
                        pe.matmul(psum[:, 2 * u], core.const("same16"), aT[:, u, 0], start=True, stop=True).then_inc(s_mean, 1)
                        pe.matmul(psum[:, 2 * u + 1], w("wg"), hT[:, u], start=True, stop=True).then_inc(s_gate, 1)
                    for u in range(2):
                        pe.wait_ge(s_dev, i * 2 + u + 1)
                        pe.matmul(psum[:, 6 + u], core.const("same16"), scratch[:, u, 0],
                                  start=True, stop=True).then_inc(s_var, 1)
                if post == "gate":
                    for u in range(2):
                        pe.wait_ge(s_aT, i * 2 + u + 1)
                        pe.matmul(psum[:, 2 * u], w("wg"), aT[:, u, 0], start=True, stop=True).then_inc(s_gate, 1)
                for u in range(2):
                    pe.wait_ge(s_post if post else s_aT, i * 2 + u + 1)
                    for k in range(TPC):
                        last = pe.matmul(psum[:, 4 + u, k * P:(k + 1) * P], aT[:, u, 3 if post else 0, k * P:(k + 1) * P],
                                         w("wo"), start=True, stop=True)
                    last.then_inc(s_out, 1)

        @block.scalar
        def _(act):
            arrived(act)
            if post == "gate":
                act.wait_ge(s_bias_rot, 2)
            with act.Fori(0, PAIRS) as i:
                for u in range(2):
                    act.wait_ge(s_turn, i * 2 + u + 1)
                    act.activation(hT[:, u], psum[:, 4 * u], ACT.Identity, bias=w("ln_b") if second else 0.0,
                                   scale=w("ln_w") if second else 1.0).then_inc(s_hT, 1)
                if not rotate:
                    for u in range(2):
                        act.wait_ge(s_proj, i * 2 + u + 1)
                        act.activation(qT[:, u], psum[:, 4 * u + 1], ACT.Identity, bias=w("bq")).then_inc(s_q, 1)
                        act.activation(kT[:, u], psum[:, 4 * u + 2], ACT.Identity, bias=w("bk")).then_inc(s_k, 1)
                if qk_norm:
                    for u in range(2):
                        for a in range(2):
                            act.wait_ge(s_ms, (i * 2 + u) * 2 + a + 1)
                            act.activation(scratch[:, u, a], psum[:, 4 * u + 2 * a], ACT.Sqrt,
                                           scale=1.0 / dh, bias=core.const("eps6")[:, 0:1]).then_inc(s_ms_sb, 1)
                for step in range(8 + 2):
                    if step < 8 and softmax:
                        act.wait_ge(s_sub, i * 8 + step + 1)
                        act.activation(E[:, step % 4], E[:, step % 4], ACT.Exp, scale=scale).then_inc(s_exp, 1)
                    if step >= 2:
                        n = step - 2
                        act.wait_ge(s_eT, i * 8 + n + 1)
                        act.activation(ET[:, n % 4].rearrange("p g c -> p (g c)"), bank_of(2 + n % 2), ACT.Copy).then_inc(s_ET, 1)
                for u in range(2):
                    act.wait_ge(s_fold, i * 8 + 4 * u + 4)
                    act.activation(aT[:, u, 0], psum[:, 6 + u], ACT.Identity, bias=w("bv")).then_inc(s_aT, 1)
                if post == "group_norm":
                    for u in range(2):
                        act.wait_ge(s_gate, i * 2 + u + 1)
                        act.activation(aT[:, u, 2], psum[:, 2 * u + 1], ACT.Sigmoid).then_inc(s_sig, 1)
                    for u in range(2):
                        act.wait_ge(s_var, i * 2 + u + 1)
                        act.activation(scratch[:, u, 1], psum[:, 6 + u], ACT.Sqrt, scale=1.0 / dh,
                                       bias=core.const("eps5")[:, 0:1]).then_inc(s_var_sb, 1)
                if post == "gate":
                    for u in range(2):
                        act.wait_ge(s_gate, i * 2 + u + 1)
                        act.activation(aT[:, u, 1], psum[:, 2 * u], ACT.Exp, scale=-1.0, bias=bg_neg[:]).then_inc(s_sig, 1)

        @block.vector
        def _(dve):
            dve.wait_ge(s_zero, 1)
            arrived(dve)
            if rotate:
                br = bias_rot
                for a in range(2):
                    dve.tensor_scalar(br[:, a * S:(a + 1) * S], core.const(rotate[2 * a]), w(("bq", "bk")[a]), None,
                                      ALU.mult).then_inc(s_kept, 1)
                    dve.wait_ge(s_kept, a + 1)
                    last = dve.scalar_tensor_tensor(out=br[:, a * S:(a + 1) * S], in0=core.const(rotate[2 * a + 1]),
                                                    scalar=w(("bq_swap", "bk_swap")[a]), in1=br[:, a * S:(a + 1) * S],
                                                    op0=ALU.mult, op1=ALU.add)
                last.then_inc(s_bias_rot, 1)
                if post == "gate":
                    dve.tensor_scalar(bg_neg[:], w("bg"), -1.0, None, ALU.mult).then_inc(s_bias_rot, 1)
            with dve.Fori(0, PAIRS) as i:
                link = Link(dve, s_link, i * (2 * post_steps + 2))
                x_of = [lambda k, u=u: X[:, bass.ds(i * 8 + 4 * u + k, 1)] for u in range(2)]
                y_of = [lambda k, u=u: Y[:, u, k] for u in range(2)]
                y2_of = [lambda k, u=u: Y2[:, u, k] for u in range(2)]
                for u in range(2):
                    norm.dve_stats(dve, x_of[u], i * 2 + u, u)
                for u in range(2):
                    norm.dve_apply(dve, y_of[u], x_of[u], i * 2 + u, u, s_norm)
                if second:
                    for u in range(2):
                        dve.wait_ge(s_norm, i * 2 + u + 1)
                        norm2.dve_stats(dve, y_of[u], i * 2 + u, u)
                    for u in range(2):
                        norm2.dve_apply(dve, y2_of[u], y_of[u], i * 2 + u, u, s_norm2)
                for u in range(2):
                    dve.wait_ge(s_proj, i * 2 + u + 1)
                    for b in range(BPT):
                        last = dve.tensor_copy(v_own[b * S:(b + 1) * S, 4 * u:4 * u + 4, b],
                                               psum[b * S:(b + 1) * S, 4 * u + 3].rearrange("p (t c) -> p t c", c=P))
                    last.then_inc(s_v, 1)
                if rotate:
                    for u in range(2):
                        for m, at in enumerate((1, 0, 2, 1)):
                            if m == 3:
                                dve.wait_ge(s_swap_k, i * 2 + u + 1)
                            dve.tensor_tensor(rot[:, u, m].rearrange("p (b s) -> p b s", s=S),
                                              psum[:, 4 * u + at].rearrange("p (b s) -> p b s", s=S),
                                              spread(core.const(rotate[m]), CHUNK // S, 1), ALU.mult).then_inc(s_rot, 1)
                if qk_norm:
                    for u in range(2):
                        for a, t, s_t in ((0, qT, s_q), (1, kT, s_k)):
                            dve.wait_ge(s_t, i * 2 + u + 1)
                            dve.tensor_tensor(scratch[:, u, a], t[:, u], t[:, u], ALU.mult).then_inc(s_square, 1)
                    for u in range(2):
                        for a in range(2):
                            dve.wait_ge(s_ms_sb, (i * 2 + u) * 2 + a + 1)
                            dve.reciprocal(scratch[:, u, a], scratch[:, u, a]).then_inc(s_power, 1)
                    for u in range(2):
                        for a, t in ((0, qT), (1, kT)):
                            dve.wait_ge(s_power, (i * 2 + u) * 2 + a + 1)
                            dve.scalar_tensor_tensor(out=t[:, u], in0=t[:, u], scalar=w(("qn", "kn")[a]), in1=scratch[:, u, a],
                                                     op0=ALU.mult, op1=ALU.mult).then_inc(s_unit, 1)

                def head(n):
                    e = E[:, n % 4]
                    src = bank_of(n % 2).rearrange("p (m k) -> p m k", k=S)
                    dve.wait_ge(s_score, i * 8 + n + 1)
                    if mask == "decay":
                        dve.tensor_tensor(e.rearrange("p (g b) k -> p g b k", b=BPT),
                                          bank_of(n % 2).rearrange("p (g b k) -> p g b k", b=BPT, k=S),
                                          spread(core.const2("decay0", "decay1").rearrange("p (g k) -> p g k", k=S), BPT, 2),
                                          ALU.mult).then_inc(s_mask, 1)
                        return
                    if mask == "causal":
                        dve.tensor_tensor(e, src, spread(core.const("causal_neg"), GB, 1), ALU.add).then_inc(s_mask, 1)
                        src = e
                        dve.wait_ge(s_mask, i * 8 + n + 1)
                    if mask == "fill":
                        dve.tensor_tensor(e, src, spread(core.const("causal"), GB, 1), ALU.mult).then_inc(s_kept, 1)
                        dve.wait_ge(s_kept, i * 8 + n + 1)
                        dve.tensor_tensor(e, e, spread(core.const("causal_fill"), GB, 1), ALU.add).then_inc(s_mask, 1)
                        src = e
                        dve.wait_ge(s_mask, i * 8 + n + 1)
                    dve.tensor_reduce(top[:, n % 4], src, AX.X, ALU.max).then_inc(s_top, 1)
                    dve.wait_ge(s_top, i * 8 + n + 1)
                    dve.tensor_tensor(e, src, spread(top[:, n % 4], S, 2), ALU.subtract).then_inc(s_sub, 1)

                def sums(n):
                    dve.wait_ge(s_exp, i * 8 + n + 1)
                    dve.tensor_reduce(total[:, n, 0], E[:, n % 4], AX.X, ALU.add).then_inc(s_sum, 1)
                    dve.wait_ge(s_sum, i * 8 + n + 1)
                    dve.reciprocal(total[:, n, 1], total[:, n, 0]).then_inc(s_recip, 1)

                def scaled(n):
                    src = psum[:, 4 + n % 2].rearrange("p (m c) -> p m c", c=GW)
                    mine = O_own[:, n % 4].rearrange("p b (g c) -> p g b c", c=GW)
                    by_group = lambda a: a.rearrange("p (g b) c -> p g b c", b=BPT)
                    own_all = spread(spread(own, G, 1), BPT, 2)
                    dve.wait_ge(s_pv, i * 8 + n + 1)
                    if not softmax:
                        dve.tensor_tensor(mine, by_group(src), own_all, ALU.mult).then_inc(s_scaled, 1)
                        return
                    dve.wait_ge(s_recip, i * 8 + n + 1)
                    dve.tensor_tensor(O[:, n % 4], src, spread(total[:, n, 1], GW, 2), ALU.mult).then_inc(s_scaled, 1)
                    dve.wait_ge(s_scaled, i * 8 + n + 1)
                    dve.tensor_tensor(mine, by_group(O[:, n % 4]), own_all, ALU.mult).then_inc(s_own, 1)

                for step in range(8 + 5):
                    if step < 8:
                        head(step)
                    if 0 <= step - 1 < 8 and softmax:
                        sums(step - 1)
                    if 0 <= step - 5 < 8:
                        scaled(step - 5)
                if post == "group_norm":
                    for u in range(2):
                        dve.wait_ge(s_aT, i * 2 + u + 1)
                        dve.wait_ge(s_mean, i * 2 + u + 1)
                        dve.scalar_tensor_tensor(out=aT[:, u, 1], in0=psum[:, 2 * u], scalar=-1.0 / dh, in1=aT[:, u, 0],
                                                 op0=ALU.mult, op1=ALU.add).then_inc(s_centred, 1)
                        dve.wait_ge(s_centred, i * 2 + u + 1)
                        dve.tensor_tensor(scratch[:, u, 0], aT[:, u, 1], aT[:, u, 1], ALU.mult).then_inc(s_dev, 1)
                    for u in range(2):
                        dve.wait_ge(s_sig, i * 2 + u + 1)
                        link(dve.tensor_tensor(aT[:, u, 2], aT[:, u, 2], psum[:, 2 * u + 1], ALU.mult))
                        dve.wait_ge(s_var_sb, i * 2 + u + 1)
                        link(dve.reciprocal(scratch[:, u, 1], scratch[:, u, 1]))
                        link(dve.tensor_tensor(aT[:, u, 1], aT[:, u, 1], scratch[:, u, 1], ALU.mult))
                        link(dve.tensor_scalar(aT[:, u, 1], aT[:, u, 1], w("gn_w"), w("gn_b"), ALU.mult, ALU.add))
                        dve.tensor_tensor(aT[:, u, 3], aT[:, u, 1], aT[:, u, 2], ALU.mult).then_inc(s_post, 1)
                if post == "gate":
                    for u in range(2):
                        dve.wait_ge(s_sig, i * 2 + u + 1)
                        link(dve.tensor_scalar(aT[:, u, 1], aT[:, u, 1], 1.0, None, ALU.add))
                        link(dve.reciprocal(aT[:, u, 1], aT[:, u, 1]))
                        dve.tensor_tensor(aT[:, u, 3], aT[:, u, 0], aT[:, u, 1], ALU.mult).then_inc(s_post, 1)
                for u in range(2):
                    dve.wait_ge(s_out, i * 2 + u + 1)
                    to = dest[:, bass.ds(i * 8 + 4 * u, 4)]
                    stay = Y[:, u] if keep is not None else to
                    link(dve.tensor_tensor(Y2[:, u], psum[:, 4 + u].rearrange("p (t c) -> p t c", c=P),
                                           spread(w("bo"), TPC, 1), ALU.add))
                    dve.tensor_tensor(to, Y2[:, u], stay, ALU.add).then_inc(s_done, 1)
        sc.close_block()


def front(core, name, weights, hT_all, logits=None, second=None, keep=None, logits_bias=False):
    nc, X = core.nc, core.X
    ident = core.const("ident")
    PAIRS = CHUNKS // 2
    source, first = (X, True) if keep is None or keep[1] == "store" else (keep[0], False)
    with Scope(core, name) as sc:
        psum = sc.banks()
        w, arrived, fetch = sc.weights(weights)
        norm = Norm(sc, "ln", "eps5") if first else None
        norm2 = Norm(sc, "ln2", second[0], rms=second[1]) if second else None
        Y = sc.sb("normed", [P, 2, TPC, P])
        Y2 = sc.sb("normed2", [P, 2, TPC, P]) if second else Y
        s_norm, s_norm2, s_turn, s_hT = sc.sem("norm"), sc.sem("norm2"), sc.sem("turn"), sc.sem("hT")
        s_logits, s_logits_out, s_free = sc.sem("logits"), sc.sem("logits_out"), sc.sem("free")
        s_routed, passed_dve = sc.sem("routed"), sc.sem("passed_dve")
        hT = sc.sb("hT", [P, 2, CHUNK])
        block = sc.open_block()

        @block.sync
        def _(sp):
            fetch(sp)

        @block.gpsimd
        def _(pool):
            with pool.Fori(0, PAIRS) as i:
                for u in range(2):
                    if first:
                        norm.pool_rstd(pool, i * 2 + u, u)
                    if second:
                        norm2.pool_rstd(pool, i * 2 + u, u)
                for u in range(2):
                    gate(pool, s_hT, i * 2 + u + 1, s_free)
                    pool.tensor_copy(hT_all[:, bass.ds((i * 2 + u) * CHUNK, CHUNK)], hT[:, u]).then_inc(s_logits_out, 1)

        @block.tensor
        def _(pe):
            arrived(pe)
            with pe.Fori(0, PAIRS) as i:
                for u in range(2):
                    pe.wait_ge(s_norm2 if second else s_norm, i * 2 + u + 1)
                    for k in range(TPC):
                        last = pe.transpose(psum[:, u, k * P:(k + 1) * P], Y2[:, u, k], ident)
                    last.then_inc(s_turn, 1)
                if logits is not None:
                    for u in range(2):
                        pe.wait_ge(s_hT, i * 2 + u + 1)
                        for k in range(TPC):
                            last = pe.matmul(psum[:, 2 + u, k * 8:(k + 1) * 8], hT[:, u, k * P:(k + 1) * P], w("router"),
                                             start=True, stop=True)
                        last.then_inc(s_logits, 1)

        @block.scalar
        def _(act):
            arrived(act)
            with act.Fori(0, PAIRS) as i:
                for u in range(2):
                    act.wait_ge(s_turn, i * 2 + u + 1)
                    act.activation(hT[:, u], psum[:, u], ACT.Identity, bias=w("ln_b") if second else 0.0,
                                   scale=w("ln_w") if second else 1.0).then_inc(s_hT, 1)

        @block.vector
        def _(dve):
            arrived(dve)
            with dve.Fori(0, PAIRS) as i:
                for u in range(2):
                    at = lambda k: bass.ds(i * 8 + 4 * u + k, 1)
                    y = (lambda k: keep[0][:, at(k)]) if keep else (lambda k: Y[:, u, k])
                    if first:
                        norm.dve_stats(dve, lambda k: X[:, at(k)], i * 2 + u, u)
                        norm.dve_apply(dve, y, lambda k: X[:, at(k)], i * 2 + u, u, s_norm)
                        dve.wait_ge(s_norm, i * 2 + u + 1)
                    if second:
                        norm2.dve_stats(dve, y, i * 2 + u, u)
                        norm2.dve_apply(dve, lambda k: Y2[:, u, k], y, i * 2 + u, u, s_norm2)
                if logits is not None:
                    for u in range(2):
                        dve.wait_ge(s_logits, i * 2 + u + 1)
                        dve.tensor_tensor(logits[:, bass.ds(i * 8 + 4 * u, TPC)],
                                          psum[:, 2 + u, 0:32].rearrange("p (t e) -> p t e", e=8),
                                          spread(w("router_b"), TPC, 1), ALU.add).then_inc(s_routed, 1)
                gate(dve, s_logits_out, i * 2 + 2, passed_dve)
        sc.close_block()


def first_of_max(dve, link, values, best, cand, onehot, order):
    E8 = values.shape[2]
    link(dve.tensor_reduce(best, values, AX.X, ALU.max))
    link(dve.tensor_tensor(cand, values, spread(best, E8, 2), ALU.is_equal))
    link(dve.tensor_tensor(cand, cand, order, ALU.mult))
    link(dve.tensor_reduce(best, cand, AX.X, ALU.max))
    link(dve.tensor_tensor(onehot, cand, spread(best, E8, 2), ALU.is_equal))


def gates(core, name, logits, comb, kind, capacity=None):
    nc = core.nc
    with Scope(core, name) as sc:
        psum = sc.banks()
        new = lambda n, e=8: sc.sb(n, [P, TILES, e])
        l, cand, one, two, t8, p8, rank1, rank2, tot = [new(n) for n in
            ("l", "cand", "one", "two", "t8", "p8", "rank1", "rank2", "tot")]
        tot_b = new("tot_b")
        best, v1, v2, r, ex = [sc.sb(n, [P, TILES]) for n in ("best", "v1", "v2", "r", "ex")]
        s_link, s_exp, s_need, s_rank = sc.sem("link"), sc.sem("exp"), sc.sem("need"), sc.sem("rank")
        order = spread(core.const("experts"), TILES, 1)
        flat = lambda a: a[:].rearrange("p t e -> p (t e)")
        block = sc.open_block()

        @block.vector
        def _(dve):
            link = Link(dve, s_link, 0)
            tt = lambda out, a, b, op: link(dve.tensor_tensor(out, a, b, op))
            over = lambda a: spread(a[:], 8, 2)
            link(dve.tensor_copy(l[:], logits[:]))
            if kind == "probs":
                link(dve.tensor_reduce(v1[:], l[:], AX.X, ALU.max))
                dve.tensor_tensor(t8[:], l[:], over(v1), ALU.subtract).then_inc(s_need, 1)
                dve.wait_ge(s_exp, 1)
                link(dve.tensor_reduce(r[:], p8[:], AX.X, ALU.add))
                link(dve.reciprocal(v1[:], r[:]))
                tt(l[:], p8[:], over(v1), ALU.mult)
            first_of_max(dve, link, l[:], best[:], cand[:], one[:], order)
            if kind == "top1":
                link(dve.tensor_copy(comb[:], one[:]))
                return
            link(dve.tensor_reduce(v1[:], l[:], AX.X, ALU.max))
            link(dve.scalar_tensor_tensor(out=t8[:], in0=one[:], scalar=-1e30, in1=l[:], op0=ALU.mult, op1=ALU.add))
            link(dve.tensor_reduce(v2[:], t8[:], AX.X, ALU.max))
            first_of_max(dve, link, t8[:], best[:], cand[:], two[:], order)
            dve.tensor_tensor(ex[:], v2[:], v1[:], ALU.subtract).then_inc(s_need, 1)
            dve.wait_ge(s_exp, 2 if kind == "probs" else 1)
            link(dve.tensor_scalar(ex[:], r[:], 1.0, None, ALU.add))
            link(dve.reciprocal(v1[:], ex[:]))
            tt(v2[:], v1[:], r[:], ALU.mult)
            if kind == "capacity":
                dve.wait_ge(s_rank, 1)
                ranks = [psum[:, a, 0:256].rearrange("p (t e) -> p t e", e=8) for a in range(4)]
                for mine, rank, out in ((0, rank1, one), (1, rank2, two)):
                    link(dve.memset(tot[:, 0:1], 0.0))
                    link(dve.tensor_copy(tot[:, 1:TILES], ranks[2 * mine + 1][:, 0:TILES - 1]))
                    a, b, step = tot, tot_b, 1
                    while step < TILES:
                        link(dve.tensor_copy(b[:, 0:step], a[:, 0:step]))
                        tt(b[:, step:TILES], a[:, step:TILES], a[:, 0:TILES - step], ALU.add)
                        a, b, step = b, a, 2 * step
                    tt(rank[:], a[:], ranks[2 * mine], ALU.add)
                    if mine == 0:
                        tt(cand[:, 0], a[:, TILES - 1], ranks[1][:, TILES - 1], ALU.add)
                    else:
                        tt(rank[:], rank[:], spread(cand[:, 0], TILES, 1), ALU.add)
                    link(dve.tensor_scalar(t8[:], rank[:], float(capacity), None, ALU.is_le))
                    tt(out[:], out[:], t8[:], ALU.mult)
            tt(one[:], one[:], over(v1), ALU.mult)
            tt(two[:], two[:], over(v2), ALU.mult)
            tt(comb[:], one[:], two[:], ALU.add)

        @block.scalar
        def _(act):
            if kind == "probs":
                act.wait_ge(s_need, 1)
                act.activation(p8[:], t8[:], ACT.Exp).then_inc(s_exp, 1)
            if kind != "top1":
                act.wait_ge(s_need, 2 if kind == "probs" else 1)
                act.activation(r[:], ex[:], ACT.Exp).then_inc(s_exp, 1)

        @block.tensor
        def _(pe):
            if kind == "capacity":
                pe.wait_ge(s_need, 1)
                for a, (table, choice) in enumerate((("upto", one), ("ones", one), ("upto", two), ("ones", two))):
                    last = pe.matmul(psum[:, a, 0:256], core.const(table), flat(choice), start=True, stop=True)
                last.then_inc(s_rank, 1)
        sc.close_block()


def experts(core, name, weights, hT_all, comb, E, nf, kind, base=None, shared=False, out_bias=False, b2=False):
    nc, X = core.nc, core.X
    pair = kind in ("silu", "glu")
    width = 2 if pair else 1
    jobs = [(e, nf) for e in range(E)] + ([(E, 1)] if shared else [])
    NJ = len(jobs)
    blocks = sum(n for _, n in jobs)
    first_block = [sum(n for _, n in jobs[:e]) for e in range(NJ)]
    RING = 4 // width
    with Scope(core, name) as sc:
        psum = sc.banks()
        w, arrived, fetch = sc.weights(weights)
        act_sb = sc.sb("act", [P, RING, CHUNK]) if pair else None
        hidden = sc.sb("hidden", [P, 2, nf, CHUNK])
        combT = sc.sb("combT", [8, TPC, P]) if b2 else None
        s_up, s_act, s_hidden = sc.sem("up"), sc.sem("act"), sc.sem("hidden")
        s_down, s_acc, s_base = sc.sem("down"), sc.sem("acc"), sc.sem("base")
        s_cT, s_combT, s_b2 = sc.sem("cT"), sc.sem("combT"), sc.sem("b2")
        comb_now = sc.sb("comb_now", [P, TPC, 8]) if comb is not None else None
        s_comb, s_b2_added = sc.sem("comb"), sc.sem("b2_added")
        block = sc.open_block()

        @block.sync
        def _(sp):
            fetch(sp)

        @block.tensor
        def _(pe):
            arrived(pe)
            with pe.Fori(0, CHUNKS) as c:
                rhs = hT_all[:, bass.ds(c * CHUNK, CHUNK)]
                if b2:
                    pe.wait_ge(s_comb, c + 1)
                    for k in range(TPC):
                        last = pe.transpose(psum[0:8, 6, k * P:(k + 1) * P], comb_now[:, k], core.const("ident"))
                    last.then_inc(s_cT, 1)

                def up(j):
                    for f in range(jobs[j][1]):
                        m = first_block[j] + f
                        if m >= RING:
                            pe.wait_ge(s_hidden, c * blocks + m - RING + 1)
                        for half in range(width):
                            last = pe.matmul(psum[:, (m % RING) * width + half], w("up")[:, (m * width + half) * P:(m * width + half + 1) * P],
                                             rhs, start=True, stop=True)
                        last.then_inc(s_up, 1)

                def down(j):
                    n = jobs[j][1]
                    pe.wait_ge(s_hidden, c * blocks + first_block[j] + n)
                    if j >= 2:
                        pe.wait_ge(s_acc, c * NJ + j - 1)
                    for k in range(TPC):
                        for f in range(n):
                            m = first_block[j] + f
                            last = pe.matmul(psum[:, 4 + j % 2, k * P:(k + 1) * P], hidden[:, j % 2, f, k * P:(k + 1) * P],
                                             w("down")[:, m * P:(m + 1) * P], start=(f == 0), stop=(f == n - 1))
                    last.then_inc(s_down, 1)

                for j in range(NJ + 1):
                    if j < NJ:
                        up(j)
                    if j == 0 and b2:
                        pe.wait_ge(s_combT, c + 1)
                        for k in range(TPC):
                            last = pe.matmul(psum[:, 7, k * P:(k + 1) * P], combT[:, k], w("b2")[0:8], start=True, stop=True)
                        last.then_inc(s_b2, 1)
                    if j >= 1:
                        down(j - 1)

        @block.scalar
        def _(act):
            arrived(act)
            with act.Fori(0, CHUNKS) as c:
                if b2:
                    act.wait_ge(s_cT, c + 1)
                    act.activation(combT[:].rearrange("p k t -> p (k t)"), psum[0:8, 6], ACT.Copy).then_inc(s_combT, 1)
                for j in range(NJ):
                    for f in range(jobs[j][1]):
                        m = first_block[j] + f
                        at = (m % RING) * width
                        act.wait_ge(s_up, c * blocks + m + 1)
                        if kind == "silu":
                            if m >= RING:
                                act.wait_ge(s_hidden, c * blocks + m - RING + 1)
                            act.activation(act_sb[:, m % RING], psum[:, at], ACT.Silu).then_inc(s_act, 1)
                        elif kind == "glu":
                            if m >= RING:
                                act.wait_ge(s_hidden, c * blocks + m - RING + 1)
                            act.activation(act_sb[:, m % RING], psum[:, at + 1], ACT.Sigmoid,
                                           bias=w("b1")[:, 2 * m + 1:2 * m + 2]).then_inc(s_act, 1)
                        else:
                            if f == 0 and j >= 2:
                                act.wait_ge(s_down, c * NJ + j - 1)
                            elif f == 0 and j < 2:
                                act.wait_ge(s_base, c + 1)
                            act.activation(hidden[:, j % 2, f], psum[:, at],
                                           ACT.Gelu_apprx_tanh if kind == "gelu_tanh" else ACT.Gelu,
                                           bias=w("b1")[:, m:m + 1] if kind == "gelu_tanh" else 0.0).then_inc(s_hidden, 1)

        @block.vector
        def _(dve):
            arrived(dve)
            with dve.Fori(0, CHUNKS) as c:
                chunk = bass.ds(c * TPC, TPC)
                if comb is not None:
                    dve.tensor_copy(comb_now[:], comb[:, chunk]).then_inc(s_comb, 1)
                if out_bias:
                    dve.tensor_tensor(X[:, chunk], X[:, chunk], spread(w("bo"), TPC, 1), ALU.add).then_inc(s_b2, 1)
                    dve.wait_ge(s_b2, c + 1)
                if base is not None:
                    dve.tensor_tensor(X[:, chunk], X[:, chunk], base[:, chunk], ALU.add).then_inc(s_base, 1)
                else:
                    dve.engine_nop().then_inc(s_base, 1)
                if comb is not None:
                    dve.wait_ge(s_comb, c + 1)
                dve.wait_ge(s_base, c + 1)
                if b2:
                    dve.wait_ge(s_b2, c + 1)
                    dve.tensor_tensor(X[:, chunk], psum[:, 7].rearrange("p (k d) -> p k d", k=TPC), X[:, chunk],
                                      ALU.add).then_inc(s_b2_added, 1)
                    dve.wait_ge(s_b2_added, c + 1)

                def add(j):
                    dve.wait_ge(s_down, c * NJ + j + 1)
                    if j >= 1:
                        dve.wait_ge(s_acc, c * NJ + j)
                    if comb is None or j >= E:
                        dve.tensor_tensor(X[:, chunk], psum[:, 4 + j % 2].rearrange("p (k d) -> p k d", k=TPC), X[:, chunk],
                                          ALU.add).then_inc(s_acc, 1)
                        return
                    for k in range(TPC):
                        xk = X[:, bass.ds(c * TPC + k, 1)]
                        last = dve.scalar_tensor_tensor(out=xk, in0=psum[:, 4 + j % 2:5 + j % 2, k * P:(k + 1) * P],
                                                        scalar=comb_now[:, k, j:j + 1], in1=xk, op0=ALU.mult, op1=ALU.add)
                    last.then_inc(s_acc, 1)

                for j in range(NJ):
                    if pair:
                        for f in range(jobs[j][1]):
                            m = first_block[j] + f
                            at = (m % RING) * width
                            dve.wait_ge(s_act, c * blocks + m + 1)
                            if f == 0 and j >= 2:
                                dve.wait_ge(s_down, c * NJ + j - 1)
                            if kind == "silu":
                                dve.tensor_tensor(hidden[:, j % 2, f], act_sb[:, m % RING], psum[:, at + 1], ALU.mult).then_inc(s_hidden, 1)
                            else:
                                dve.scalar_tensor_tensor(out=hidden[:, j % 2, f], in0=psum[:, at], scalar=w("b1")[:, 2 * m:2 * m + 1],
                                                         in1=act_sb[:, m % RING], op0=ALU.add, op1=ALU.mult).then_inc(s_hidden, 1)
                    if j >= 1:
                        add(j - 1)
                add(NJ - 1)
                dve.wait_ge(s_acc, c * NJ + NJ)
        sc.close_block()



def cross_attention(core, name, weights, hT_all, context, scale, mask=None):
    nc, X = core.nc, core.X
    N, G = 8, 4
    own, ident, fold_m = core.const("own8"), core.const("ident"), core.const("fold")
    with Scope(core, name) as sc:
        psum = sc.banks()
        S_BANK, K_BANK, V_BANK, T_BANK, O_BANK = 0, 4, 5, 6, 7
        w, arrived, fetch = sc.weights(weights)
        ctx_sb = sc.sb("context", [P, N, SK])
        kT = sc.sb("kT", [P, 3, SK])
        v_sb = sc.sb("v", [P, 3, 2, P])
        v_last = sc.sb("v_last", [G, 3, P])
        qT = sc.sb("qT", [P, 2, P])
        q_heads = sc.sb("q_heads", [P, 2, BPT, 16, S])
        E = sc.sb("E", [P, 2, G, SK])
        ET = sc.sb("ET", [P, 2, 2, G * P])
        E_last = sc.sb("E_last", [G, 2, P])
        top = sc.sb("top", [P, 2, G])
        negtop = sc.sb("negtop", [P, 2, G])
        total = sc.sb("total", [P, 2, G])
        inverse = sc.sb("inverse", [P, 2, G])
        O = sc.sb("O", [P, 2, 2, P])
        aT = sc.sb("aT", [P, 2, P])
        Xb = sc.sb("sum", [P, 2, P])
        if mask is not None:
            mask_int = sc.sb("mask_int", [P, SK], mybir.dt.int32)
            mask_neg = sc.sb("mask_neg", [P, SK], BF16)
            ident_bf = sc.sb("ident_bf", [P, P], BF16)
        s_ctx = [sc.sem(f"ctx{n}") for n in range(N)]
        s_mask, s_mask_ready = sc.sem("mask"), sc.sem("mask_ready")
        s_qp, s_q, s_heads = sc.sem("qp"), sc.sem("q"), sc.sem("heads")
        s_kp, s_k, s_vp, s_v = sc.sem("kp"), sc.sem("k"), sc.sem("vp"), sc.sem("v")
        s_score, s_top, s_neg, s_exp = sc.sem("score"), sc.sem("top"), sc.sem("neg"), sc.sem("exp")
        s_t, s_ET, s_pv, s_fold = sc.sem("t"), sc.sem("ET"), sc.sem("pv"), sc.sem("fold")
        s_ET1, s_ETl, s_tl = sc.sem("ET1"), sc.sem("ETl"), sc.sem("tl")
        s_t1 = sc.sem("t1")
        s_inv, s_scaled, s_own, s_aT = sc.sem("inv"), sc.sem("scaled"), sc.sem("own"), sc.sem("aT")
        s_out, s_bias, s_done, passed_pool = sc.sem("out"), sc.sem("bias"), sc.sem("done"), sc.sem("passed_pool")
        passed_dve = sc.sem("passed_dve")
        block = sc.open_block()
        TURNS = B // N

        @block.sync
        def _(sp):
            fetch(sp)
            if mask is not None:
                for j in range(4):
                    sp.dma_start(mask_int[j * S:(j + 1) * S], mask).then_inc(s_mask, 16)
            for n in range(N):
                sp.dma_start(ctx_sb[:, n], context[:, n]).then_inc(s_ctx[n], 16)
            with sp.Fori(1, TURNS) as i:
                for n in range(N):
                    sp.wait_ge(s_vp, i * N - N + n + 1)
                    sp.dma_start(ctx_sb[:, n], context[:, bass.ds(i * N + n, 1)]).then_inc(s_ctx[n], 16)

        @block.gpsimd
        def _(pool):
            with pool.Fori(0, TURNS) as i:
                for t in range(2):
                    pool.wait_ge(s_q, i * 2 + t + 1)
                    pool.tensor_tensor(q_heads[:, t], spread(qT[:, t].rearrange("p (b s) -> p b s", s=S), 16, 2),
                                       spread(spread(core.const("heads16"), BPT, 1), S, 3), ALU.mult).then_inc(s_heads, 1)

        @block.tensor
        def _(pe):
            arrived(pe)
            if mask is not None:
                pe.wait_ge(s_mask_ready, 2)
            with pe.Fori(0, TURNS) as i:
                for t in range(2):
                    pe.matmul(psum[:, T_BANK, t * P:(t + 1) * P], w("wq"), hT_all[:, bass.ds((i * 2 + t) * P, P)],
                              start=True, stop=True).then_inc(s_qp, 1)

                def project(n):
                    pe.wait_ge(s_ctx[n], i * 16 + 16)
                    if n >= 1:
                        pe.wait_ge(s_k, i * N + n)
                    pe.matmul(psum[:, K_BANK, 0:SK], w("wk"), ctx_sb[:, n], start=True, stop=True).then_inc(s_kp, 1)
                    if n >= 1:
                        pe.wait_ge(s_v, i * N + n)
                    for c in range(2):
                        pe.matmul(psum[:, V_BANK, c * P:(c + 1) * P], ctx_sb[:, n, c * P:(c + 1) * P], w("wv"),
                                  start=True, stop=True)
                    pe.matmul(psum[0:G, V_BANK, 2 * P:3 * P], ctx_sb[:, n, SK - 1:SK].to_broadcast([P, G]), w("wv"),
                              start=True, stop=True).then_inc(s_vp, 1)

                def scores(n):
                    pe.wait_ge(s_k, i * N + n + 1)
                    if n % 4 == 0:
                        pe.wait_ge(s_heads, i * 2 + n // 4 + 1)
                    for g in range(G):
                        if n >= 1:
                            pe.wait_ge(s_exp, (i * N + n - 1) * G + g + 1)
                        last = pe.matmul(psum[:, S_BANK + g, 0:SK], q_heads[:, n // 4, n % 4, 4 * g:4 * g + 4].rearrange("p h s -> p (h s)"),
                                         kT[:, n % 3], start=True, stop=mask is None)
                        if mask is not None:
                            last = pe.matmul(psum[:, S_BANK + g, 0:SK], ident_bf[:], mask_neg[:], start=False, stop=True)
                    last.then_inc(s_score, 1)

                def turn(n):
                    pe.wait_ge(s_exp, (i * N + n) * G + G)
                    for c in range(2):
                        if c == 1:
                            pe.wait_ge(s_ET, i * N + n + 1)
                        elif n >= 1:
                            pe.wait_ge(s_ET1, i * N + n)
                        else:
                            pe.wait_ge(s_q, i * 2 + 2)
                        for g in range(G):
                            last = pe.transpose(psum[:, T_BANK, g * P:(g + 1) * P], E[:, n % 2, g, c * P:(c + 1) * P], ident)
                        last.then_inc((s_t, s_t1)[c], 1)
                        if c == 0:
                            if n >= 1:
                                pe.wait_ge(s_aT, i * N + n)
                            if n == 4:
                                pe.wait_ge(s_bias, i * 2 + 1)
                            pe.transpose(psum[0:G, O_BANK, 2 * P:3 * P], E[:, n % 2, :, SK - 1], ident).then_inc(s_tl, 1)

                def values(n):
                    pe.wait_ge(s_v, i * N + n + 1)
                    pe.wait_ge(s_ETl, i * N + n + 1)
                    out = psum[:, O_BANK, 0:P]
                    pe.matmul(out, E_last[:, n % 2], v_last[:, n % 3], start=True, stop=False)
                    pe.wait_ge(s_ET1, i * N + n + 1)
                    for g in range(G):
                        for c in range(2):
                            last = pe.matmul(psum[:, O_BANK, g * 32:(g + 1) * 32], ET[:, n % 2, c, g * P:(g + 1) * P],
                                             v_sb[:, n % 3, c, g * 32:(g + 1) * 32], start=False,
                                             stop=(g == G - 1 and c == 1))
                    last.then_inc(s_pv, 1)

                def fold(n):
                    pe.wait_ge(s_own, i * N + n + 1)
                    pe.matmul(psum[:, O_BANK, P:P + S], O[:, n % 2, 1], fold_m, start=True, stop=True).then_inc(s_fold, 1)

                def output(t):
                    pe.wait_ge(s_aT, i * N + 4 * t + 4)
                    pe.matmul(psum[:, O_BANK, 3 * P:4 * P], aT[:, t], w("wo"), start=True, stop=True).then_inc(s_out, 1)

                project(0)
                for step in range(N + 2):
                    if step < N:
                        scores(step)
                    if step >= 2:
                        fold(step - 2)
                    if step + 1 < N:
                        project(step + 1)
                    if step - 2 in (3, 7):
                        output((step - 2) // 4)
                    if 1 <= step < N + 1:
                        turn(step - 1)
                        values(step - 1)

        @block.scalar
        def _(act):
            arrived(act)
            with act.Fori(0, TURNS) as i:
                act.wait_ge(s_qp, i * 2 + 2)
                for t in range(2):
                    act.activation(qT[:, t], psum[:, T_BANK, t * P:(t + 1) * P], ACT.Identity, bias=w("bq")).then_inc(s_q, 1)

                def keys(n):
                    act.wait_ge(s_kp, i * N + n + 1)
                    if n >= 3:
                        act.wait_ge(s_score, i * N + n - 2)
                    act.activation(kT[:, n % 3], psum[:, K_BANK, 0:SK], ACT.Identity, bias=w("bk")).then_inc(s_k, 1)

                def exponentials(n):
                    act.wait_ge(s_neg, i * N + n + 1)
                    if n >= 2:
                        act.wait_ge(s_t1, i * N + n - 1)
                        act.wait_ge(s_inv, i * N + n - 1)
                    for g in range(G):
                        act.activation(E[:, n % 2, g], psum[:, S_BANK + g, 0:SK], ACT.Exp, scale=scale,
                                       bias=negtop[:, n % 2, g:g + 1], accum_out=total[:, n % 2, g:g + 1]).then_inc(s_exp, 1)

                def second_half(n):
                    act.wait_ge(s_t1, i * N + n + 1)
                    act.activation(ET[:, n % 2, 1], psum[:, T_BANK], ACT.Copy).then_inc(s_ET1, 1)

                def folded(n):
                    act.wait_ge(s_fold, i * N + n + 1)
                    act.activation(aT[:, n // 4, (n % 4) * S:(n % 4 + 1) * S], psum[:, O_BANK, P:P + S], ACT.Identity,
                                   bias=w("bv")).then_inc(s_aT, 1)

                keys(0)
                for step in range(N + 2):
                    if step >= 2:
                        folded(step - 2)
                    if step + 1 < N:
                        keys(step + 1)
                    if step < N:
                        exponentials(step)
                    if 1 <= step < N + 1:
                        second_half(step - 1)

        @block.vector
        def _(dve):
            arrived(dve)
            if mask is not None:
                dve.wait_ge(s_mask, 64)
                dve.tensor_copy(ident_bf[:], ident).then_inc(s_mask_ready, 1)
                dve.tensor_scalar(mask_neg[:], mask_int[:], 0.0, -1e30, ALU.is_equal, ALU.mult).then_inc(s_mask_ready, 1)
            with dve.Fori(0, TURNS) as i:
                def values_out(n):
                    dve.wait_ge(s_vp, i * N + n + 1)
                    if n >= 3:
                        dve.wait_ge(s_pv, i * N + n - 2)
                    dve.tensor_copy(v_sb[:, n % 3], psum[:, V_BANK, 0:2 * P].rearrange("p (c d) -> p c d", c=2))
                    dve.tensor_tensor(v_last[:, n % 3], psum[0:G, V_BANK, 2 * P:3 * P], core.const("group_of")[0:G],
                                      ALU.mult).then_inc(s_v, 1)

                def maximum(n):
                    dve.wait_ge(s_score, i * N + n + 1)
                    dve.tensor_reduce(top[:, n % 2], psum[:, S_BANK:S_BANK + G, 0:SK], AX.X, ALU.max).then_inc(s_top, 1)
                    dve.wait_ge(s_top, i * N + n + 1)
                    dve.tensor_scalar(negtop[:, n % 2], top[:, n % 2], -scale, None, ALU.mult).then_inc(s_neg, 1)

                def first_half(n):
                    dve.wait_ge(s_exp, (i * N + n) * G + G)
                    dve.reciprocal(inverse[:, n % 2], total[:, n % 2]).then_inc(s_inv, 1)
                    dve.wait_ge(s_t, i * N + n + 1)
                    dve.tensor_copy(ET[:, n % 2, 0], psum[:, T_BANK]).then_inc(s_ET, 1)
                    dve.wait_ge(s_tl, i * N + n + 1)
                    dve.tensor_copy(E_last[:, n % 2], psum[0:G, O_BANK, 2 * P:3 * P]).then_inc(s_ETl, 1)

                def scaled(n):
                    dve.wait_ge(s_pv, i * N + n + 1)
                    dve.wait_ge(s_inv, i * N + n + 1)
                    dve.tensor_tensor(O[:, n % 2, 0].rearrange("p (g c) -> p g c", g=G),
                                      psum[:, O_BANK, 0:P].rearrange("p (g c) -> p g c", g=G),
                                      spread(inverse[:, n % 2], 32, 2), ALU.mult).then_inc(s_scaled, 1)
                    dve.wait_ge(s_scaled, i * N + n + 1)
                    dve.tensor_tensor(O[:, n % 2, 1].rearrange("p (g c) -> p g c", g=G),
                                      O[:, n % 2, 0].rearrange("p (g c) -> p g c", g=G),
                                      spread(own, G, 1), ALU.mult).then_inc(s_own, 1)

                def output(t):
                    dve.wait_ge(s_out, i * 2 + t + 1)
                    dve.tensor_tensor(Xb[:, t], psum[:, O_BANK, 3 * P:4 * P], w("bo"), ALU.add).then_inc(s_bias, 1)
                    dve.wait_ge(s_bias, i * 2 + t + 1)
                    xt = X[:, bass.ds(i * 2 + t, 1)]
                    dve.tensor_tensor(xt, Xb[:, t:t + 1], xt, ALU.add).then_inc(s_done, 1)

                values_out(0)
                for step in range(N + 2):
                    if step < N:
                        maximum(step)
                    if step + 1 < N:
                        values_out(step + 1)
                    if step - 2 in (3, 7):
                        output((step - 2) // 4)
                    if 1 <= step < N + 1:
                        first_half(step - 1)
                        scaled(step - 1)
        sc.close_block()


GENERATED = {}
_at = 0
for _name, _width in (("ca", 384), ("cp", 128), ("cf", 512), ("cm", 512),
                      ("ca_b", 3), ("cp_b", 128), ("cf_b", 4), ("cm_b", 128)):
    GENERATED[_name] = (_at, _width)
    _at += _width
GEN_WIDTH = _at


def generate(core, name, weights, out):
    nc = core.nc
    with Scope(core, name) as sc:
        w, arrived, fetch = sc.weights(weights)
        s_link, s_sum, s_tanh = sc.sem("link"), sc.sem("sum"), sc.sem("tanh")
        block = sc.open_block()

        @block.sync
        def _(sp):
            fetch(sp)

        @block.vector
        def _(dve):
            link = Link(dve, s_link, 0)
            arrived(dve)
            link(dve.tensor_copy(out[:, GEN_WIDTH:GEN_WIDTH + 4], w("norms")))
            for n, (at, width) in enumerate(GENERATED.values()):
                sl = slice(at, at + width)
                link(dve.tensor_scalar(out[:, sl], w("sub0")[:, sl], w("wl")[:, 2 * n:2 * n + 1], None, ALU.mult))
                dve.scalar_tensor_tensor(out=out[:, sl], in0=w("sub1")[:, sl], scalar=w("wl")[:, 2 * n + 1:2 * n + 2],
                                         in1=out[:, sl], op0=ALU.mult, op1=ALU.add).then_inc(s_sum, 1)
            dve.wait_ge(s_tanh, 1)
            link(dve.tensor_tensor(out[:, 0:GEN_WIDTH], out[:, 0:GEN_WIDTH], w("W"), ALU.mult))
            link(dve.tensor_tensor(out[:, 0:GEN_WIDTH], out[:, 0:GEN_WIDTH], w("B"), ALU.add))

        @block.scalar
        def _(act):
            act.wait_ge(s_sum, len(GENERATED))
            act.activation(out[:, 0:GEN_WIDTH], out[:, 0:GEN_WIDTH], ACT.Tanh).then_inc(s_tanh, 1)
        sc.close_block()


ROUND = 12582912.0


def quantised_ffn(core, name, weights, hT_all):
    nc, X = core.nc, core.X
    PAIRS, NF = CHUNKS // 2, 4
    ident, ones = core.const("ident"), core.const("ones")
    with Scope(core, name) as sc:
        psum = sc.banks()
        w, arrived, fetch = sc.weights(weights)
        w_abs = sc.sb("w_abs", [P, 2, NF * P])
        w_int = sc.sb("w_int", [P, 2, NF * P])
        up = sc.sb("up", [P, NF * P], BF16)
        down = sc.sb("down", [P, NF * P], BF16)
        s_w = sc.sb("scale_w", [P, NF + 1])
        peak = sc.sb("peak", [P, 4])
        s_in = sc.sb("scale_in", [P, 2])
        inv_w = sc.sb("inverse_w", [P, NF + 1])
        inv_in = sc.sb("inverse_in", [P, 2])
        s_out = sc.sb("scale_out", [P, NF + 1])
        bq = sc.sb("bias", [P, NF + 1])
        tmp = sc.sb("bias_steps", [P, 6, NF])
        diagonal = sc.sb("diagonal", [P, 4, P])
        rows = sc.sb("rows", [P, 2, P])
        shifted = sc.sb("shifted", [P, 2, CHUNK])
        x_int = sc.sb("x_int", [P, 2, CHUNK], BF16)
        H = sc.sb("H", [P, NF, TOK])
        highest = sc.sb("highest", [P, NF, CHUNK])
        shifted2 = sc.sb("shifted2", [P, 2, NF, CHUNK])
        h_int = sc.sb("h_int", [P, 2, NF, CHUNK], BF16)
        product = sc.sb("product", [P, 2, TPC, P])
        s_link, s_w_int, s_turned, s_w_bf = sc.sem("link"), sc.sem("w_int"), sc.sem("turned"), sc.sem("w_bf")
        s_diagonal, s_spread, s_ready = sc.sem("diagonal"), sc.sem("spread"), sc.sem("ready")
        s_div, s_shift, s_x_int, s_up, s_H = sc.sem("div"), sc.sem("shift"), sc.sem("x_int"), sc.sem("up"), sc.sem("H")
        s_high, s_div2, s_shift2, s_h_int = sc.sem("high"), sc.sem("div2"), sc.sem("shift2"), sc.sem("h_int")
        s_down, s_prod, s_bias, s_done = sc.sem("down"), sc.sem("prod"), sc.sem("bias"), sc.sem("done")
        passed_act, passed_dve = sc.sem("passed_act"), sc.sem("passed_dve")
        block = sc.open_block()

        @block.sync
        def _(sp):
            fetch(sp)

        @block.vector
        def _(dve):
            link = Link(dve, s_link, 0)
            arrived(dve)

            def divided(out, x, inverse):
                return dve.tensor_scalar(out, x, inverse, ROUND, ALU.mult, ALU.add)

            def whole_maximum(n, least, steps):
                dve.tensor_scalar(diagonal[:, n], ident, peak[:, 2 * n:2 * n + 1], None, ALU.mult).then_inc(s_diagonal, 1)
                dve.wait_ge(s_spread, n + 1)
                link(dve.tensor_reduce(peak[:, 2 * n + 1:2 * n + 2], psum[:, n, 0:P], AX.X, ALU.max))
                link(dve.tensor_scalar(s_in[:, n:n + 1], peak[:, 2 * n + 1:2 * n + 2], least, 1.0 / steps, ALU.max, ALU.mult))
                link(dve.reciprocal(inv_in[:, n:n + 1], s_in[:, n:n + 1]))

            def bias_on_grid(n, at, width):
                scale, b = s_out[:, at:at + width], w("b")[:, at:at + width]
                r, a, ra, small, sign = (tmp[:, k, 0:width] for k in range(5))
                link(dve.tensor_scalar(scale, s_w[:, at:at + width], s_in[:, n:n + 1], None, ALU.mult))
                link(dve.reciprocal(tmp[:, 5, 0:width], scale))
                link(dve.tensor_tensor(r, b, tmp[:, 5, 0:width], ALU.mult))
                link(dve.scalar_tensor_tensor(out=a, in0=r, scalar=-1.0, in1=r, op0=ALU.mult, op1=ALU.max))
                link(dve.tensor_scalar(ra, a, 8388608.0, 8388608.0, ALU.add, ALU.subtract))
                link(dve.tensor_tensor(ra, ra, a, ALU.subtract))
                link(dve.tensor_scalar(small, a, 8388608.0, None, ALU.is_lt))
                link(dve.tensor_tensor(ra, ra, small, ALU.mult))
                link(dve.tensor_tensor(a, a, ra, ALU.add))
                link(dve.tensor_scalar(sign, r, 0.0, 2.0, ALU.is_ge, ALU.mult))
                link(dve.tensor_scalar(sign, sign, 1.0, None, ALU.subtract))
                link(dve.tensor_tensor(a, a, sign, ALU.mult))
                link(dve.tensor_tensor(bq[:, at:at + width], a, scale, ALU.mult))

            link(dve.tensor_reduce(peak[:, 0:1], hT_all[:], AX.X, ALU.max))
            for n, part in enumerate(("w1", "w2")):
                link(dve.scalar_tensor_tensor(out=w_abs[:, n], in0=w(part), scalar=-1.0, in1=w(part), op0=ALU.mult, op1=ALU.max))
            link(dve.tensor_reduce(s_w[:, 0:NF], w_abs[:, 0].rearrange("p (f d) -> p f d", d=P), AX.X, ALU.max))
            link(dve.tensor_reduce(s_w[:, NF:NF + 1], w_abs[:, 1], AX.X, ALU.max))
            link(dve.tensor_scalar(s_w[:], s_w[:], 1e-8, 1.0 / 127.0, ALU.max, ALU.mult))
            link(dve.reciprocal(inv_w[:], s_w[:]))
            for f in range(NF):
                link(divided(w_int[:, 0, f * P:(f + 1) * P], w("w1")[:, f * P:(f + 1) * P], inv_w[:, f:f + 1]))
            link(divided(w_int[:, 1], w("w2"), inv_w[:, NF:NF + 1]))
            link(dve.tensor_scalar(w_int[:], w_int[:], ROUND + 127.0, ROUND - 128.0, ALU.min, ALU.max))
            dve.tensor_scalar(w_int[:], w_int[:], ROUND, None, ALU.subtract).then_inc(s_w_int, 1)
            whole_maximum(0, 1e-8, 255.0)
            bias_on_grid(0, 0, NF)
            link(dve.memset(highest[:], 0.0))
            dve.engine_nop().then_inc(s_ready, 1)
            with dve.Fori(0, PAIRS) as i:
                for u in range(2):
                    divided(shifted[:, u:u + 1], hT_all[:].rearrange("p (c n) -> p c n", n=CHUNK)[:, bass.ds(i * 2 + u, 1)],
                            inv_in[:, 0:1]).then_inc(s_div, 1)
                    dve.wait_ge(s_div, i * 2 + u + 1)
                    dve.tensor_scalar(shifted[:, u], shifted[:, u], ROUND + 255.0, ROUND, ALU.min, ALU.max).then_inc(s_shift, 1)
                for u in range(2):
                    dve.wait_ge(s_H, (i * 2 + u) * NF + NF)
                    dve.tensor_tensor(highest[:], H[:, :, bass.ds((i * 2 + u) * CHUNK, CHUNK)], highest[:], ALU.max).then_inc(s_high, 1)
                    dve.wait_ge(s_high, i * 2 + u + 1)
            link(dve.tensor_reduce(peak[:, 2:3], highest[:], AX.XY, ALU.max))
            whole_maximum(1, 1e-8, 255.0)
            bias_on_grid(1, NF, 1)
            dve.tensor_scalar(diagonal[:, 2], ident, s_out[:, NF:NF + 1], None, ALU.mult).then_inc(s_diagonal, 1)
            dve.tensor_scalar(diagonal[:, 3], ident, bq[:, NF:NF + 1], None, ALU.mult).then_inc(s_diagonal, 1)
            dve.wait_ge(s_spread, 4)
            dve.tensor_copy(rows[:], psum[:, 2, 0:2 * P].rearrange("p (n d) -> p n d", n=2)).then_inc(s_ready, 1)
            dve.wait_ge(s_ready, 2)
            with dve.Fori(0, PAIRS) as i:
                for u in range(2):
                    dve.tensor_scalar(shifted2[:, u], H[:, :, bass.ds((i * 2 + u) * CHUNK, CHUNK)], inv_in[:, 1:2], ROUND,
                                      ALU.mult, ALU.add).then_inc(s_div2, 1)
                    dve.wait_ge(s_div2, i * 2 + u + 1)
                    dve.tensor_scalar(shifted2[:, u], shifted2[:, u], ROUND + 255.0, ROUND, ALU.min, ALU.max).then_inc(s_shift2, 1)
                for u in range(2):
                    dve.wait_ge(s_down, i * 2 + u + 1)
                    dve.tensor_tensor(product[:, u], psum[:, 4 + u].rearrange("p (k d) -> p k d", k=TPC),
                                      spread(rows[:, 0], TPC, 1), ALU.mult).then_inc(s_prod, 1)
                    dve.wait_ge(s_prod, i * 2 + u + 1)
                    dve.wait_ge(s_bias, i * 2 + u + 1)
                    xc = X[:, bass.ds((i * 2 + u) * TPC, TPC)]
                    dve.tensor_tensor(xc, product[:, u], xc, ALU.add).then_inc(s_done, 1)

        @block.gpsimd
        def _(pool):
            pool.wait_ge(s_ready, 2)
            with pool.Fori(0, CHUNKS) as c:
                xc = X[:, bass.ds(c * TPC, TPC)]
                pool.tensor_tensor(xc, xc, spread(rows[:, 1], TPC, 1), ALU.add).then_inc(s_bias, 1)

        @block.tensor
        def _(pe):
            pe.wait_ge(s_w_int, 1)
            for n in range(2):
                for f in range(NF):
                    pe.transpose(psum[:, 6 + n, f * P:(f + 1) * P], w_int[:, n, f * P:(f + 1) * P], ident).then_inc(s_turned, 1)
            pe.wait_ge(s_diagonal, 1)
            pe.matmul(psum[:, 0, 0:P], ones, diagonal[:, 0], start=True, stop=True).then_inc(s_spread, 1)
            pe.wait_ge(s_w_bf, 2)
            with pe.Fori(0, PAIRS) as i:
                for u in range(2):
                    pe.wait_ge(s_x_int, i * 2 + u + 1)
                    for f in range(NF):
                        pe.matmul(psum[:, 4 * u + f], up[:, f * P:(f + 1) * P], x_int[:, u], start=True, stop=True).then_inc(s_up, 1)
            pe.wait_ge(s_diagonal, 2)
            pe.matmul(psum[:, 1, 0:P], ones, diagonal[:, 1], start=True, stop=True).then_inc(s_spread, 1)
            pe.wait_ge(s_diagonal, 4)
            for n in range(2):
                pe.matmul(psum[:, 2, n * P:(n + 1) * P], ones, diagonal[:, 2 + n], start=True, stop=True).then_inc(s_spread, 1)
            with pe.Fori(0, PAIRS) as i:
                for u in range(2):
                    pe.wait_ge(s_h_int, i * 2 + u + 1)
                    for k in range(TPC):
                        for f in range(NF):
                            last = pe.matmul(psum[:, 4 + u, k * P:(k + 1) * P], h_int[:, u, f, k * P:(k + 1) * P],
                                             down[:, f * P:(f + 1) * P], start=(f == 0), stop=(f == NF - 1))
                    last.then_inc(s_down, 1)

        @block.scalar
        def _(act):
            magic = core.const("magic")
            act.wait_ge(s_turned, 2 * NF)
            act.activation(up[:], psum[:, 6], ACT.Copy).then_inc(s_w_bf, 1)
            act.activation(down[:], psum[:, 7], ACT.Copy).then_inc(s_w_bf, 1)
            act.wait_ge(s_ready, 1)
            with act.Fori(0, PAIRS) as i:
                for u in range(2):
                    act.wait_ge(s_shift, i * 2 + u + 1)
                    act.activation(x_int[:, u], shifted[:, u], ACT.Identity, bias=magic).then_inc(s_x_int, 1)
                for u in range(2):
                    for f in range(NF):
                        gate(act, s_up, (i * 2 + u) * NF + f + 1, passed_act)
                        act.activation(H[:, f, bass.ds((i * 2 + u) * CHUNK, CHUNK)], psum[:, 4 * u + f], ACT.Relu,
                                       scale=s_out[:, f:f + 1], bias=bq[:, f:f + 1]).then_inc(s_H, 1)
            with act.Fori(0, PAIRS) as i:
                for u in range(2):
                    act.wait_ge(s_shift2, i * 2 + u + 1)
                    act.activation(h_int[:, u], shifted2[:, u], ACT.Identity, bias=magic).then_inc(s_h_int, 1)
        sc.close_block()



DEPTH = 6
ATTN_WIDTH, FFN_WIDTH = 5 * P + 2, 8 * P + 2


def linear_transformer(core, name, stream):
    nc, X = core.nc, core.X
    ident = core.const("ident")
    HEADS, DH = 8, P // 8
    NF = 4
    with Scope(core, name) as sc:
        psum = sc.banks()
        attn_w = sc.sb("attn_w", [P, ATTN_WIDTH])
        ffn_w = sc.sb("ffn_w", [P, FFN_WIDTH])
        wq, wk, wv, wo, bo = (attn_w[:, n * P:(n + 1) * P] for n in range(5))
        ln1, ln2 = attn_w[:, 5 * P:5 * P + 2], ffn_w[:, 8 * P:8 * P + 2]
        norm0, norm1, norm2 = Norm(sc, "ln0", "eps5"), Norm(sc, "ln1", "eps5"), Norm(sc, "ln2", "eps5")
        Y1, Y2 = sc.sb("normed1", [P, TPC, P]), sc.sb("normed2", [P, TPC, P])
        hT1, hT2 = sc.sb("hT1", [P, CHUNK]), sc.sb("hT2", [P, CHUNK])
        q, k = sc.sb("q", [P, CHUNK]), sc.sb("k", [P, CHUNK])
        q_stat, k_stat = sc.sb("q_stat", [P, 3, TPC * HEADS]), sc.sb("k_stat", [P, 3, CHUNK // S])
        k_tok, qT = sc.sb("k_tok", [P, CHUNK]), sc.sb("qT", [P, CHUNK])
        v_own = sc.sb("v_own", [P, TPC, BPT, P])
        ctx = sc.sb("ctx", [P, 2, BPT, P])
        aT = sc.sb("aT", [P, CHUNK])
        hidden = sc.sb("hidden", [P, NF, CHUNK])
        s_attn_w, s_ffn_w, s_zero = sc.sem("attn_w"), sc.sem("ffn_w"), sc.sem("zero")
        s_norm0, s_norm1, s_norm2 = sc.sem("norm0"), sc.sem("norm1"), sc.sem("norm2")
        s_turn1, s_turn2, s_hT1, s_hT2 = sc.sem("turn1"), sc.sem("turn2"), sc.sem("hT1"), sc.sem("hT2")
        s_proj, s_v = sc.sem("proj"), sc.sem("v")
        s_less, s_exp, s_soft, s_soft_link = sc.sem("less"), sc.sem("exp"), sc.sem("soft"), sc.sem("soft_link")
        s_k_turn, s_q_turn, s_k_tok, s_qT = sc.sem("k_turn"), sc.sem("q_turn"), sc.sem("k_tok"), sc.sem("qT")
        s_ctx, s_own, s_a, s_aT = sc.sem("ctx"), sc.sem("own"), sc.sem("a"), sc.sem("aT")
        s_bo, s_wo, s_mid = sc.sem("bo"), sc.sem("wo"), sc.sem("mid")
        s_slope = sc.sem("slope")
        s_up, s_hidden, s_down, s_layer = sc.sem("up"), sc.sem("hidden"), sc.sem("down"), sc.sem("layer")
        passed_dve = sc.sem("passed_dve")
        attn_dram, ffn_dram = core.packs["l_attn"][0], core.packs["l_ffn"][0]
        tiles = lambda ap: ap.rearrange("p (t c) -> p t c", c=P)
        block = sc.open_block()

        def layers(eng, A, F, both, layer_starts=None, layer_ends=None):
            with eng.Fori(0, DEPTH) as d:
                if layer_starts:
                    layer_starts(d)
                A(0, d * CHUNKS)
                with eng.Fori(0, CHUNKS // 2 - 1) as i:
                    for m in range(2):
                        both((i * 2 + m + 1, d * CHUNKS + i * 2 + m + 1), (i * 2 + m, d * CHUNKS + i * 2 + m))
                both((CHUNKS - 1, d * CHUNKS + CHUNKS - 1), (CHUNKS - 2, d * CHUNKS + CHUNKS - 2))
                F(CHUNKS - 1, d * CHUNKS + CHUNKS - 1)
                if layer_ends:
                    layer_ends(d)

        @block.sync
        def _(sp):
            sp.dma_start(attn_w[:], attn_dram[:, 0:ATTN_WIDTH]).then_inc(s_attn_w, 16)
            sp.dma_start(ffn_w[:], ffn_dram[:, 0:FFN_WIDTH]).then_inc(s_ffn_w, 16)
            with sp.Fori(1, DEPTH) as d:
                sp.wait_ge(s_mid, d * CHUNKS)
                sp.dma_start(attn_w[:], attn_dram[:, bass.ds(d * ATTN_WIDTH, ATTN_WIDTH)]).then_inc(s_attn_w, 16)
                sp.wait_ge(s_layer, d * CHUNKS)
                sp.dma_start(ffn_w[:], ffn_dram[:, bass.ds(d * FFN_WIDTH, FFN_WIDTH)]).then_inc(s_ffn_w, 16)

        @block.gpsimd
        def _(pool):
            pool.memset(v_own[:], 0.0).then_inc(s_zero, 1)
            with pool.Fori(0, CHUNKS // 2) as i:
                for u in range(2):
                    norm0.pool_rstd(pool, i * 2 + u, u)

            def add_bias(n, done):
                pool.wait_ge(s_norm1, done + 1)
                xc = stream[:, bass.ds(n * TPC, TPC)] if not isinstance(n, int) else stream[:, n * TPC:(n + 1) * TPC]
                pool.tensor_tensor(xc, xc, spread(bo, TPC, 1), ALU.add).then_inc(s_bo, 1)

            def A(n, done):
                norm1.pool_rstd(pool, done, 0)
                add_bias(n, done)

            def both(a, f):
                norm1.pool_rstd(pool, a[1], 0)
                norm2.pool_rstd(pool, f[1], 0)
                add_bias(*a)

            layers(pool, A, lambda n, done: norm2.pool_rstd(pool, done, 0), both,
                   layer_starts=lambda d: pool.wait_ge(s_attn_w, d * 16 + 16))

        @block.tensor
        def _(pe):
            def turn(Y, bank, s_from, s_to, done):
                pe.wait_ge(s_from, done + 1)
                for t in range(TPC):
                    last = pe.transpose(psum[:, bank, t * P:(t + 1) * P], Y[:, t], ident)
                last.then_inc(s_to, 1)

            def project(done):
                pe.wait_ge(s_hT1, done + 1)
                pe.matmul(psum[:, 2], wk, hT1[:], start=True, stop=True).then_inc(s_proj, 1)
                for bank, weight in ((1, wq), (3, wv)):
                    for t in range(TPC):
                        last = pe.matmul(psum[:, bank, t * P:(t + 1) * P], hT1[:, t * P:(t + 1) * P], weight,
                                         start=True, stop=True)
                    last.then_inc(s_proj, 1)

            def turn_soft(done):
                for n, (src, bank, s_to) in enumerate(((k, 0, s_k_turn), (q, 2, s_q_turn))):
                    pe.wait_ge(s_soft, done * 2 + n + 1)
                    for t in range(TPC):
                        last = pe.transpose(psum[:, bank, t * P:(t + 1) * P], src[:, t * P:(t + 1) * P], ident)
                    last.then_inc(s_to, 1)

            def context(t, done):
                if t == 0:
                    pe.wait_ge(s_v, done + 1)
                    pe.wait_ge(s_k_tok, done + 1)
                if t >= 2:
                    pe.wait_ge(s_own, done * TPC + t - 1)
                pe.matmul(psum[:, 1 + 2 * (t % 2)], k_tok[:, t * P:(t + 1) * P], v_own[:, t].rearrange("p b c -> p (b c)"),
                          start=True, stop=True).then_inc(s_ctx, 1)

            def attend(t, done):
                pe.wait_ge(s_own, done * TPC + t + 1)
                if t == 0:
                    pe.wait_ge(s_qT, done + 1)
                for b in range(BPT):
                    sl = slice(t * P + b * S, t * P + (b + 1) * S)
                    last = pe.matmul(psum[:, 0, sl], ctx[:, t % 2, b], qT[:, sl], start=True, stop=True)
                last.then_inc(s_a, 1)

            def attn_out(done):
                pe.wait_ge(s_aT, done + 1)
                for t in range(TPC):
                    last = pe.matmul(psum[:, 2, t * P:(t + 1) * P], aT[:, t * P:(t + 1) * P], wo, start=True, stop=True)
                last.then_inc(s_wo, 1)

            def up(done):
                pe.wait_ge(s_hT2, done + 1)
                for f in range(NF):
                    pe.matmul(psum[:, 5 + f if f < 3 else 4], ffn_w[:, f * P:(f + 1) * P], hT2[:], start=True,
                              stop=True).then_inc(s_up, 1)

            def down(t, done):
                if t == 0:
                    pe.wait_ge(s_hidden, done * NF + NF)
                for f in range(NF):
                    last = pe.matmul(psum[:, 5, t * P:(t + 1) * P], hidden[:, f, t * P:(t + 1) * P],
                                     ffn_w[:, (NF + f) * P:(NF + f + 1) * P], start=(f == 0), stop=(f == NF - 1))
                if t == TPC - 1:
                    last.then_inc(s_down, 1)

            def A(n, done):
                turn(Y1, 0, s_norm1, s_turn1, done)
                project(done)
                turn_soft(done)
                context(0, done)
                context(1, done)
                for t in range(TPC):
                    attend(t, done)
                    if t + 2 < TPC:
                        context(t + 2, done)
                attn_out(done)

            def F(n, done):
                turn(Y2, 4, s_norm2, s_turn2, done)
                up(done)
                for t in range(TPC):
                    down(t, done)

            def both(a, f):
                a, f = a[1], f[1]
                turn(Y1, 0, s_norm1, s_turn1, a)
                project(a)
                turn(Y2, 4, s_norm2, s_turn2, f)
                up(f)
                turn_soft(a)
                context(0, a)
                context(1, a)
                for t in range(TPC):
                    down(t, f)
                    attend(t, a)
                    if t + 2 < TPC:
                        context(t + 2, a)
                attn_out(a)

            def weights_in(d):
                pe.wait_ge(s_attn_w, d * 16 + 16)
                pe.wait_ge(s_ffn_w, d * 16 + 16)

            layers(pe, A, F, both, layer_starts=weights_in)

        @block.scalar
        def _(act):
            def features(bank, out, ln, s_from, s_to, done):
                act.wait_ge(s_from, done + 1)
                act.activation(out, psum[:, bank], ACT.Identity, bias=ln[:, 1:2], scale=ln[:, 0:1]).then_inc(s_to, 1)

            def exponential(n, done):
                act.wait_ge(s_less, done * 2 + n + 1)
                x = (k, q)[n][:]
                act.activation(x, x, ACT.Exp).then_inc(s_exp, 1)

            def slope(f, done):
                act.wait_ge(s_up, done * NF + f + 1)
                act.activation(hidden[:, f], psum[:, 5 + f if f < 3 else 4], ACT.Copy, scale=0.01).then_inc(s_slope, 1)

            def turned(bank, out, s_from, s_to, done):
                act.wait_ge(s_from, done + 1)
                act.activation(out, psum[:, bank], ACT.Copy).then_inc(s_to, 1)

            def rest(done):
                turned(0, k_tok[:], s_k_turn, s_k_tok, done)
                turned(2, qT[:], s_q_turn, s_qT, done)
                act.wait_ge(s_a, done * TPC + TPC)
                act.activation(aT[:], psum[:, 0], ACT.Copy).then_inc(s_aT, 1)

            def A(n, done):
                features(0, hT1[:], ln1, s_turn1, s_hT1, done)
                exponential(0, done)
                exponential(1, done)
                rest(done)

            def F(n, done):
                features(4, hT2[:], ln2, s_turn2, s_hT2, done)
                for f in range(NF):
                    slope(f, done)

            def both(a, f):
                a, f = a[1], f[1]
                features(0, hT1[:], ln1, s_turn1, s_hT1, a)
                features(4, hT2[:], ln2, s_turn2, s_hT2, f)
                exponential(0, a)
                slope(0, f)
                exponential(1, a)
                for m in range(1, NF):
                    slope(m, f)
                rest(a)

            def weights_in(d):
                act.wait_ge(s_attn_w, d * 16 + 16)
                act.wait_ge(s_ffn_w, d * 16 + 16)

            layers(act, A, F, both, layer_starts=weights_in)

        @block.vector
        def _(dve):
            with dve.Fori(0, CHUNKS // 2) as i:
                x_of = lambda u: (lambda t: X[:, bass.ds(i * 8 + u * 4 + t, 1)])
                for u in range(2):
                    norm0.dve_stats(dve, x_of(u), i * 2 + u, u)
                for u in range(2):
                    norm0.dve_apply(dve, lambda t: stream[:, bass.ds(i * 8 + u * 4 + t, 1)], x_of(u), i * 2 + u, u, s_norm0)
            dve.wait_ge(s_norm0, CHUNKS)
            dve.wait_ge(s_zero, 1)
            dve.engine_nop()

            def part(n, t, count=1):
                at = n * TPC + t
                return stream[:, at:at + count] if isinstance(at, int) else stream[:, bass.ds(at, count)]

            def soften(m, done):
                bank, x, stat, width = ((2, k, k_stat, S), (1, q, q_stat, DH))[m]
                groups = x[:].rearrange("p (g w) -> p g w", w=width)
                source = psum[:, bank].rearrange("p (g w) -> p g w", w=width)
                dve.wait_ge(s_proj, done * 3 + m + 1)
                dve.tensor_reduce(stat[:, 0], source, AX.X, ALU.max).then_inc(s_soft_link, 1)
                dve.wait_ge(s_soft_link, done * 6 + m + 1)
                dve.tensor_tensor(groups, source, spread(stat[:, 0], width, 2), ALU.subtract).then_inc(s_less, 1)

            def normalise(m, done):
                x, stat, width = ((k, k_stat, S), (q, q_stat, DH))[m]
                groups = x[:].rearrange("p (g w) -> p g w", w=width)
                dve.wait_ge(s_exp, done * 2 + m + 1)
                dve.tensor_reduce(stat[:, 1], groups, AX.X, ALU.add).then_inc(s_soft_link, 1)
                dve.wait_ge(s_soft_link, done * 6 + 2 * m + 3)
                dve.reciprocal(stat[:, 2], stat[:, 1]).then_inc(s_soft_link, 1)
                dve.wait_ge(s_soft_link, done * 6 + 2 * m + 4)
                dve.tensor_tensor(groups, groups, spread(stat[:, 2], width, 2), ALU.mult).then_inc(s_soft, 1)

            def leaky(f, done):
                dve.wait_ge(s_slope, done * NF + f + 1)
                dve.tensor_tensor(hidden[:, f], psum[:, 5 + f if f < 3 else 4], hidden[:, f], ALU.max).then_inc(s_hidden, 1)

            def attention(done, ffn=None):
                soften(0, done)
                soften(1, done)
                dve.wait_ge(s_proj, done * 3 + 3)
                for b in range(BPT):
                    rows = slice(b * S, (b + 1) * S)
                    last = dve.tensor_copy(v_own[rows, :, b], tiles(psum[:, 3])[rows])
                last.then_inc(s_v, 1)
                if ffn is not None:
                    leaky(0, ffn)
                normalise(0, done)
                if ffn is not None:
                    leaky(1, ffn)
                normalise(1, done)
                if ffn is not None:
                    leaky(2, ffn)
                    leaky(3, ffn)
                for t in range(TPC):
                    dve.wait_ge(s_ctx, done * TPC + t + 1)
                    dve.tensor_tensor(ctx[:, t % 2], psum[:, 1 + 2 * (t % 2)].rearrange("p (b c) -> p b c", b=BPT),
                                      spread(core.const("same16"), BPT, 1), ALU.mult).then_inc(s_own, 1)

            def attention_added(n, done):
                dve.wait_ge(s_wo, done + 1)
                dve.wait_ge(s_bo, done + 1)
                dve.tensor_tensor(part(n, 0, TPC), tiles(psum[:, 2]), part(n, 0, TPC), ALU.add).then_inc(s_mid, 1)
                gate(dve, s_mid, done + 1, passed_dve)

            def ffn_added(n, done):
                dve.wait_ge(s_down, done + 1)
                dve.tensor_tensor(part(n, 0, TPC), tiles(psum[:, 5]), part(n, 0, TPC), ALU.add).then_inc(s_layer, 1)

            def stats(norm, n, done):
                norm.dve_stats(dve, lambda t: part(n, t), done, 0)

            def apply(norm, Y, s_norm, n, done):
                norm.dve_apply(dve, lambda t: Y[:, t:t + 1], lambda t: part(n, t), done, 0, s_norm)

            def A(n, done):
                stats(norm1, n, done)
                apply(norm1, Y1, s_norm1, n, done)
                attention(done)

            def F(n, done):
                attention_added(n, done)
                stats(norm2, n, done)
                apply(norm2, Y2, s_norm2, n, done)
                for f in range(NF):
                    leaky(f, done)
                ffn_added(n, done)

            def both(a, f):
                stats(norm1, *a)
                attention_added(*f)
                stats(norm2, *f)
                apply(norm1, Y1, s_norm1, *a)
                apply(norm2, Y2, s_norm2, *f)
                attention(a[1], f[1])
                ffn_added(*f)

            layers(dve, A, F, both, layer_ends=lambda d: gate(dve, s_layer, d * CHUNKS + CHUNKS, passed_dve))
            dve.tensor_tensor(X[:], X[:], stream[:], ALU.add)
        sc.close_block()


def program(nc, x, out, const, packs, context, context32, mask):
    tiles_of = lambda a: a.rearrange("(t b) s d -> (b s) t d", b=BPT)
    with ExitStack() as ctx:
        X = ctx.enter_context(nc.sbuf_tensor("X", [P, TILES, P], F32))
        inner = ctx.enter_context(nc.sbuf_tensor("inner", [P, TILES, P], F32))
        const_sb = ctx.enter_context(nc.sbuf_tensor("const_sb", [P, CONST_WIDTH], F32))
        s_loaded = ctx.enter_context(nc.semaphore("loaded"))
        s_stored = ctx.enter_context(nc.semaphore("stored"))
        core = Core(nc, packs, X, const_sb)
        with nc.Block() as block:
            @block.sync
            def _(sp):
                sp.dma_start(const_sb[:], const).then_inc(s_loaded, 16)
                sp.dma_start(X[:], tiles_of(x)).then_inc(s_loaded, 16)
                sp.wait_ge(s_loaded, 32)
        r8 = 8 ** -0.5
        hT_all = core.hT_all = ctx.enter_context(nc.sbuf_tensor("hT_all", [P, TOK], F32))
        logits = ctx.enter_context(nc.sbuf_tensor("logits", [P, TILES, 8], F32))
        comb = ctx.enter_context(nc.sbuf_tensor("comb", [P, TILES, 8], F32))

        def moe(name, router, kind, gate_kind, E, nf, capacity=None, **more):
            front(core, name + "_front", router, hT_all, logits=logits, **more.pop("front", {}))
            gates(core, name + "_gates", logits, comb, gate_kind, capacity)
            experts(core, name, name, hT_all, comb, E, nf, kind, **more)

        generated = ctx.enter_context(nc.sbuf_tensor("generated", [P, GEN_WIDTH + 4], F32))

        def generated_as(names):
            def at(name):
                start, width = names[name]
                return generated[:, start:start + width]
            return at

        def cross(name, scale, mask=None):
            front(core, name + "_front", lambda n: None, hT_all)
            cross_attention(core, name, name, hT_all, context, scale, mask)

        def quantised():
            front(core, "q_front", lambda n: None, hT_all)
            quantised_ffn(core, "q_ffn", "q_ffn", hT_all)

        def third_self():
            at = {n: a for n, (a, _) in GENERATED.items()}
            generate(core, "t_gen", "t_gen", generated)
            small_attention(core, "t_self", generated_as(dict(
                wq=(at["ca"], P), wk=(at["ca"] + P, P), wv=(at["ca"] + 2 * P, P), wo=(at["cp"], P), bq=(at["ca_b"], 1),
                bk=(at["ca_b"] + 1, 1), bv=(at["ca_b"] + 2, 1), bo=(at["cp_b"], P),
                ln_w=(GEN_WIDTH, 1), ln_b=(GEN_WIDTH + 1, 1))), 16, r8, mask="fill", second=("eps5", False), keep=inner)
            source = generated_as(dict(up=(at["cf"], 512), down=(at["cm"], 512), b1=(at["cf_b"], 4), bo=(at["cm_b"], P),
                                       ln_w=(GEN_WIDTH + 2, 1), ln_b=(GEN_WIDTH + 3, 1)))
            front(core, "t_front", source, hT_all, second=("eps5", False), keep=(inner, "source"))
            experts(core, "t_mlp", source, hT_all, None, 1, 4, "gelu_tanh", base=inner, out_bias=True)

        def fourth():
            small_attention(core, "u_self", "u_self", 16, r8, mask="causal", second=("eps6", True), keep=inner,
                            rotate=("rcos", "rsin", "rcos", "rsin"), qk_norm=True, post="gate")
            moe("u_moe", "u_router", "glu", "top1", 8, 2, base=inner, b2=True,
                front=dict(second=("eps6", True), keep=(inner, "source")))

        steps = {
            1: lambda: cross("a_cross", r8),
            7: lambda: cross("e_cross", r8),
            9: quantised,
            10: lambda: cross("t_cross", r8, mask),
            11: third_self,
            12: fourth,
            2: lambda: linear_transformer(core, "l", inner),
            3: lambda: moe("a_moe", "a_router", "silu", "probs", 8, 3, shared=True, front=dict(second=("eps5", False))),
            6: lambda: moe("c_moe", "c_router", "gelu", "capacity", 8, 4, capacity=1280),
            4: lambda: small_attention(core, "c_cross", "c_cross", 16, r8, context=context32, mask="causal"),
            5: lambda: small_attention(core, "c_self", "c_self", 16, r8),
            8: lambda: small_attention(core, "retention", "retention", 8, 1.0, mask="decay", softmax=False,
                                       rotate=("xcos_q", "xsin_q", "xcos_k", "xsin_k"), post="group_norm"),
        }
        for n in SUBLAYERS:
            steps[n]()
        with nc.Block() as block:
            @block.sync
            def _(sp):
                sp.dma_start(tiles_of(out), X[:]).then_inc(s_stored, 16)
                sp.wait_ge(s_stored, 16)



def column(v):
    return np.ascontiguousarray(v.reshape(-1, P).T)


def row(v):
    return np.broadcast_to(v[None], (P, v.shape[-1]))


def block_diagonal(w):
    h, d, _ = w.shape
    out = np.zeros((h * d, h * d), w.dtype)
    for n in range(h):
        out[n * d:(n + 1) * d, n * d:(n + 1) * d] = w[n]
    return out


ZERO_COLUMN, ZERO_ROW = np.zeros((P, 1), np.float32), np.zeros((P, P), np.float32)


def pack_inputs(v):
    neighbours = np.arange(P) ^ 1
    qkv, b_qkv = v["L1_attn_w_qkv"].T, column(v["L1_attn_b_qkv"])
    packs = {
        "c_cross": dict(wq=v["L1_xattn_q_w"], wk=v["L1_xattn_k_w"], wv=v["L1_xattn_v_w"], wo=v["L1_xattn_o_w"],
                        bq=column(v["L1_xattn_q_b"]), bk=column(v["L1_xattn_k_b"]), bv=column(v["L1_xattn_v_b"]),
                        bo=row(v["L1_xattn_o_b"])),
        "c_self": dict(wq=qkv[:, 0:P], wk=qkv[:, P:2 * P], wv=qkv[:, 2 * P:], wo=v["L1_attn_w_out"].T,
                       bq=b_qkv[:, 0:1], bk=b_qkv[:, 1:2], bv=b_qkv[:, 2:3], bo=row(v["L1_attn_b_out"])),
        "retention": dict(wq=block_diagonal(v["L2_attn_W_Q"]), wk=block_diagonal(v["L2_attn_W_K"]),
                          wv=block_diagonal(v["L2_attn_W_V"]), wg=v["L2_attn_W_G"], wo=v["L2_attn_W_O"],
                          wq_swap=block_diagonal(v["L2_attn_W_Q"])[:, neighbours],
                          wk_swap=block_diagonal(v["L2_attn_W_K"])[:, neighbours],
                          gn_w=column(v["L2_attn_gn_weight"]), gn_b=column(v["L2_attn_gn_bias"]),
                          bq=ZERO_COLUMN, bk=ZERO_COLUMN, bq_swap=ZERO_COLUMN, bk_swap=ZERO_COLUMN,
                          bv=ZERO_COLUMN, bo=ZERO_ROW),
    }
    packs["a_cross"] = dict(wq=v["L0_xattn_Wq"].T, wk=v["L0_xattn_Wkv"][0:P].T, wv=v["L0_xattn_Wkv"][P:].T,
                            wo=v["L0_xattn_Wout"].T, bq=ZERO_COLUMN, bk=ZERO_COLUMN, bv=ZERO_COLUMN,
                            bo=row(v["L0_xattn_bout"]))
    heads_side = lambda a: a.transpose(1, 0, 2).reshape(P, P)
    packs["e_cross"] = dict(wq=heads_side(v["L2_xattn_Wq"]), wk=heads_side(v["L2_xattn_Wk"]),
                            wv=heads_side(v["L2_xattn_Wv"]), wo=v["L2_xattn_Wo"].T, bq=ZERO_COLUMN, bk=ZERO_COLUMN,
                            bv=ZERO_COLUMN, bo=ZERO_ROW)
    packs["t_cross"] = dict(wq=v["L3_xattn_wq"].T, wk=v["L3_xattn_wk"].T, wv=v["L3_xattn_wv"].T, wo=v["L3_xattn_wo"].T,
                            bq=column(v["L3_xattn_bq"]), bk=column(v["L3_xattn_bk"]), bv=column(v["L3_xattn_bv"]),
                            bo=row(v["L3_xattn_bo"]))
    get = lambda kind, d: v["L0_attn_" + kind][d]
    packs["l_attn"] = {str(d): np.concatenate([get(kind, d) for kind in ("wq", "wk", "wv", "wo")] + [
        row(get("bo", d)), column(get("ln1_w", d)), column(get("ln1_b", d))], axis=1) for d in range(DEPTH)}
    packs["l_ffn"] = {str(d): np.concatenate([get("w1", d)] + [get("w2", d)[n * P:(n + 1) * P] for n in range(4)] + [
        column(get("ln2_w", d)), column(get("ln2_b", d))], axis=1) for d in range(DEPTH)}
    w1 = v["L2_ffn_w1"].reshape(4, P, P).transpose(1, 0, 2).reshape(P, 4 * P)
    packs["q_ffn"] = dict(w1=w1, w2=v["L2_ffn_w2"], b=np.concatenate([column(v["L2_ffn_b1"]), column(v["L2_ffn_b2"])], axis=1))
    gen = {}
    halves = lambda a: np.concatenate([a[:, n * P:(n + 1) * P].T for n in range(a.shape[1] // P)], axis=1)
    for part in ("sub0", "sub1", "W", "B"):
        get = lambda name, kind: (v[f"L3_attn_{name}_{part}_{kind}"] if part in "WB" else
                                  v[f"L3_attn_{name}_sub_{kind}"][int(part[3])])
        gen[part] = np.concatenate([get("ca", "w").T, get("cp", "w").T, get("cf", "w").T, halves(get("cm", "w")),
                                    column(get("ca", "b")), row(get("cp", "b")), column(get("cf", "b")),
                                    row(get("cm", "b"))], axis=1)
    gen["wl"] = np.concatenate([row(v[f"L3_attn_{n}_Wl_{k}"][0]) for k in "wb" for n in ("ca", "cp", "cf", "cm")], axis=1)
    gen["norms"] = np.stack([v["L3_attn_" + n] for n in ("ln1_g", "ln1_b", "ln2_g", "ln2_b")], axis=1)
    packs["t_gen"] = gen
    across, kv = np.arange(P) ^ 4, (np.arange(P) // 32) * 8 + np.arange(P) % 8
    f = lambda name: v["L3_ffn_" + name]
    packs["u_self"] = dict(wq=f("Wq"), wk=f("Wk")[:, kv], wv=f("Wv")[:, kv], wo=f("Wo"), wq_swap=f("Wq")[:, across],
                           wk_swap=f("Wk")[:, kv][:, across], bq=column(f("bq")), bk=column(f("bk")[kv]),
                           bv=column(f("bv")[kv]), bq_swap=column(f("bq")[across]), bk_swap=column(f("bk")[kv][across]),
                           bo=row(f("bo")), qn=column(np.tile(f("qn_w"), 16)), kn=column(np.tile(f("kn_w"), 16)),
                           wg=block_diagonal(np.broadcast_to(f("Wg"), (16, 8, 8))), bg=column(np.tile(f("bg"), 16)),
                           ln_w=column(f("ln1_w")), ln_b=ZERO_COLUMN)
    packs["u_router"] = dict(ln_w=column(f("ln2_w")), ln_b=ZERO_COLUMN, router=f("Wr"), router_b=row(f("br")))
    order = [(e, n, h) for e in range(8) for n in range(2) for h in range(2)]
    b2 = np.zeros((P, P), np.float32)
    b2[0:8] = f("b2")
    packs["u_moe"] = dict(up=np.concatenate([f("W1")[e][:, h * 256 + n * P:h * 256 + (n + 1) * P] for e, n, h in order], axis=1),
                          b1=np.stack([f("b1")[e, h * 256 + n * P:h * 256 + (n + 1) * P] for e, n, h in order], axis=1),
                          down=np.concatenate([f("W2")[e, n * P:(n + 1) * P] for e in range(8) for n in range(2)], axis=1), b2=b2)
    gu, sgu = v["L0_ffn_gate_up_w"], v["L0_ffn_shared_gate_up_w"]
    blocks = [gu[e, half * 384 + f * P:half * 384 + (f + 1) * P].T for e in range(8) for f in range(3) for half in range(2)]
    packs["a_router"] = dict(ln_w=column(v["L0_ffn_ln_gamma"]), ln_b=column(v["L0_ffn_ln_beta"]),
                             router=v["L0_ffn_router_w"].T, router_b=ZERO_ROW[:, 0:8])
    packs["a_moe"] = dict(up=np.concatenate(blocks + [sgu[0:P].T, sgu[P:].T], axis=1),
                          down=np.concatenate([v["L0_ffn_down_w"][e][:, f * P:(f + 1) * P].T for e in range(8) for f in range(3)]
                                              + [v["L0_ffn_shared_down_w"].T], axis=1))
    packs["c_router"] = dict(router=v["L1_ffn_w_g"], router_b=ZERO_ROW[:, 0:8])
    packs["c_moe"] = dict(up=np.concatenate(list(v["L1_ffn_c_fc"]), axis=1),
                          down=np.concatenate([v["L1_ffn_c_proj"][e, f * P:(f + 1) * P] for e in range(8) for f in range(4)], axis=1))
    return packs


def kernel(**inputs):
    import concourse.bacc as bacc
    from concourse.bass_utils import run_bass_kernel_spmd

    v = {name: np.asarray(a) for name, a in inputs.items()}
    nc = bacc.Bacc("TRN2", target_bir_lowering=False, num_devices=1)
    arrays = {}

    def dram(name, array):
        arrays[name] = np.ascontiguousarray(array)
        return nc.dram_tensor(name, arrays[name].shape, mybir.dt.from_np(arrays[name].dtype), kind="ExternalInput").ap()

    packs = {}
    for name, parts in pack_inputs(v).items():
        at, places = 0, {}
        for part, array in parts.items():
            places[part] = (at, array.shape[1])
            at += array.shape[1]
        packs[name] = (dram("pack_" + name, np.concatenate(list(parts.values()), axis=1)), places)
    x = dram("x", v["x"])
    const = dram("const", np.concatenate(list(CONSTANTS.values()), axis=1))
    context = v["ctx_1024"].transpose(2, 0, 1)
    context32 = dram("context32", context[:, :, 0:S].reshape(P, TOK))
    out = nc.dram_tensor("out", v["x"].shape, F32, kind="ExternalOutput").ap()
    program(nc, x, out, const, packs, dram("context", context), context32,
            dram("mask", v["mask_1x1xSxS2_ik0"][0, 0]))
    return run_bass_kernel_spmd(nc, [arrays], core_ids=[0]).results[0]["out"]
```

```python
from contextlib import ExitStack

import numpy as np

import concourse.bass as bass
from concourse import mybir

ALU = mybir.AluOpType
ACT = mybir.ActivationFunctionType
AX = mybir.AxisListType
F32 = mybir.dt.float32
BF16 = mybir.dt.bfloat16

P = 128
S = 32
B = 128
TOK = B * S
TILES = TOK // P
BPT = P // S
TPC = 4
CHUNK = TPC * P
CHUNKS = TILES // TPC
SK = 257
SUBLAYERS = range(1, 13)


def constants():
    c = {}
    ch = np.arange(P)
    c["ident"] = np.eye(P)
    c["heads16"] = (ch[:, None] // 8 == np.arange(16)[None]).astype(float)
    c["heads8"] = (ch[:, None] // 16 == np.arange(8)[None]).astype(float)
    row = np.arange(P)
    c["own8"] = (row[:, None] // S == np.arange(32)[None] // 8).astype(float)
    c["own16"] = (row[:, None] // S == np.arange(64)[None] // 16).astype(float)
    c["fold"] = (row[:, None] % S == np.arange(S)[None]).astype(float)
    c["causal"] = (np.arange(S)[None] <= row[:, None] % S).astype(float)
    c["causal_neg"] = (c["causal"] - 1.0) * 1e30
    c["causal_fill"] = (c["causal"] - 1.0) * 1e4 * 8 ** 0.5
    c["same8"] = (ch[:, None] // 8 == ch[None] // 8).astype(float)
    c["same16"] = (ch[:, None] // 16 == ch[None] // 16).astype(float)
    pos = np.arange(S, dtype=np.float32)
    d = 16
    scale = (np.arange(0, d, 2, dtype=np.float32) + np.float32(0.4 * d)) / np.float32(1.4 * d)
    sc = scale[None] ** (pos / np.float32(512.0))[:, None]
    inv = (1.0 / np.float32(10000.0) ** (np.arange(d // 2, dtype=np.float32) / np.float32(d // 2)))
    ang = pos[:, None] * inv[None].astype(np.float32)
    pair = (ch % 16) // 2
    sign = np.where(ch % 2 == 0, -1.0, 1.0)[:, None]
    c["xcos_q"] = (np.cos(ang) * sc).T[pair]
    c["xsin_q"] = (np.sin(ang) * sc).T[pair] * sign
    c["xcos_k"] = (np.cos(ang) / sc).T[pair]
    c["xsin_k"] = (np.sin(ang) / sc).T[pair] * sign
    inv = (1.0 / np.float32(10000.0) ** (np.arange(0, 8, 2, dtype=np.float32) / np.float32(8)))
    ang = pos[:, None] * inv[None].astype(np.float32)
    sign = np.where(ch % 8 < 4, -1.0, 1.0)[:, None]
    c["rcos"] = np.cos(ang).T[ch % 4]
    c["rsin"] = np.sin(ang).T[ch % 4] * sign
    gam = 1.0 - np.exp(np.linspace(np.log(1.0 / 32.0), np.log(1.0 / 512.0), 8))
    gam = gam.astype(np.float32).astype(float)
    diff = (row[:, None] % S) - np.arange(S)[None]
    for g in range(2):
        ga = gam[4 * g + row // S][:, None]
        c[f"decay{g}"] = np.where(diff >= 0, ga ** np.maximum(diff, 0), 0.0)
    c["ones"] = np.ones((P, P))
    c["mhalf"] = np.full((P, TPC), -0.5)
    c["eps5"] = np.full((P, TPC), 1e-5)
    c["eps6"] = np.full((P, TPC), 1e-6)
    c["group_of"] = np.zeros((P, P))
    c["group_of"][0:4] = np.arange(4)[:, None] == np.arange(P)[None] // 32
    c["group_of_late"] = np.roll(c["group_of"], 4, axis=0)
    c["head_in_group"] = (ch[:, None] // 8 % 4 == np.arange(4)[None]).astype(float)
    c["magic"] = np.full((P, 1), -12582912.0)
    c["experts"] = np.tile(8.0 - np.arange(8.0), (P, 1))
    c["upto"] = (np.arange(P)[:, None] <= np.arange(P)[None]).astype(float)
    return {k: np.asarray(v, np.float32) for k, v in c.items()}


CONSTANTS = constants()
CONST_AT = {}
_at = 0
for _name, _value in CONSTANTS.items():
    CONST_AT[_name] = (_at, _value.shape[1])
    _at += _value.shape[1]
CONST_WIDTH = _at


class Core:

    def __init__(self, nc, packs, x_sb, const_sb):
        self.nc, self.packs, self.X, self.const_sb = nc, packs, x_sb, const_sb

    def const2(self, first, second):
        (at, width), (at2, width2) = CONST_AT[first], CONST_AT[second]
        assert at2 == at + width
        return self.const_sb[:, at:at2 + width2]

    def const(self, name):
        at, width = CONST_AT[name]
        return self.const_sb[:, at:at + width]


class Link:

    def __init__(self, eng, sem, done):
        self.eng, self.sem, self.done, self.count = eng, sem, done, 0

    def __call__(self, instruction):
        self.count += 1
        instruction.then_inc(self.sem, 1)
        self.eng.wait_ge(self.sem, self.done + self.count)


class Scope(ExitStack):

    def __init__(self, core, name):
        super().__init__()
        self.core, self.nc, self.name, self.sems = core, core.nc, name, []

    def sb(self, name, shape, dt=F32):
        return self.enter_context(self.nc.sbuf_tensor(f"{self.name}_{name}", shape, dt))

    def banks(self):
        return self.enter_context(self.nc.psum_tensor(f"{self.name}_psum", [P, 8, 512], F32))

    def sem(self, name):
        sem = self.enter_context(self.nc.semaphore(f"{self.name}_{name}"))
        self.sems.append(sem)
        return sem

    def weights(self, source):
        if isinstance(source, tuple):
            return source[0], source[1], lambda eng: None
        if not isinstance(source, str):
            return source, lambda eng: None, lambda eng: None
        s_w = self.sem("weights")
        dram, at = self.core.packs[source]
        tile = self.sb("weights", list(dram.shape))

        def fetch(eng):
            eng.dma_start(tile[:], dram).then_inc(s_w, 16)

        return (lambda name: tile[:, at[name][0]:at[name][0] + at[name][1]]), lambda eng: eng.wait_ge(s_w, 16), fetch

    def open_block(self):
        self.block_guard = self.nc.Block()
        return self.block_guard.__enter__()

    def close_block(self):
        self.block_guard.__exit__(None, None, None)
        self.clear()

    def clear(self):
        with self.nc.Block() as block:
            @block.gpsimd
            def _(pool):
                for sem in self.sems:
                    pool.sem_clear(sem)


def gate(eng, sem, value, passed):
    eng.wait_ge(sem, value)
    eng.sem_inc(passed, 1)


def spread(ap, reps, axis):
    shape = list(ap.shape)
    shape.insert(axis, reps)
    return ap.unsqueeze(axis).to_broadcast(shape)


class Norm:

    def __init__(self, sc, name, eps, rms=False):
        self.eps, self.rms = sc.core.const(eps), rms
        self.mhalf = sc.core.const("mhalf")
        self.stats = sc.sb(name + "_stats", [P, 2, TPC, 6])
        self.moments = sc.sb(name + "_moments", [P, 2, TPC, 2])
        self.square = sc.sb(name + "_square", [P, 2, TPC]) if rms else None
        self.rstd = sc.sb(name + "_rstd", [P, 2, 2, TPC])
        self.s_stats = sc.sem(name + "_stats")
        self.s_moments = sc.sem(name + "_moments")
        self.s_square = sc.sem(name + "_square")
        self.s_var = sc.sem(name + "_var")
        self.s_rstd = sc.sem(name + "_rstd")
        self.passed_dve = sc.sem(name + "_passed_dve")

    def dve_stats(self, dve, tile_of, c, u):
        for k in range(TPC):
            last = dve.bn_stats(self.stats[:, u, k], tile_of(k))
        last.then_inc(self.s_stats, 1)
        gate(dve, self.s_stats, c + 1, self.passed_dve)
        for k in range(TPC):
            last = dve.bn_aggr(self.moments[:, u, k], self.stats[:, u, k])
        last.then_inc(self.s_moments, 1)
        if self.rms:
            mean, var = self.moments[:, u, :, 0], self.moments[:, u, :, 1]
            dve.wait_ge(self.s_moments, c + 1)
            dve.tensor_tensor(self.square[:, u], mean, mean, ALU.mult).then_inc(self.s_square, 1)
            dve.wait_ge(self.s_square, 2 * c + 1)
            dve.tensor_tensor(self.square[:, u], self.square[:, u], var, ALU.add).then_inc(self.s_square, 1)

    def pool_rstd(self, pool, c, u):
        pool.wait_ge(*((self.s_square, 2 * c + 2) if self.rms else (self.s_moments, c + 1)))
        var = self.square[:, u] if self.rms else self.moments[:, u, :, 1]
        pool.tensor_tensor(self.rstd[:, u, 0], var, self.eps, ALU.add).then_inc(self.s_var, 1)
        pool.wait_ge(self.s_var, c + 1)
        pool.tensor_tensor(self.rstd[:, u, 1], self.rstd[:, u, 0], self.mhalf, ALU.pow).then_inc(self.s_rstd, 1)

    def dve_apply(self, dve, out_of, tile_of, c, u, s_out):
        dve.wait_ge(self.s_rstd, c + 1)
        for k in range(TPC):
            if self.rms:
                last = dve.tensor_scalar(out_of(k), tile_of(k), self.rstd[:, u, 1, k:k + 1], None, ALU.mult)
            else:
                last = dve.tensor_scalar(out_of(k), tile_of(k), self.moments[:, u, k, 0:1],
                                         self.rstd[:, u, 1, k:k + 1], ALU.subtract, ALU.mult)
        last.then_inc(s_out, 1)



def small_attention(core, name, weights, heads, scale, context=None, mask=None, second=None,
                    keep=None, rotate=None, qk_norm=False, post=None, softmax=True):
    nc, X = core.nc, core.X
    dh = P // heads
    G = heads // 4
    GW = 4 * dh
    GB = G * BPT
    own, head_of, ident = core.const(f"own{dh}"), core.const(f"heads{heads}"), core.const("ident")
    dest = keep if keep is not None else X
    PAIRS = CHUNKS // 2
    with Scope(core, name) as sc:
        psum = sc.banks()
        w, arrived, fetch = sc.weights(weights)
        norm = Norm(sc, "ln", "eps5")
        norm2 = Norm(sc, "ln2", second[0], rms=second[1]) if second else None
        Y = sc.sb("normed", [P, 2, TPC, P])
        Y2 = sc.sb("normed2", [P, 2, TPC, P]) if second else Y
        hT = sc.sb("hT", [P, 2, CHUNK])
        cT = sc.sb("cT", [P, 2, CHUNK]) if context is not None else hT
        qT = sc.sb("qT", [P, 2, CHUNK])
        kT = sc.sb("kT", [P, 2, CHUNK])
        q_heads = sc.sb("q_heads", [P, 4, BPT, heads, S])
        v_own = core.hT_all[:].rearrange("p (t b c) -> p t b c", b=BPT, c=P)
        by_key = sc.sb("by_key", [P, 2, G * P])
        E = sc.sb("E", [P, 4, GB, S])
        ET = sc.sb("ET", [P, 4, G, P])
        top = sc.sb("top", [P, 4, GB])
        total = sc.sb("total", [P, 8, 2, GB])
        O = sc.sb("O", [P, 4, GB, GW])
        O_own = sc.sb("O_own", [P, 4, BPT, P])
        aT = sc.sb("aT", [P, 2, 4, CHUNK])
        rot = sc.sb("rot", [P, 2, 4, CHUNK]) if rotate else None
        scratch = sc.sb("scratch", [P, 2, 2, CHUNK]) if qk_norm or post else None
        s_zero, s_ctx = sc.sem("zero"), [sc.sem("ctx0"), sc.sem("ctx1")]
        s_norm, s_norm2, s_turn, s_hT = sc.sem("norm"), sc.sem("norm2"), sc.sem("turn"), sc.sem("hT")
        s_proj, s_q, s_k, s_v = sc.sem("proj"), sc.sem("q"), sc.sem("k"), sc.sem("v")
        s_heads, s_score, s_mask = sc.sem("heads"), sc.sem("score"), sc.sem("mask")
        s_by_key, s_by_key_out = sc.sem("by_key"), sc.sem("by_key_out")
        s_top, s_sub, s_exp, s_sum = sc.sem("top"), sc.sem("sub"), sc.sem("exp"), sc.sem("sum")
        s_recip, s_eT, s_ET, s_pv = sc.sem("recip"), sc.sem("eT"), sc.sem("ET"), sc.sem("pv")
        s_scaled, s_own, s_fold, s_aT = sc.sem("scaled"), sc.sem("own"), sc.sem("fold"), sc.sem("aT")
        s_out, s_done, s_post = sc.sem("out"), sc.sem("done"), sc.sem("post")
        passed_dve, passed_pool = sc.sem("passed_dve"), sc.sem("passed_pool")
        s_link, s_kept = sc.sem("link"), sc.sem("kept")
        if rotate:
            s_rot, s_swap_k, s_bias_rot = sc.sem("rot"), sc.sem("swap_k"), sc.sem("bias_rot")
            s_rot_link = sc.sem("rot_link")
        if qk_norm:
            s_square, s_ms, s_ms_sb = sc.sem("square"), sc.sem("ms"), sc.sem("ms_sb")
            s_power, s_unit = sc.sem("power"), sc.sem("unit")
        if post:
            s_gate, s_sig = sc.sem("gate"), sc.sem("sig")
        if post == "group_norm":
            s_mean, s_centred, s_dev = sc.sem("mean"), sc.sem("centred"), sc.sem("dev")
            s_var, s_var_sb = sc.sem("var"), sc.sem("var_sb")
        bias_rot = sc.sb("bias_rot", [P, 2 * S]) if rotate else None
        s_q_final = s_unit if qk_norm else s_q
        q_count = 2 if qk_norm else 1
        post_steps = {"group_norm": 4, "gate": 0, None: 0}[post]
        bank_of = lambda at: psum[:, at, 0:G * P]

        def rotated(eng, link, i, a, dst, s_dst):
            for u in range(2):
                eng.wait_ge(s_rot, (i * 2 + u) * 4 + 2 * a + 2)
                r = rot[:, u, 2 * a].rearrange("p (b s) -> p b s", s=S)
                link(eng.tensor_tensor(r, r, spread(bias_rot[:, a * S:(a + 1) * S], CHUNK // S, 1), ALU.add))
                eng.tensor_tensor(dst[:, u], rot[:, u, 2 * a], rot[:, u, 2 * a + 1], ALU.add).then_inc(s_dst, 1)

        block = sc.open_block()

        @block.sync
        def _(sp):
            fetch(sp)
            if context is not None:
                for u in range(2):
                    sp.dma_start(cT[:, u], context[:, u * CHUNK:(u + 1) * CHUNK]).then_inc(s_ctx[u], 16)
                with sp.Fori(1, PAIRS) as i:
                    for u in range(2):
                        sp.wait_ge(s_proj, i * 2 - 1 + u)
                        sp.dma_start(cT[:, u], context[:, bass.ds((i * 2 + u) * CHUNK, CHUNK)]).then_inc(s_ctx[u], 16)

        @block.gpsimd
        def _(pool):
            pool.memset(v_own, 0.0).then_inc(s_zero, 1)
            if rotate:
                arrived(pool)
                pool.wait_ge(s_bias_rot, 1)
            with pool.Fori(0, PAIRS) as i:
                for u in range(2):
                    norm.pool_rstd(pool, i * 2 + u, u)
                if second:
                    for u in range(2):
                        norm2.pool_rstd(pool, i * 2 + u, u)
                if rotate:
                    rotated(pool, Link(pool, s_rot_link, i * 2), i, 0, qT, s_q)
                for n in range(8):
                    u, t = divmod(n, TPC)
                    pool.wait_ge(s_q_final, (i * 2 + u) * q_count + 1)
                    if n >= 4:
                        pool.wait_ge(s_score, i * 8 + n - 3)
                    pool.tensor_tensor(q_heads[:, n % 4],
                                       spread(qT[:, u, t * P:(t + 1) * P].rearrange("p (b s) -> p b s", s=S), heads, 2),
                                       spread(spread(head_of, BPT, 1), S, 3), ALU.mult).then_inc(s_heads, 1)

        @block.tensor
        def _(pe):
            arrived(pe)
            with pe.Fori(0, PAIRS) as i:
                for u in range(2):
                    pe.wait_ge(s_norm2 if second else s_norm, i * 2 + u + 1)
                    for k in range(TPC):
                        last = pe.transpose(psum[:, 4 * u, k * P:(k + 1) * P], Y2[:, u, k], ident)
                    last.then_inc(s_turn, 1)
                for u in range(2):
                    pe.wait_ge(s_hT, i * 2 + u + 1)
                    if context is not None:
                        pe.wait_ge(s_ctx[u], i * 16 + 16)
                    pe.matmul(psum[:, 4 * u + 1], w("wq"), hT[:, u], start=True, stop=True)
                    pe.matmul(psum[:, 4 * u + 2], w("wk"), cT[:, u], start=True, stop=True)
                    if rotate:
                        pe.matmul(psum[:, 4 * u], w("wq_swap"), hT[:, u], start=True, stop=True)
                    for k in range(TPC):
                        last = pe.matmul(psum[:, 4 * u + 3, k * P:(k + 1) * P], cT[:, u, k * P:(k + 1) * P],
                                         w("wv"), start=True, stop=True)
                    last.then_inc(s_proj, 1)
                if rotate:
                    for u in range(2):
                        pe.wait_ge(s_rot, (i * 2 + u) * 4 + 1)
                        pe.matmul(psum[:, 4 * u + 1], w("wk_swap"), hT[:, u], start=True, stop=True).then_inc(s_swap_k, 1)
                if qk_norm:
                    for u in range(2):
                        for a in range(2):
                            pe.wait_ge(s_square, (i * 2 + u) * 2 + a + 1)
                            pe.matmul(psum[:, 4 * u + 2 * a], core.const("same8"), scratch[:, u, a],
                                      start=True, stop=True).then_inc(s_ms, 1)

                def projected(u):
                    pe.wait_ge(s_v, i * 2 + u + 1)
                    pe.wait_ge(s_k, i * 2 + u + 1)
                    pe.wait_ge(s_q_final, (i * 2 + u + 1) * q_count)

                def scores_by_key(n):
                    u, t = divmod(n, TPC)
                    if n == 0:
                        projected(0)
                    pe.wait_ge(s_heads, i * 8 + n + 1)
                    if n >= 1:
                        pe.wait_ge(s_by_key_out, i * 8 + n)
                    for b in range(BPT):
                        last = pe.matmul(psum[b * S:(b + 1) * S, 0, 0:G * P], kT[:, u, t * P + b * S:t * P + (b + 1) * S],
                                         q_heads[:, n % 4, b].rearrange("p h s -> p (h s)"), start=True, stop=True)
                    last.then_inc(s_by_key, 1)

                def scores(n):
                    pe.wait_ge(s_by_key_out, i * 8 + n + 1)
                    if n >= 1:
                        pe.wait_ge(s_mask if mask else s_sub, i * 8 + n)
                    for g in range(G):
                        last = pe.transpose(psum[:, 1, g * P:(g + 1) * P], by_key[:, n % 2, g * P:(g + 1) * P], ident)
                    last.then_inc(s_score, 1)

                def turn(n):
                    pe.wait_ge(s_exp if softmax else s_mask, i * 8 + n + 1)
                    if n >= 2:
                        pe.wait_ge(s_ET, i * 8 + n - 1)
                    for g in range(G):
                        last = pe.transpose(psum[:, 2 + n % 2, g * P:(g + 1) * P],
                                            E[:, n % 4, g * BPT:(g + 1) * BPT].rearrange("p b k -> p (b k)"), ident)
                    last.then_inc(s_eT, 1)

                def values(n):
                    pe.wait_ge(s_ET, i * 8 + n + 1)
                    if n == 0:
                        projected(1)
                    if n >= 2:
                        pe.wait_ge(s_scaled, i * 8 + n - 1)
                    bank = psum[:, 4 + n % 2].rearrange("p (g b c) -> p g b c", b=BPT, c=GW)
                    for g in range(G):
                        last = pe.matmul(bank[:, g], ET[:, n % 4, g], v_own[:, n, :, g * GW:(g + 1) * GW],
                                         start=True, stop=True)
                    last.then_inc(s_pv, 1)

                def fold(n):
                    u, t = divmod(n, TPC)
                    pe.wait_ge(s_own if softmax else s_scaled, i * 8 + n + 1)
                    for b in range(BPT):
                        last = pe.matmul(psum[:, 6 + u, t * P + b * S:t * P + (b + 1) * S],
                                         O_own[:, n % 4, b], core.const("fold"), start=True, stop=True)
                    last.then_inc(s_fold, 1)

                for step in range(8 + 7):
                    if 0 <= step - 1 < 8:
                        scores(step - 1)
                    if step < 8:
                        scores_by_key(step)
                    if 0 <= step - 3 < 8:
                        turn(step - 3)
                    if 0 <= step - 5 < 8:
                        values(step - 5)
                    if 0 <= step - 7 < 8:
                        fold(step - 7)
                if post == "group_norm":
                    for u in range(2):
                        pe.wait_ge(s_aT, i * 2 + u + 1)
                        pe.matmul(psum[:, 2 * u], core.const("same16"), aT[:, u, 0], start=True, stop=True).then_inc(s_mean, 1)
                        pe.matmul(psum[:, 2 * u + 1], w("wg"), hT[:, u], start=True, stop=True).then_inc(s_gate, 1)
                    for u in range(2):
                        pe.wait_ge(s_dev, i * 2 + u + 1)
                        pe.matmul(psum[:, 6 + u], core.const("same16"), scratch[:, u, 0],
                                  start=True, stop=True).then_inc(s_var, 1)
                if post == "gate":
                    for u in range(2):
                        pe.wait_ge(s_aT, i * 2 + u + 1)
                        pe.matmul(psum[:, 2 * u], w("wg"), aT[:, u, 0], start=True, stop=True).then_inc(s_gate, 1)
                for u in range(2):
                    pe.wait_ge(s_post if post else s_aT, i * 2 + u + 1)
                    for k in range(TPC):
                        last = pe.matmul(psum[:, 4 + u, k * P:(k + 1) * P], aT[:, u, 3 if post else 0, k * P:(k + 1) * P],
                                         w("wo"), start=True, stop=True)
                    last.then_inc(s_out, 1)

        @block.scalar
        def _(act):
            arrived(act)
            with act.Fori(0, PAIRS) as i:
                for u in range(2):
                    act.wait_ge(s_turn, i * 2 + u + 1)
                    act.activation(hT[:, u], psum[:, 4 * u], ACT.Identity, bias=w("ln_b") if second else 0.0,
                                   scale=w("ln_w") if second else 1.0).then_inc(s_hT, 1)
                if not rotate:
                    for u in range(2):
                        act.wait_ge(s_proj, i * 2 + u + 1)
                        act.activation(qT[:, u], psum[:, 4 * u + 1], ACT.Identity, bias=w("bq")).then_inc(s_q, 1)
                        act.activation(kT[:, u], psum[:, 4 * u + 2], ACT.Identity, bias=w("bk")).then_inc(s_k, 1)
                if qk_norm:
                    for u in range(2):
                        for a in range(2):
                            act.wait_ge(s_ms, (i * 2 + u) * 2 + a + 1)
                            act.activation(scratch[:, u, a], psum[:, 4 * u + 2 * a], ACT.Sqrt,
                                           scale=1.0 / dh, bias=core.const("eps6")[:, 0:1]).then_inc(s_ms_sb, 1)
                for step in range(8 + 3):
                    if step < 8:
                        act.wait_ge(s_by_key, i * 8 + step + 1)
                        act.activation(by_key[:, step % 2], bank_of(0), ACT.Copy).then_inc(s_by_key_out, 1)
                    if 0 <= step - 1 < 8 and softmax:
                        n = step - 1
                        act.wait_ge(s_sub, i * 8 + n + 1)
                        act.activation(E[:, n % 4], E[:, n % 4], ACT.Exp, scale=scale).then_inc(s_exp, 1)
                    if step >= 3:
                        n = step - 3
                        act.wait_ge(s_eT, i * 8 + n + 1)
                        act.activation(ET[:, n % 4].rearrange("p g c -> p (g c)"), bank_of(2 + n % 2), ACT.Copy).then_inc(s_ET, 1)
                for u in range(2):
                    act.wait_ge(s_fold, i * 8 + 4 * u + 4)
                    act.activation(aT[:, u, 0], psum[:, 6 + u], ACT.Identity, bias=w("bv")).then_inc(s_aT, 1)
                if post == "group_norm":
                    for u in range(2):
                        act.wait_ge(s_gate, i * 2 + u + 1)
                        act.activation(aT[:, u, 2], psum[:, 2 * u + 1], ACT.Sigmoid).then_inc(s_sig, 1)
                    for u in range(2):
                        act.wait_ge(s_var, i * 2 + u + 1)
                        act.activation(scratch[:, u, 1], psum[:, 6 + u], ACT.Sqrt, scale=1.0 / dh,
                                       bias=core.const("eps5")[:, 0:1]).then_inc(s_var_sb, 1)
                if post == "gate":
                    for u in range(2):
                        act.wait_ge(s_gate, i * 2 + u + 1)
                        act.activation(aT[:, u, 1], psum[:, 2 * u], ACT.Sigmoid, bias=w("bg")).then_inc(s_sig, 1)

        @block.vector
        def _(dve):
            dve.wait_ge(s_zero, 1)
            arrived(dve)
            if rotate:
                br = bias_rot
                for a in range(2):
                    dve.tensor_scalar(br[:, a * S:(a + 1) * S], core.const(rotate[2 * a]), w(("bq", "bk")[a]), None,
                                      ALU.mult).then_inc(s_kept, 1)
                    dve.wait_ge(s_kept, a + 1)
                    last = dve.scalar_tensor_tensor(out=br[:, a * S:(a + 1) * S], in0=core.const(rotate[2 * a + 1]),
                                                    scalar=w(("bq_swap", "bk_swap")[a]), in1=br[:, a * S:(a + 1) * S],
                                                    op0=ALU.mult, op1=ALU.add)
                last.then_inc(s_bias_rot, 1)
                dve.wait_ge(s_bias_rot, 1)
            with dve.Fori(0, PAIRS) as i:
                link = Link(dve, s_link, i * (2 * post_steps + 2 + (2 if rotate else 0)))
                x_of = [lambda k, u=u: X[:, bass.ds(i * 8 + 4 * u + k, 1)] for u in range(2)]
                y_of = [lambda k, u=u: Y[:, u, k] for u in range(2)]
                y2_of = [lambda k, u=u: Y2[:, u, k] for u in range(2)]
                for u in range(2):
                    norm.dve_stats(dve, x_of[u], i * 2 + u, u)
                for u in range(2):
                    norm.dve_apply(dve, y_of[u], x_of[u], i * 2 + u, u, s_norm)
                if second:
                    for u in range(2):
                        dve.wait_ge(s_norm, i * 2 + u + 1)
                        norm2.dve_stats(dve, y_of[u], i * 2 + u, u)
                    for u in range(2):
                        norm2.dve_apply(dve, y2_of[u], y_of[u], i * 2 + u, u, s_norm2)
                for u in range(2):
                    dve.wait_ge(s_proj, i * 2 + u + 1)
                    for b in range(BPT):
                        last = dve.tensor_copy(v_own[b * S:(b + 1) * S, 4 * u:4 * u + 4, b],
                                               psum[b * S:(b + 1) * S, 4 * u + 3].rearrange("p (t c) -> p t c", c=P))
                    last.then_inc(s_v, 1)
                if rotate:
                    for u in range(2):
                        for m, at in enumerate((1, 0, 2, 1)):
                            if m == 3:
                                dve.wait_ge(s_swap_k, i * 2 + u + 1)
                            dve.tensor_tensor(rot[:, u, m].rearrange("p (b s) -> p b s", s=S),
                                              psum[:, 4 * u + at].rearrange("p (b s) -> p b s", s=S),
                                              spread(core.const(rotate[m]), CHUNK // S, 1), ALU.mult).then_inc(s_rot, 1)
                    rotated(dve, link, i, 1, kT, s_k)
                if qk_norm:
                    for u in range(2):
                        for a, t, s_t in ((0, qT, s_q), (1, kT, s_k)):
                            dve.wait_ge(s_t, i * 2 + u + 1)
                            dve.tensor_tensor(scratch[:, u, a], t[:, u], t[:, u], ALU.mult).then_inc(s_square, 1)
                    for u in range(2):
                        for a in range(2):
                            dve.wait_ge(s_ms_sb, (i * 2 + u) * 2 + a + 1)
                            dve.reciprocal(scratch[:, u, a], scratch[:, u, a]).then_inc(s_power, 1)
                    for u in range(2):
                        for a, t in ((0, qT), (1, kT)):
                            dve.wait_ge(s_power, (i * 2 + u) * 2 + a + 1)
                            dve.scalar_tensor_tensor(out=t[:, u], in0=t[:, u], scalar=w(("qn", "kn")[a]), in1=scratch[:, u, a],
                                                     op0=ALU.mult, op1=ALU.mult).then_inc(s_unit, 1)

                def head(n):
                    e = E[:, n % 4]
                    src = bank_of(1).rearrange("p (m k) -> p m k", k=S)
                    dve.wait_ge(s_score, i * 8 + n + 1)
                    if mask == "decay":
                        dve.tensor_tensor(e.rearrange("p (g b) k -> p g b k", b=BPT),
                                          bank_of(1).rearrange("p (g b k) -> p g b k", b=BPT, k=S),
                                          spread(core.const2("decay0", "decay1").rearrange("p (g k) -> p g k", k=S), BPT, 2),
                                          ALU.mult).then_inc(s_mask, 1)
                        return
                    if mask == "causal":
                        dve.tensor_tensor(e, src, spread(core.const("causal_neg"), GB, 1), ALU.add).then_inc(s_mask, 1)
                        src = e
                        dve.wait_ge(s_mask, i * 8 + n + 1)
                    if mask == "fill":
                        dve.tensor_tensor(e, src, spread(core.const("causal"), GB, 1), ALU.mult).then_inc(s_kept, 1)
                        dve.wait_ge(s_kept, i * 8 + n + 1)
                        dve.tensor_tensor(e, e, spread(core.const("causal_fill"), GB, 1), ALU.add).then_inc(s_mask, 1)
                        src = e
                        dve.wait_ge(s_mask, i * 8 + n + 1)
                    dve.tensor_reduce(top[:, n % 4], src, AX.X, ALU.max).then_inc(s_top, 1)
                    dve.wait_ge(s_top, i * 8 + n + 1)
                    dve.tensor_tensor(e, src, spread(top[:, n % 4], S, 2), ALU.subtract).then_inc(s_sub, 1)

                def sums(n):
                    dve.wait_ge(s_exp, i * 8 + n + 1)
                    dve.tensor_reduce(total[:, n, 0], E[:, n % 4], AX.X, ALU.add).then_inc(s_sum, 1)
                    dve.wait_ge(s_sum, i * 8 + n + 1)
                    dve.reciprocal(total[:, n, 1], total[:, n, 0]).then_inc(s_recip, 1)

                def scaled(n):
                    src = psum[:, 4 + n % 2].rearrange("p (m c) -> p m c", c=GW)
                    mine = O_own[:, n % 4].rearrange("p b (g c) -> p g b c", c=GW)
                    by_group = lambda a: a.rearrange("p (g b) c -> p g b c", b=BPT)
                    own_all = spread(spread(own, G, 1), BPT, 2)
                    dve.wait_ge(s_pv, i * 8 + n + 1)
                    if not softmax:
                        dve.tensor_tensor(mine, by_group(src), own_all, ALU.mult).then_inc(s_scaled, 1)
                        return
                    dve.wait_ge(s_recip, i * 8 + n + 1)
                    dve.tensor_tensor(O[:, n % 4], src, spread(total[:, n, 1], GW, 2), ALU.mult).then_inc(s_scaled, 1)
                    dve.wait_ge(s_scaled, i * 8 + n + 1)
                    dve.tensor_tensor(mine, by_group(O[:, n % 4]), own_all, ALU.mult).then_inc(s_own, 1)

                for step in range(8 + 5):
                    if step < 8:
                        head(step)
                    if 0 <= step - 1 < 8 and softmax:
                        sums(step - 1)
                    if 0 <= step - 5 < 8:
                        scaled(step - 5)
                if post == "group_norm":
                    for u in range(2):
                        dve.wait_ge(s_aT, i * 2 + u + 1)
                        dve.wait_ge(s_mean, i * 2 + u + 1)
                        dve.scalar_tensor_tensor(out=aT[:, u, 1], in0=psum[:, 2 * u], scalar=-1.0 / dh, in1=aT[:, u, 0],
                                                 op0=ALU.mult, op1=ALU.add).then_inc(s_centred, 1)
                        dve.wait_ge(s_centred, i * 2 + u + 1)
                        dve.tensor_tensor(scratch[:, u, 0], aT[:, u, 1], aT[:, u, 1], ALU.mult).then_inc(s_dev, 1)
                    for u in range(2):
                        dve.wait_ge(s_sig, i * 2 + u + 1)
                        link(dve.tensor_tensor(aT[:, u, 2], aT[:, u, 2], psum[:, 2 * u + 1], ALU.mult))
                        dve.wait_ge(s_var_sb, i * 2 + u + 1)
                        link(dve.reciprocal(scratch[:, u, 1], scratch[:, u, 1]))
                        link(dve.tensor_tensor(aT[:, u, 1], aT[:, u, 1], scratch[:, u, 1], ALU.mult))
                        link(dve.tensor_scalar(aT[:, u, 1], aT[:, u, 1], w("gn_w"), w("gn_b"), ALU.mult, ALU.add))
                        dve.tensor_tensor(aT[:, u, 3], aT[:, u, 1], aT[:, u, 2], ALU.mult).then_inc(s_post, 1)
                if post == "gate":
                    for u in range(2):
                        dve.wait_ge(s_sig, i * 2 + u + 1)
                        dve.tensor_tensor(aT[:, u, 3], aT[:, u, 0], aT[:, u, 1], ALU.mult).then_inc(s_post, 1)
                for u in range(2):
                    dve.wait_ge(s_out, i * 2 + u + 1)
                    to = dest[:, bass.ds(i * 8 + 4 * u, 4)]
                    stay = Y[:, u] if keep is not None else to
                    link(dve.tensor_tensor(Y2[:, u], psum[:, 4 + u].rearrange("p (t c) -> p t c", c=P),
                                           spread(w("bo"), TPC, 1), ALU.add))
                    dve.tensor_tensor(to, Y2[:, u], stay, ALU.add).then_inc(s_done, 1)
        sc.close_block()


def front(core, name, weights, hT_all, logits=None, second=None, keep=None, prefetch=None):
    nc, X = core.nc, core.X
    ident = core.const("ident")
    PAIRS = CHUNKS // 2
    source, first = (X, True) if keep is None or keep[1] == "store" else (keep[0], False)
    with Scope(core, name) as sc:
        psum = sc.banks()
        w, arrived, fetch = sc.weights(weights)
        norm = Norm(sc, "ln", "eps5") if first else None
        norm2 = Norm(sc, "ln2", second[0], rms=second[1]) if second else None
        Y = sc.sb("normed", [P, 2, TPC, P])
        Y2 = sc.sb("normed2", [P, 2, TPC, P]) if second else Y
        s_norm, s_norm2, s_turn, s_hT = sc.sem("norm"), sc.sem("norm2"), sc.sem("turn"), sc.sem("hT")
        s_logits, s_logits_out, s_free = sc.sem("logits"), sc.sem("logits_out"), sc.sem("free")
        s_routed, passed_dve = sc.sem("routed"), sc.sem("passed_dve")
        direct = logits is None
        hT = sc.sb("hT", [P, 2, CHUNK]) if not direct else None
        block = sc.open_block()

        @block.sync
        def _(sp):
            fetch(sp)
            if prefetch is not None:
                prefetch(sp)

        @block.gpsimd
        def _(pool):
            if not direct:
                pool.sem_inc(s_logits_out, 2)
            with pool.Fori(0, PAIRS) as i:
                for n in (norm, norm2):
                    for u in range(2 if n is not None else 0):
                        n.pool_rstd(pool, i * 2 + u, u)
                for u in range(0 if direct else 2):
                    gate(pool, s_hT, i * 2 + u + 1, s_free)
                    pool.tensor_copy(hT_all[:, bass.ds((i * 2 + u) * CHUNK, CHUNK)], hT[:, u]).then_inc(s_logits_out, 1)

        @block.tensor
        def _(pe):
            arrived(pe)
            with pe.Fori(0, PAIRS) as i:
                for u in range(2):
                    pe.wait_ge(s_norm2 if second else s_norm, i * 2 + u + 1)
                    for k in range(TPC):
                        last = pe.transpose(psum[:, u, k * P:(k + 1) * P], Y2[:, u, k], ident)
                    last.then_inc(s_turn, 1)
                if logits is not None:
                    for u in range(2):
                        pe.wait_ge(s_hT, i * 2 + u + 1)
                        for k in range(TPC):
                            last = pe.matmul(psum[:, 2 + u, k * 8:(k + 1) * 8], hT[:, u, k * P:(k + 1) * P], w("router"),
                                             start=True, stop=True)
                        last.then_inc(s_logits, 1)

        @block.scalar
        def _(act):
            arrived(act)
            if direct:
                act.sem_inc(s_hT, 2)
            with act.Fori(0, PAIRS) as i:
                for u in range(2):
                    if direct:
                        gate(act, s_turn, i * 2 + u + 1, s_free)
                        out = hT_all[:, bass.ds((i * 2 + u) * CHUNK, CHUNK)]
                    else:
                        act.wait_ge(s_turn, i * 2 + u + 1)
                        out = hT[:, u]
                    act.activation(out, psum[:, u], ACT.Identity, bias=w("ln_b") if second else 0.0,
                                   scale=w("ln_w") if second else 1.0).then_inc(s_hT, 1)

        @block.vector
        def _(dve):
            arrived(dve)
            with dve.Fori(0, PAIRS) as i:
                at = lambda k, u: bass.ds(i * 8 + 4 * u + k, 1)
                x_of = [lambda k, u=u: X[:, at(k, u)] for u in range(2)]
                y_of = [(lambda k, u=u: keep[0][:, at(k, u)]) if keep else (lambda k, u=u: Y[:, u, k]) for u in range(2)]
                if first:
                    for u in range(2):
                        norm.dve_stats(dve, x_of[u], i * 2 + u, u)
                gate(dve, s_hT if direct else s_logits_out, i * 2 + 2, passed_dve)
                if first:
                    for u in range(2):
                        norm.dve_apply(dve, y_of[u], x_of[u], i * 2 + u, u, s_norm)
                if second:
                    for u in range(2):
                        if first:
                            dve.wait_ge(s_norm, i * 2 + u + 1)
                        norm2.dve_stats(dve, y_of[u], i * 2 + u, u)
                    for u in range(2):
                        norm2.dve_apply(dve, lambda k: Y2[:, u, k], y_of[u], i * 2 + u, u, s_norm2)
                if logits is not None:
                    for u in range(2):
                        dve.wait_ge(s_logits, i * 2 + u + 1)
                        dve.tensor_tensor(logits[:, bass.ds(i * 8 + 4 * u, TPC)],
                                          psum[:, 2 + u, 0:32].rearrange("p (t e) -> p t e", e=8),
                                          spread(w("router_b"), TPC, 1), ALU.add).then_inc(s_routed, 1)
        sc.close_block()


def first_of_max(dve, link, values, best, cand, onehot, order):
    E8 = values.shape[2]
    link(dve.tensor_reduce(best, values, AX.X, ALU.max))
    link(dve.tensor_tensor(cand, values, spread(best, E8, 2), ALU.is_equal))
    link(dve.tensor_tensor(cand, cand, order, ALU.mult))
    link(dve.tensor_reduce(best, cand, AX.X, ALU.max))
    link(dve.tensor_tensor(onehot, cand, spread(best, E8, 2), ALU.is_equal))


def gates(core, name, logits, comb, kind, capacity=None):
    nc = core.nc
    with Scope(core, name) as sc:
        psum = sc.banks()
        new = lambda n, e=8: sc.sb(n, [P, TILES, e])
        l, cand, one, two, t8, p8, rank1, rank2, tot = [new(n) for n in
            ("l", "cand", "one", "two", "t8", "p8", "rank1", "rank2", "tot")]
        tot_b = new("tot_b")
        best, v1, v2, r, ex = [sc.sb(n, [P, TILES]) for n in ("best", "v1", "v2", "r", "ex")]
        s_link, s_exp, s_need, s_rank = sc.sem("link"), sc.sem("exp"), sc.sem("need"), sc.sem("rank")
        order = spread(core.const("experts"), TILES, 1)
        flat = lambda a: a[:].rearrange("p t e -> p (t e)")
        block = sc.open_block()

        @block.vector
        def _(dve):
            link = Link(dve, s_link, 0)
            tt = lambda out, a, b, op: link(dve.tensor_tensor(out, a, b, op))
            over = lambda a: spread(a[:], 8, 2)
            link(dve.tensor_copy(l[:], logits[:]))
            if kind == "probs":
                link(dve.tensor_reduce(v1[:], l[:], AX.X, ALU.max))
                dve.tensor_tensor(t8[:], l[:], over(v1), ALU.subtract).then_inc(s_need, 1)
                dve.wait_ge(s_exp, 1)
                link(dve.tensor_reduce(r[:], p8[:], AX.X, ALU.add))
                link(dve.reciprocal(v1[:], r[:]))
                tt(l[:], p8[:], over(v1), ALU.mult)
            first_of_max(dve, link, l[:], best[:], cand[:], one[:], order)
            if kind == "top1":
                link(dve.tensor_copy(comb[:], one[:]))
                return
            link(dve.tensor_reduce(v1[:], l[:], AX.X, ALU.max))
            link(dve.scalar_tensor_tensor(out=t8[:], in0=one[:], scalar=-1e30, in1=l[:], op0=ALU.mult, op1=ALU.add))
            link(dve.tensor_reduce(v2[:], t8[:], AX.X, ALU.max))
            first_of_max(dve, link, t8[:], best[:], cand[:], two[:], order)
            dve.tensor_tensor(ex[:], v2[:], v1[:], ALU.subtract).then_inc(s_need, 1)
            dve.wait_ge(s_exp, 2 if kind == "probs" else 1)
            link(dve.tensor_scalar(ex[:], r[:], 1.0, None, ALU.add))
            link(dve.reciprocal(v1[:], ex[:]))
            tt(v2[:], v1[:], r[:], ALU.mult)
            if kind == "capacity":
                dve.wait_ge(s_rank, 1)
                ranks = [psum[:, a, 0:256].rearrange("p (t e) -> p t e", e=8) for a in range(4)]
                for mine, rank, out in ((0, rank1, one), (1, rank2, two)):
                    link(dve.memset(tot[:, 0:1], 0.0))
                    link(dve.tensor_copy(tot[:, 1:TILES], ranks[2 * mine + 1][:, 0:TILES - 1]))
                    a, b, step = tot, tot_b, 1
                    while step < TILES:
                        link(dve.tensor_copy(b[:, 0:step], a[:, 0:step]))
                        tt(b[:, step:TILES], a[:, step:TILES], a[:, 0:TILES - step], ALU.add)
                        a, b, step = b, a, 2 * step
                    tt(rank[:], a[:], ranks[2 * mine], ALU.add)
                    if mine == 0:
                        tt(cand[:, 0], a[:, TILES - 1], ranks[1][:, TILES - 1], ALU.add)
                    else:
                        tt(rank[:], rank[:], spread(cand[:, 0], TILES, 1), ALU.add)
                    link(dve.tensor_scalar(t8[:], rank[:], float(capacity), None, ALU.is_le))
                    tt(out[:], out[:], t8[:], ALU.mult)
            tt(one[:], one[:], over(v1), ALU.mult)
            tt(two[:], two[:], over(v2), ALU.mult)
            tt(comb[:], one[:], two[:], ALU.add)

        @block.scalar
        def _(act):
            if kind == "probs":
                act.wait_ge(s_need, 1)
                act.activation(p8[:], t8[:], ACT.Exp).then_inc(s_exp, 1)
            if kind != "top1":
                act.wait_ge(s_need, 2 if kind == "probs" else 1)
                act.activation(r[:], ex[:], ACT.Exp).then_inc(s_exp, 1)

        @block.tensor
        def _(pe):
            if kind == "capacity":
                pe.wait_ge(s_need, 1)
                for a, (table, choice) in enumerate((("upto", one), ("ones", one), ("upto", two), ("ones", two))):
                    last = pe.matmul(psum[:, a, 0:256], core.const(table), flat(choice), start=True, stop=True)
                last.then_inc(s_rank, 1)
        sc.close_block()


def experts(core, name, weights, hT_all, comb, E, nf, kind, base=None, shared=False, out_bias=False, b2=False):
    nc, X = core.nc, core.X
    pair = kind in ("silu", "glu")
    width = 2 if pair else 1
    jobs = [(e, nf) for e in range(E)] + ([(E, 1)] if shared else [])
    NJ = len(jobs)
    blocks = sum(n for _, n in jobs)
    first_block = [sum(n for _, n in jobs[:e]) for e in range(NJ)]
    RING = 4 // width
    with Scope(core, name) as sc:
        psum = sc.banks()
        w, arrived, fetch = sc.weights(weights)
        act_sb = sc.sb("act", [P, RING, CHUNK]) if pair else None
        hidden = sc.sb("hidden", [P, 2, nf, CHUNK])
        combT = sc.sb("combT", [8, TPC, P]) if b2 else None
        s_up, s_act, s_hidden = sc.sem("up"), sc.sem("act"), sc.sem("hidden")
        s_down, s_acc, s_base = sc.sem("down"), sc.sem("acc"), sc.sem("base")
        s_cT, s_combT, s_b2 = sc.sem("cT"), sc.sem("combT"), sc.sem("b2")
        comb_now = sc.sb("comb_now", [P, TPC, 8]) if comb is not None else None
        s_comb, s_b2_added = sc.sem("comb"), sc.sem("b2_added")
        block = sc.open_block()

        @block.sync
        def _(sp):
            fetch(sp)

        @block.tensor
        def _(pe):
            arrived(pe)
            with pe.Fori(0, CHUNKS) as c:
                rhs = hT_all[:, bass.ds(c * CHUNK, CHUNK)]
                if b2:
                    pe.wait_ge(s_comb, c + 1)
                    for k in range(TPC):
                        last = pe.transpose(psum[0:8, 6, k * P:(k + 1) * P], comb_now[:, k], core.const("ident"))
                    last.then_inc(s_cT, 1)

                def up(j):
                    for f in range(jobs[j][1]):
                        m = first_block[j] + f
                        if m >= RING:
                            pe.wait_ge(s_hidden, c * blocks + m - RING + 1)
                        for half in range(width):
                            last = pe.matmul(psum[:, (m % RING) * width + half], w("up")[:, (m * width + half) * P:(m * width + half + 1) * P],
                                             rhs, start=True, stop=True)
                        last.then_inc(s_up, 1)

                def down(j):
                    n = jobs[j][1]
                    pe.wait_ge(s_hidden, c * blocks + first_block[j] + n)
                    if j >= 2:
                        pe.wait_ge(s_acc, c * NJ + j - 1)
                    for k in range(TPC):
                        for f in range(n):
                            m = first_block[j] + f
                            last = pe.matmul(psum[:, 4 + j % 2, k * P:(k + 1) * P], hidden[:, j % 2, f, k * P:(k + 1) * P],
                                             w("down")[:, m * P:(m + 1) * P], start=(f == 0), stop=(f == n - 1))
                    last.then_inc(s_down, 1)

                for j in range(NJ + 1):
                    if j < NJ:
                        up(j)
                    if j == 0 and b2:
                        pe.wait_ge(s_combT, c + 1)
                        for k in range(TPC):
                            last = pe.matmul(psum[:, 7, k * P:(k + 1) * P], combT[:, k], w("b2")[0:8], start=True, stop=True)
                        last.then_inc(s_b2, 1)
                    if j >= 1:
                        down(j - 1)

        @block.scalar
        def _(act):
            arrived(act)
            with act.Fori(0, CHUNKS) as c:
                if b2:
                    act.wait_ge(s_cT, c + 1)
                    act.activation(combT[:].rearrange("p k t -> p (k t)"), psum[0:8, 6], ACT.Copy).then_inc(s_combT, 1)
                for j in range(NJ):
                    for f in range(jobs[j][1]):
                        m = first_block[j] + f
                        at = (m % RING) * width
                        act.wait_ge(s_up, c * blocks + m + 1)
                        if kind == "silu":
                            if m >= RING:
                                act.wait_ge(s_hidden, c * blocks + m - RING + 1)
                            act.activation(act_sb[:, m % RING], psum[:, at], ACT.Silu).then_inc(s_act, 1)
                        elif kind == "glu":
                            if m >= RING:
                                act.wait_ge(s_hidden, c * blocks + m - RING + 1)
                            act.activation(act_sb[:, m % RING], psum[:, at + 1], ACT.Sigmoid,
                                           bias=w("b1")[:, 2 * m + 1:2 * m + 2]).then_inc(s_act, 1)
                        else:
                            if f == 0 and j >= 2:
                                act.wait_ge(s_down, c * NJ + j - 1)
                            elif f == 0 and j < 2:
                                act.wait_ge(s_base, c + 1)
                            act.activation(hidden[:, j % 2, f], psum[:, at],
                                           ACT.Gelu_apprx_tanh if kind == "gelu_tanh" else ACT.Gelu,
                                           bias=w("b1")[:, m:m + 1] if kind == "gelu_tanh" else 0.0).then_inc(s_hidden, 1)

        @block.vector
        def _(dve):
            arrived(dve)
            with dve.Fori(0, CHUNKS) as c:
                chunk = bass.ds(c * TPC, TPC)
                if comb is not None:
                    dve.tensor_copy(comb_now[:], comb[:, chunk]).then_inc(s_comb, 1)
                if out_bias:
                    dve.tensor_tensor(X[:, chunk], X[:, chunk], spread(w("bo"), TPC, 1), ALU.add).then_inc(s_b2, 1)
                    dve.wait_ge(s_b2, c + 1)
                if base is not None:
                    dve.tensor_tensor(X[:, chunk], X[:, chunk], base[:, chunk], ALU.add).then_inc(s_base, 1)
                else:
                    dve.engine_nop().then_inc(s_base, 1)
                if comb is not None:
                    dve.wait_ge(s_comb, c + 1)
                dve.wait_ge(s_base, c + 1)
                if b2:
                    dve.wait_ge(s_b2, c + 1)
                    dve.tensor_tensor(X[:, chunk], psum[:, 7].rearrange("p (k d) -> p k d", k=TPC), X[:, chunk],
                                      ALU.add).then_inc(s_b2_added, 1)
                    dve.wait_ge(s_b2_added, c + 1)

                def add(j):
                    dve.wait_ge(s_down, c * NJ + j + 1)
                    if j >= 1:
                        dve.wait_ge(s_acc, c * NJ + j)
                    if comb is None or j >= E:
                        dve.tensor_tensor(X[:, chunk], psum[:, 4 + j % 2].rearrange("p (k d) -> p k d", k=TPC), X[:, chunk],
                                          ALU.add).then_inc(s_acc, 1)
                        return
                    for k in range(TPC):
                        xk = X[:, bass.ds(c * TPC + k, 1)]
                        last = dve.scalar_tensor_tensor(out=xk, in0=psum[:, 4 + j % 2:5 + j % 2, k * P:(k + 1) * P],
                                                        scalar=comb_now[:, k, j:j + 1], in1=xk, op0=ALU.mult, op1=ALU.add)
                    last.then_inc(s_acc, 1)

                for j in range(NJ):
                    if pair:
                        for f in range(jobs[j][1]):
                            m = first_block[j] + f
                            at = (m % RING) * width
                            dve.wait_ge(s_act, c * blocks + m + 1)
                            if f == 0 and j >= 2:
                                dve.wait_ge(s_down, c * NJ + j - 1)
                            if kind == "silu":
                                dve.tensor_tensor(hidden[:, j % 2, f], act_sb[:, m % RING], psum[:, at + 1], ALU.mult).then_inc(s_hidden, 1)
                            else:
                                dve.scalar_tensor_tensor(out=hidden[:, j % 2, f], in0=psum[:, at], scalar=w("b1")[:, 2 * m:2 * m + 1],
                                                         in1=act_sb[:, m % RING], op0=ALU.add, op1=ALU.mult).then_inc(s_hidden, 1)
                    if j >= 1:
                        add(j - 1)
                add(NJ - 1)
                dve.wait_ge(s_acc, c * NJ + NJ)
        sc.close_block()



def cross_attention(core, name, weights, hT_all, context, scale, mask=None):
    nc, X = core.nc, core.X
    N, G = 8, 4
    TURNS = B // N
    ident = core.const("ident")
    LAST = 2 * G
    with Scope(core, name) as sc:
        psum = sc.banks()
        S_BANK, K_BANK, V_BANK, T_BANK, O_BANK = 0, 4, 5, 6, 7
        w, arrived, fetch = sc.weights(weights)
        ctx_sb = sc.sb("context", [P, N, SK])
        kT = sc.sb("kT", [P, 2, SK])
        v_sb = sc.sb("v", [P, 4, 2, P])
        v_last = sc.sb("v_last", [LAST, 4, P])
        qT = sc.sb("qT", [P, 2, P])
        q_heads = sc.sb("q_heads", [P, 2, BPT, 16, S])
        E = sc.sb("E", [P, 2, LAST, SK])
        ET = sc.sb("ET", [P, 2, 2, G * P])
        E_last = sc.sb("E_last", [LAST, 2, P])
        top = sc.sb("top", [P, 2, G])
        negtop = sc.sb("negtop", [P, 2, G])
        total = sc.sb("total", [P, 2, G])
        factor = sc.sb("factor", [P, P])
        O = sc.sb("O", [P, P])
        O_sum = sc.sb("O_sum", [P, 2, S])
        aT = sc.sb("aT", [P, 2, P])
        Xb = sc.sb("sum", [P, 2, P])
        if mask is not None:
            mask_int = sc.sb("mask_int", [P, SK], mybir.dt.int32)
            mask_neg = sc.sb("mask_neg", [P, SK], BF16)
            ident_bf = sc.sb("ident_bf", [P, P], BF16)
        s_ctx = [sc.sem(f"ctx{n}") for n in range(N)]
        s_mask, s_mask_ready = sc.sem("mask"), sc.sem("mask_ready")
        s_qp, s_q, s_heads = sc.sem("qp"), sc.sem("q"), sc.sem("heads")
        s_kp, s_k, s_vp, s_v = sc.sem("kp"), sc.sem("k"), sc.sem("vp"), sc.sem("v")
        s_score, s_top, s_neg, s_exp = sc.sem("score"), sc.sem("top"), sc.sem("neg"), sc.sem("exp")
        s_t, s_t1, s_tl = sc.sem("t"), sc.sem("t1"), sc.sem("tl")
        s_ET, s_ET1, s_ETl = sc.sem("ET"), sc.sem("ET1"), sc.sem("ETl")
        s_pv, s_fold, s_inv, s_scaled = sc.sem("pv"), sc.sem("fold"), sc.sem("inv"), sc.sem("scaled")
        s_factor, s_aT, s_out, s_bias, s_done = sc.sem("factor"), sc.sem("aT"), sc.sem("out"), sc.sem("bias"), sc.sem("done")
        block = sc.open_block()

        def turns(eng, step):
            for n in range(N):
                step(0, n)
            with eng.Fori(1, TURNS - 1) as i:
                for n in range(N):
                    step(i, n)
            for n in range(N + 2):
                step(TURNS - 1, n)

        def exists(i, n):
            return not isinstance(i, int) or 0 <= i * N + n < B

        @block.sync
        def _(sp):
            fetch(sp)
            if mask is not None:
                for j in range(4):
                    sp.dma_start(mask_int[j * S:(j + 1) * S], mask).then_inc(s_mask, 16)
            for n in range(N):
                sp.dma_start(ctx_sb[:, n], context[:, n]).then_inc(s_ctx[n], 16)
            with sp.Fori(1, TURNS) as i:
                for n in range(N):
                    sp.wait_ge(s_vp, i * N - N + n + 1)
                    sp.wait_ge(s_kp, i * N - N + n + 1)
                    sp.dma_start(ctx_sb[:, n], context[:, bass.ds(i * N + n, 1)]).then_inc(s_ctx[n], 16)

        @block.gpsimd
        def _(pool):
            with pool.Fori(0, TURNS) as i:
                for t in range(2):
                    pool.wait_ge(s_q, i * 2 + t + 1)
                    pool.tensor_tensor(q_heads[:, t], spread(qT[:, t].rearrange("p (b s) -> p b s", s=S), 16, 2),
                                       spread(spread(core.const("heads16"), BPT, 1), S, 3), ALU.mult).then_inc(s_heads, 1)

        @block.tensor
        def _(pe):
            arrived(pe)
            if mask is not None:
                pe.wait_ge(s_mask_ready, 2)

            def queries(i, t):
                tile = (i * 2 + t) * P
                source = hT_all[:, tile:tile + P] if isinstance(tile, int) else hT_all[:, bass.ds(tile, P)]
                pe.matmul(psum[:, T_BANK, 0:P], w("wq"), source, start=True, stop=True).then_inc(s_qp, 1)

            def project_values(i, n):
                pe.wait_ge(s_ctx[n % N], i * 16 + n // N * 16 + 16)
                if exists(i, n - 1):
                    pe.wait_ge(s_v, i * N + n)
                for c in range(2):
                    pe.matmul(psum[:, V_BANK, c * P:(c + 1) * P], ctx_sb[:, n % N, c * P:(c + 1) * P], w("wv"),
                              start=True, stop=True)
                pe.matmul(psum[0:LAST, V_BANK, 2 * P:3 * P], ctx_sb[:, n % N, SK - 1:SK].to_broadcast([P, LAST]), w("wv"),
                          start=True, stop=True).then_inc(s_vp, 1)

            def project_keys(i, n):
                if exists(i, n - 2):
                    pe.wait_ge(s_ET1, i * N + n - 1)
                pe.matmul(psum[:, K_BANK, 0:SK], w("wk"), ctx_sb[:, n % N], start=True, stop=True).then_inc(s_kp, 1)

            def scores(i, n):
                pe.wait_ge(s_k, i * N + n + 1)
                if n % 4 == 0:
                    pe.wait_ge(s_heads, i * 2 + n // 4 + 1)
                for g in range(G):
                    if exists(i, n - 1):
                        pe.wait_ge(s_exp, (i * N + n - 1) * G + g + 1)
                    last = pe.matmul(psum[:, S_BANK + g, 0:SK], q_heads[:, n // 4, n % 4, 4 * g:4 * g + 4].rearrange("p h s -> p (h s)"),
                                     kT[:, n % 2], start=True, stop=mask is None)
                    if mask is not None:
                        last = pe.matmul(psum[:, S_BANK + g, 0:SK], ident_bf[:], mask_neg[:], start=False, stop=True)
                    last.then_inc(s_score, 1)

            def turn(i, n):
                pe.wait_ge(s_exp, (i * N + n) * G + G)
                if n % 4 == 1 and exists(i, n + 3):
                    pe.wait_ge(s_q, i * 2 + n // 4 + 2)
                for c, bank in ((0, T_BANK), (1, K_BANK)):
                    for g in range(G):
                        last = pe.transpose(psum[:, bank, g * P:(g + 1) * P], E[:, n % 2, g, c * P:(c + 1) * P], ident)
                    last.then_inc((s_t, s_t1)[c], 1)

            def turn_last(i, n):
                pe.wait_ge(s_inv, i * N + n + 1)
                if exists(i, n - 1):
                    pe.wait_ge(s_scaled, i * N + n)
                if n % 4 == 0 and exists(i, n - 4):
                    pe.wait_ge(s_bias, i * 2 + n // 4)
                pe.transpose(psum[0:LAST, O_BANK, 2 * P:3 * P], E[:, n % 2, :, SK - 1], ident).then_inc(s_tl, 1)

            def values(i, n):
                pe.wait_ge(s_v, i * N + n + 1)
                pe.wait_ge(s_ETl, i * N + n + 1)
                pe.matmul(psum[:, O_BANK, P:2 * P], core.const("group_of_late")[0:LAST], E_last[:, n % 2], start=True, stop=True)
                pe.matmul(psum[:, O_BANK, 0:P], v_last[:, n % 4], E_last[:, n % 2], start=True, stop=False)
                pe.wait_ge(s_ET, i * N + n + 1)
                pe.wait_ge(s_ET1, i * N + n + 1)
                for c in range(2):
                    for g in range(G):
                        last = pe.matmul(psum[g * 32:(g + 1) * 32, O_BANK, 0:P], v_sb[:, n % 4, c, g * 32:(g + 1) * 32],
                                         ET[:, n % 2, c, g * P:(g + 1) * P], start=False, stop=(c == 1))
                last.then_inc(s_pv, 1)

            def output(i, t):
                pe.wait_ge(s_aT, i * N + 4 * t + 4)
                pe.matmul(psum[:, O_BANK, 3 * P:4 * P], aT[:, t % 2], w("wo"), start=True, stop=True).then_inc(s_out, 1)

            def step(i, n):
                if exists(i, n):
                    scores(i, n)
                if exists(i, n - 1):
                    turn(i, n - 1)
                if exists(i, n - 2) and (n - 2) % 4 == 3:
                    output(i, (n - 2) // 4)
                if exists(i, n - 1):
                    turn_last(i, n - 1)
                if exists(i, n + 1):
                    project_values(i, n + 1)
                    project_keys(i, n + 1)
                if exists(i, n - 1):
                    values(i, n - 1)
                if n % 4 == 1 and exists(i, n + 3):
                    queries(i, n // 4 + 1)

            queries(0, 0)
            project_values(0, 0)
            project_keys(0, 0)
            turns(pe, step)

        @block.scalar
        def _(act):
            arrived(act)

            def queries(i, t):
                act.wait_ge(s_qp, i * 2 + t + 1)
                act.activation(qT[:, t % 2], psum[:, T_BANK, 0:P], ACT.Identity, bias=w("bq")).then_inc(s_q, 1)

            def keys(i, n):
                act.wait_ge(s_kp, i * N + n + 1)
                if exists(i, n - 2):
                    act.wait_ge(s_score, (i * N + n - 1) * G)
                act.activation(kT[:, n % 2], psum[:, K_BANK, 0:SK], ACT.Identity, bias=w("bk")).then_inc(s_k, 1)

            def exponentials(i, n, half):
                act.wait_ge(s_neg, (i * N + n) * 2 + half + 1)
                if exists(i, n - 2) and half == 0:
                    act.wait_ge(s_tl, i * N + n - 1)
                for g in (2 * half, 2 * half + 1):
                    act.activation(E[:, n % 2, g], psum[:, S_BANK + g, 0:SK], ACT.Exp, scale=scale,
                                   bias=negtop[:, n % 2, g:g + 1], accum_out=total[:, n % 2, g:g + 1]).then_inc(s_exp, 1)

            def second_half(i, n):
                act.wait_ge(s_t1, i * N + n + 1)
                act.activation(ET[:, n % 2, 1], psum[:, K_BANK], ACT.Copy).then_inc(s_ET1, 1)

            def folded(i, n):
                act.wait_ge(s_fold, i * N + n + 1)
                act.activation(aT[:, n // 4 % 2, (n % 4) * S:(n % 4 + 1) * S], O_sum[:, n % 2], ACT.Identity,
                               bias=w("bv")).then_inc(s_aT, 1)

            def step(i, n):
                if exists(i, n):
                    exponentials(i, n, 0)
                if exists(i, n - 2):
                    folded(i, n - 2)
                if exists(i, n - 1):
                    second_half(i, n - 1)
                if exists(i, n + 1):
                    keys(i, n + 1)
                if exists(i, n):
                    exponentials(i, n, 1)
                if n % 4 == 1 and exists(i, n + 3):
                    queries(i, n // 4 + 1)

            queries(0, 0)
            keys(0, 0)
            turns(act, step)

        @block.vector
        def _(dve):
            arrived(dve)
            if mask is not None:
                dve.wait_ge(s_mask, 64)
                dve.tensor_copy(ident_bf[:], ident).then_inc(s_mask_ready, 1)
                dve.tensor_scalar(mask_neg[:], mask_int[:], 0.0, -1e30, ALU.is_equal, ALU.mult).then_inc(s_mask_ready, 1)

            def values_out(i, n):
                dve.wait_ge(s_vp, i * N + n + 1)
                dve.tensor_copy(v_sb[:, n % 4], psum[:, V_BANK, 0:2 * P].rearrange("p (c d) -> p c d", c=2))
                dve.tensor_tensor(v_last[:, n % 4], psum[0:LAST, V_BANK, 2 * P:3 * P], core.const("group_of")[0:LAST],
                                  ALU.mult).then_inc(s_v, 1)

            def maximum(i, n, half):
                at = slice(2 * half, 2 * half + 2)
                dve.wait_ge(s_score, (i * N + n) * G + 2 * half + 2)
                dve.tensor_reduce(top[:, n % 2, at], psum[:, S_BANK + 2 * half:S_BANK + 2 * half + 2, 0:SK], AX.X,
                                  ALU.max).then_inc(s_top, 1)
                dve.wait_ge(s_top, (i * N + n) * 2 + half + 1)
                dve.tensor_scalar(negtop[:, n % 2, at], top[:, n % 2, at], -scale, None, ALU.mult).then_inc(s_neg, 1)

            def first_half(i, n):
                dve.wait_ge(s_t, i * N + n + 1)
                dve.tensor_copy(ET[:, n % 2, 0], psum[:, T_BANK]).then_inc(s_ET, 1)

            def reciprocals(i, n):
                dve.wait_ge(s_exp, (i * N + n) * G + G)
                dve.reciprocal(E[:, n % 2, G:LAST, SK - 1], total[:, n % 2]).then_inc(s_inv, 1)

            def last_key(i, n):
                dve.wait_ge(s_tl, i * N + n + 1)
                dve.tensor_copy(E_last[:, n % 2], psum[0:LAST, O_BANK, 2 * P:3 * P]).then_inc(s_ETl, 1)

            def scaled(i, n):
                heads = lambda ap: ap.rearrange("p (j q) -> p j q", j=4)
                dve.wait_ge(s_pv, i * N + n + 1)
                dve.tensor_tensor(heads(factor[:]), heads(psum[:, O_BANK, P:2 * P]), spread(core.const("head_in_group"), S, 2),
                                  ALU.mult).then_inc(s_factor, 1)
                dve.wait_ge(s_factor, i * N + n + 1)
                dve.tensor_tensor(O[:], psum[:, O_BANK, 0:P], factor[:], ALU.mult).then_inc(s_scaled, 1)
                dve.wait_ge(s_scaled, i * N + n + 1)
                dve.tensor_reduce(O_sum[:, n % 2], O[:].rearrange("p (j q) -> p q j", j=4), AX.X, ALU.add).then_inc(s_fold, 1)

            def output(i, t):
                dve.wait_ge(s_out, i * 2 + t + 1)
                dve.tensor_tensor(Xb[:, t % 2], psum[:, O_BANK, 3 * P:4 * P], w("bo"), ALU.add).then_inc(s_bias, 1)
                dve.wait_ge(s_bias, i * 2 + t + 1)
                at = i * 2 + t
                xt = X[:, at:at + 1] if isinstance(at, int) else X[:, bass.ds(at, 1)]
                dve.tensor_tensor(xt, Xb[:, t % 2:t % 2 + 1], xt, ALU.add).then_inc(s_done, 1)

            def step(i, n):
                if exists(i, n):
                    maximum(i, n, 0)
                if exists(i, n - 1):
                    reciprocals(i, n - 1)
                if exists(i, n):
                    maximum(i, n, 1)
                if exists(i, n - 1):
                    first_half(i, n - 1)
                if exists(i, n - 2) and (n - 2) % 4 == 3:
                    output(i, (n - 2) // 4)
                if exists(i, n - 1):
                    last_key(i, n - 1)
                if exists(i, n + 1):
                    values_out(i, n + 1)
                if exists(i, n - 1):
                    scaled(i, n - 1)

            values_out(0, 0)
            turns(dve, step)
        sc.close_block()


GENERATED = {}
_at = 0
for _name, _width in (("ca", 384), ("cp", 128), ("cf", 512), ("cm", 512),
                      ("ca_b", 3), ("cp_b", 128), ("cf_b", 4), ("cm_b", 128)):
    GENERATED[_name] = (_at, _width)
    _at += _width
GEN_WIDTH = _at


def generate(core, name, weights, out):
    nc = core.nc
    with Scope(core, name) as sc:
        w, arrived, fetch = sc.weights(weights)
        s_link, s_sum, s_tanh = sc.sem("link"), sc.sem("sum"), sc.sem("tanh")
        block = sc.open_block()

        @block.sync
        def _(sp):
            fetch(sp)

        @block.vector
        def _(dve):
            link = Link(dve, s_link, 0)
            arrived(dve)
            link(dve.tensor_copy(out[:, GEN_WIDTH:GEN_WIDTH + 4], w("norms")))
            for n, (at, width) in enumerate(GENERATED.values()):
                sl = slice(at, at + width)
                link(dve.tensor_scalar(out[:, sl], w("sub0")[:, sl], w("wl")[:, 2 * n:2 * n + 1], None, ALU.mult))
                dve.scalar_tensor_tensor(out=out[:, sl], in0=w("sub1")[:, sl], scalar=w("wl")[:, 2 * n + 1:2 * n + 2],
                                         in1=out[:, sl], op0=ALU.mult, op1=ALU.add).then_inc(s_sum, 1)
            dve.wait_ge(s_tanh, 1)
            link(dve.tensor_tensor(out[:, 0:GEN_WIDTH], out[:, 0:GEN_WIDTH], w("W"), ALU.mult))
            link(dve.tensor_tensor(out[:, 0:GEN_WIDTH], out[:, 0:GEN_WIDTH], w("B"), ALU.add))

        @block.scalar
        def _(act):
            act.wait_ge(s_sum, len(GENERATED))
            act.activation(out[:, 0:GEN_WIDTH], out[:, 0:GEN_WIDTH], ACT.Tanh).then_inc(s_tanh, 1)
        sc.close_block()


ROUND = 12582912.0


def quantised_ffn(core, name, weights, hT_all):
    nc, X = core.nc, core.X
    PAIRS, NF = CHUNKS // 2, 4
    ident, ones = core.const("ident"), core.const("ones")
    with Scope(core, name) as sc:
        psum = sc.banks()
        w, arrived, fetch = sc.weights(weights)
        w_abs = sc.sb("w_abs", [P, 2, NF * P])
        w_int = sc.sb("w_int", [P, 2, NF * P])
        up = sc.sb("up", [P, NF * P], BF16)
        down = sc.sb("down", [P, NF * P], BF16)
        s_w = sc.sb("scale_w", [P, NF + 1])
        peak = sc.sb("peak", [P, 4])
        s_in = sc.sb("scale_in", [P, 2])
        inv_w = sc.sb("inverse_w", [P, NF + 1])
        inv_in = sc.sb("inverse_in", [P, 2])
        s_out = sc.sb("scale_out", [P, NF + 1])
        bq = sc.sb("bias", [P, NF + 1])
        tmp = sc.sb("bias_steps", [P, 6, NF])
        diagonal = sc.sb("diagonal", [P, 4, P])
        rows = sc.sb("rows", [P, 2, P])
        shifted = sc.sb("shifted", [P, 2, CHUNK])
        x_int = sc.sb("x_int", [P, 2, CHUNK], BF16)
        H = sc.sb("H", [P, NF, TOK])
        highest = sc.sb("highest", [P, NF, CHUNK])
        shifted2 = sc.sb("shifted2", [P, 2, NF, CHUNK])
        h_int = sc.sb("h_int", [P, 2, NF, CHUNK], BF16)
        product = sc.sb("product", [P, 2, TPC, P])
        s_link, s_w_int, s_turned, s_w_bf = sc.sem("link"), sc.sem("w_int"), sc.sem("turned"), sc.sem("w_bf")
        s_diagonal, s_spread, s_ready = sc.sem("diagonal"), sc.sem("spread"), sc.sem("ready")
        s_div, s_shift, s_x_int, s_up, s_H = sc.sem("div"), sc.sem("shift"), sc.sem("x_int"), sc.sem("up"), sc.sem("H")
        s_high, s_div2, s_shift2, s_h_int = sc.sem("high"), sc.sem("div2"), sc.sem("shift2"), sc.sem("h_int")
        s_down, s_prod, s_bias, s_done = sc.sem("down"), sc.sem("prod"), sc.sem("bias"), sc.sem("done")
        passed_act, passed_dve = sc.sem("passed_act"), sc.sem("passed_dve")
        block = sc.open_block()

        @block.sync
        def _(sp):
            fetch(sp)

        @block.vector
        def _(dve):
            link = Link(dve, s_link, 0)
            arrived(dve)

            def divided(out, x, inverse):
                return dve.tensor_scalar(out, x, inverse, ROUND, ALU.mult, ALU.add)

            def whole_maximum(n, least, steps):
                dve.tensor_scalar(diagonal[:, n], ident, peak[:, 2 * n:2 * n + 1], None, ALU.mult).then_inc(s_diagonal, 1)
                dve.wait_ge(s_spread, n + 1)
                link(dve.tensor_reduce(peak[:, 2 * n + 1:2 * n + 2], psum[:, n, 0:P], AX.X, ALU.max))
                link(dve.tensor_scalar(s_in[:, n:n + 1], peak[:, 2 * n + 1:2 * n + 2], least, 1.0 / steps, ALU.max, ALU.mult))
                link(dve.reciprocal(inv_in[:, n:n + 1], s_in[:, n:n + 1]))

            def bias_on_grid(n, at, width):
                scale, b = s_out[:, at:at + width], w("b")[:, at:at + width]
                r, a, ra, small, sign = (tmp[:, k, 0:width] for k in range(5))
                link(dve.tensor_scalar(scale, s_w[:, at:at + width], s_in[:, n:n + 1], None, ALU.mult))
                link(dve.reciprocal(tmp[:, 5, 0:width], scale))
                link(dve.tensor_tensor(r, b, tmp[:, 5, 0:width], ALU.mult))
                link(dve.scalar_tensor_tensor(out=a, in0=r, scalar=-1.0, in1=r, op0=ALU.mult, op1=ALU.max))
                link(dve.tensor_scalar(ra, a, 8388608.0, 8388608.0, ALU.add, ALU.subtract))
                link(dve.tensor_tensor(ra, ra, a, ALU.subtract))
                link(dve.tensor_scalar(small, a, 8388608.0, None, ALU.is_lt))
                link(dve.tensor_tensor(ra, ra, small, ALU.mult))
                link(dve.tensor_tensor(a, a, ra, ALU.add))
                link(dve.tensor_scalar(sign, r, 0.0, 2.0, ALU.is_ge, ALU.mult))
                link(dve.tensor_scalar(sign, sign, 1.0, None, ALU.subtract))
                link(dve.tensor_tensor(a, a, sign, ALU.mult))
                link(dve.tensor_tensor(bq[:, at:at + width], a, scale, ALU.mult))

            link(dve.tensor_reduce(peak[:, 0:1], hT_all[:], AX.X, ALU.max))
            for n, part in enumerate(("w1", "w2")):
                link(dve.scalar_tensor_tensor(out=w_abs[:, n], in0=w(part), scalar=-1.0, in1=w(part), op0=ALU.mult, op1=ALU.max))
            link(dve.tensor_reduce(s_w[:, 0:NF], w_abs[:, 0].rearrange("p (f d) -> p f d", d=P), AX.X, ALU.max))
            link(dve.tensor_reduce(s_w[:, NF:NF + 1], w_abs[:, 1], AX.X, ALU.max))
            link(dve.tensor_scalar(s_w[:], s_w[:], 1e-8, 1.0 / 127.0, ALU.max, ALU.mult))
            link(dve.reciprocal(inv_w[:], s_w[:]))
            for f in range(NF):
                link(divided(w_int[:, 0, f * P:(f + 1) * P], w("w1")[:, f * P:(f + 1) * P], inv_w[:, f:f + 1]))
            link(divided(w_int[:, 1], w("w2"), inv_w[:, NF:NF + 1]))
            link(dve.tensor_scalar(w_int[:], w_int[:], ROUND + 127.0, ROUND - 128.0, ALU.min, ALU.max))
            dve.tensor_scalar(w_int[:], w_int[:], ROUND, None, ALU.subtract).then_inc(s_w_int, 1)
            whole_maximum(0, 1e-8, 255.0)
            bias_on_grid(0, 0, NF)
            link(dve.memset(highest[:], 0.0))
            dve.engine_nop().then_inc(s_ready, 1)
            with dve.Fori(0, PAIRS) as i:
                for u in range(2):
                    divided(shifted[:, u:u + 1], hT_all[:].rearrange("p (c n) -> p c n", n=CHUNK)[:, bass.ds(i * 2 + u, 1)],
                            inv_in[:, 0:1]).then_inc(s_div, 1)
                    dve.wait_ge(s_div, i * 2 + u + 1)
                    dve.tensor_scalar(shifted[:, u], shifted[:, u], ROUND + 255.0, ROUND, ALU.min, ALU.max).then_inc(s_shift, 1)
                for u in range(2):
                    dve.wait_ge(s_H, (i * 2 + u) * NF + NF)
                    dve.tensor_tensor(highest[:], H[:, :, bass.ds((i * 2 + u) * CHUNK, CHUNK)], highest[:], ALU.max).then_inc(s_high, 1)
                    dve.wait_ge(s_high, i * 2 + u + 1)
            link(dve.tensor_reduce(peak[:, 2:3], highest[:], AX.XY, ALU.max))
            whole_maximum(1, 1e-8, 255.0)
            bias_on_grid(1, NF, 1)
            dve.tensor_scalar(diagonal[:, 2], ident, s_out[:, NF:NF + 1], None, ALU.mult).then_inc(s_diagonal, 1)
            dve.tensor_scalar(diagonal[:, 3], ident, bq[:, NF:NF + 1], None, ALU.mult).then_inc(s_diagonal, 1)
            dve.wait_ge(s_spread, 4)
            dve.tensor_copy(rows[:], psum[:, 2, 0:2 * P].rearrange("p (n d) -> p n d", n=2)).then_inc(s_ready, 1)
            dve.wait_ge(s_ready, 2)
            with dve.Fori(0, PAIRS) as i:
                for u in range(2):
                    dve.tensor_scalar(shifted2[:, u], H[:, :, bass.ds((i * 2 + u) * CHUNK, CHUNK)], inv_in[:, 1:2], ROUND,
                                      ALU.mult, ALU.add).then_inc(s_div2, 1)
                    dve.wait_ge(s_div2, i * 2 + u + 1)
                    dve.tensor_scalar(shifted2[:, u], shifted2[:, u], ROUND + 255.0, ROUND, ALU.min, ALU.max).then_inc(s_shift2, 1)
                for u in range(2):
                    dve.wait_ge(s_down, i * 2 + u + 1)
                    dve.tensor_tensor(product[:, u], psum[:, 4 + u].rearrange("p (k d) -> p k d", k=TPC),
                                      spread(rows[:, 0], TPC, 1), ALU.mult).then_inc(s_prod, 1)
                    dve.wait_ge(s_prod, i * 2 + u + 1)
                    dve.wait_ge(s_bias, i * 2 + u + 1)
                    xc = X[:, bass.ds((i * 2 + u) * TPC, TPC)]
                    dve.tensor_tensor(xc, product[:, u], xc, ALU.add).then_inc(s_done, 1)

        @block.gpsimd
        def _(pool):
            pool.wait_ge(s_ready, 2)
            with pool.Fori(0, CHUNKS) as c:
                xc = X[:, bass.ds(c * TPC, TPC)]
                pool.tensor_tensor(xc, xc, spread(rows[:, 1], TPC, 1), ALU.add).then_inc(s_bias, 1)

        @block.tensor
        def _(pe):
            pe.wait_ge(s_w_int, 1)
            for n in range(2):
                for f in range(NF):
                    pe.transpose(psum[:, 6 + n, f * P:(f + 1) * P], w_int[:, n, f * P:(f + 1) * P], ident).then_inc(s_turned, 1)
            pe.wait_ge(s_diagonal, 1)
            pe.matmul(psum[:, 0, 0:P], ones, diagonal[:, 0], start=True, stop=True).then_inc(s_spread, 1)
            pe.wait_ge(s_w_bf, 2)
            with pe.Fori(0, PAIRS) as i:
                for u in range(2):
                    pe.wait_ge(s_x_int, i * 2 + u + 1)
                    for f in range(NF):
                        pe.matmul(psum[:, 4 * u + f], up[:, f * P:(f + 1) * P], x_int[:, u], start=True, stop=True).then_inc(s_up, 1)
            pe.wait_ge(s_diagonal, 2)
            pe.matmul(psum[:, 1, 0:P], ones, diagonal[:, 1], start=True, stop=True).then_inc(s_spread, 1)
            pe.wait_ge(s_diagonal, 4)
            for n in range(2):
                pe.matmul(psum[:, 2, n * P:(n + 1) * P], ones, diagonal[:, 2 + n], start=True, stop=True).then_inc(s_spread, 1)
            with pe.Fori(0, PAIRS) as i:
                for u in range(2):
                    pe.wait_ge(s_h_int, i * 2 + u + 1)
                    for k in range(TPC):
                        for f in range(NF):
                            last = pe.matmul(psum[:, 4 + u, k * P:(k + 1) * P], h_int[:, u, f, k * P:(k + 1) * P],
                                             down[:, f * P:(f + 1) * P], start=(f == 0), stop=(f == NF - 1))
                    last.then_inc(s_down, 1)

        @block.scalar
        def _(act):
            magic = core.const("magic")
            act.wait_ge(s_turned, 2 * NF)
            act.activation(up[:], psum[:, 6], ACT.Copy).then_inc(s_w_bf, 1)
            act.activation(down[:], psum[:, 7], ACT.Copy).then_inc(s_w_bf, 1)
            act.wait_ge(s_ready, 1)
            with act.Fori(0, PAIRS) as i:
                for u in range(2):
                    act.wait_ge(s_shift, i * 2 + u + 1)
                    act.activation(x_int[:, u], shifted[:, u], ACT.Identity, bias=magic).then_inc(s_x_int, 1)
                for u in range(2):
                    for f in range(NF):
                        gate(act, s_up, (i * 2 + u) * NF + f + 1, passed_act)
                        act.activation(H[:, f, bass.ds((i * 2 + u) * CHUNK, CHUNK)], psum[:, 4 * u + f], ACT.Relu,
                                       scale=s_out[:, f:f + 1], bias=bq[:, f:f + 1]).then_inc(s_H, 1)
            with act.Fori(0, PAIRS) as i:
                for u in range(2):
                    act.wait_ge(s_shift2, i * 2 + u + 1)
                    act.activation(h_int[:, u], shifted2[:, u], ACT.Identity, bias=magic).then_inc(s_h_int, 1)
        sc.close_block()



DEPTH = 6
ATTN_WIDTH, FFN_WIDTH = 5 * P + 2, 8 * P + 2


def linear_transformer(core, name, stream):
    nc, X = core.nc, core.X
    ident = core.const("ident")
    HEADS, DH = 8, P // 8
    NF = 4
    with Scope(core, name) as sc:
        psum = sc.banks()
        attn_w = sc.sb("attn_w", [P, ATTN_WIDTH])
        ffn_w = sc.sb("ffn_w", [P, FFN_WIDTH])
        wq, wk, wv, wo, bo = (attn_w[:, n * P:(n + 1) * P] for n in range(5))
        ln1, ln2 = attn_w[:, 5 * P:5 * P + 2], ffn_w[:, 8 * P:8 * P + 2]
        norm0, norm1, norm2 = Norm(sc, "ln0", "eps5"), Norm(sc, "ln1", "eps5"), Norm(sc, "ln2", "eps5")
        Y1, Y2 = sc.sb("normed1", [P, TPC, P]), sc.sb("normed2", [P, TPC, P])
        hT1, hT2 = sc.sb("hT1", [P, CHUNK]), sc.sb("hT2", [P, CHUNK])
        q, k = sc.sb("q", [P, CHUNK]), sc.sb("k", [P, CHUNK])
        q_stat, k_stat = sc.sb("q_stat", [P, 3, TPC * HEADS]), sc.sb("k_stat", [P, 3, CHUNK // S])
        k_tok, qT = sc.sb("k_tok", [P, CHUNK]), sc.sb("qT", [P, CHUNK])
        v_own = sc.sb("v_own", [P, TPC, BPT, P])
        ctx = sc.sb("ctx", [P, 2, BPT, P])
        aT = sc.sb("aT", [P, CHUNK])
        hidden = sc.sb("hidden", [P, NF, CHUNK])
        s_attn_w, s_ffn_w, s_zero = sc.sem("attn_w"), sc.sem("ffn_w"), sc.sem("zero")
        s_norm0, s_norm1, s_norm2 = sc.sem("norm0"), sc.sem("norm1"), sc.sem("norm2")
        s_turn1, s_turn2, s_hT1, s_hT2 = sc.sem("turn1"), sc.sem("turn2"), sc.sem("hT1"), sc.sem("hT2")
        s_proj, s_v = sc.sem("proj"), sc.sem("v")
        s_less, s_exp, s_soft, s_soft_link = sc.sem("less"), sc.sem("exp"), sc.sem("soft"), sc.sem("soft_link")
        s_k_turn, s_q_turn, s_k_tok, s_qT = sc.sem("k_turn"), sc.sem("q_turn"), sc.sem("k_tok"), sc.sem("qT")
        s_ctx, s_own, s_a, s_aT = sc.sem("ctx"), sc.sem("own"), sc.sem("a"), sc.sem("aT")
        s_bo, s_wo, s_mid = sc.sem("bo"), sc.sem("wo"), sc.sem("mid")
        s_slope = sc.sem("slope")
        s_up, s_hidden, s_down, s_layer = sc.sem("up"), sc.sem("hidden"), sc.sem("down"), sc.sem("layer")
        passed_dve = sc.sem("passed_dve")
        attn_dram, ffn_dram = core.packs["l_attn"][0], core.packs["l_ffn"][0]
        tiles = lambda ap: ap.rearrange("p (t c) -> p t c", c=P)
        block = sc.open_block()

        def layers(eng, A, F, both, layer_starts=None, layer_ends=None):
            with eng.Fori(0, DEPTH) as d:
                if layer_starts:
                    layer_starts(d)
                A(0, d * CHUNKS)
                with eng.Fori(0, CHUNKS // 2 - 1) as i:
                    for m in range(2):
                        both((i * 2 + m + 1, d * CHUNKS + i * 2 + m + 1), (i * 2 + m, d * CHUNKS + i * 2 + m))
                both((CHUNKS - 1, d * CHUNKS + CHUNKS - 1), (CHUNKS - 2, d * CHUNKS + CHUNKS - 2))
                F(CHUNKS - 1, d * CHUNKS + CHUNKS - 1)
                if layer_ends:
                    layer_ends(d)

        def has_next(n):
            return not isinstance(n, int) or n + 1 < CHUNKS

        @block.sync
        def _(sp):
            sp.dma_start(attn_w[:], attn_dram[:, 0:ATTN_WIDTH]).then_inc(s_attn_w, 16)
            sp.dma_start(ffn_w[:], ffn_dram[:, 0:FFN_WIDTH]).then_inc(s_ffn_w, 16)
            with sp.Fori(1, DEPTH) as d:
                sp.wait_ge(s_mid, d * CHUNKS)
                sp.dma_start(attn_w[:], attn_dram[:, bass.ds(d * ATTN_WIDTH, ATTN_WIDTH)]).then_inc(s_attn_w, 16)
                sp.wait_ge(s_layer, d * CHUNKS)
                sp.dma_start(ffn_w[:], ffn_dram[:, bass.ds(d * FFN_WIDTH, FFN_WIDTH)]).then_inc(s_ffn_w, 16)

        @block.gpsimd
        def _(pool):
            pool.memset(v_own[:], 0.0).then_inc(s_zero, 1)
            with pool.Fori(0, CHUNKS // 2) as i:
                for u in range(2):
                    norm0.pool_rstd(pool, i * 2 + u, u)

            def add_bias(n, done):
                pool.wait_ge(s_norm1, done + 1)
                xc = stream[:, bass.ds(n * TPC, TPC)] if not isinstance(n, int) else stream[:, n * TPC:(n + 1) * TPC]
                pool.tensor_tensor(xc, xc, spread(bo, TPC, 1), ALU.add).then_inc(s_bo, 1)

            def A(n, done):
                norm1.pool_rstd(pool, done, 0)
                add_bias(n, done)
                norm1.pool_rstd(pool, done + 1, 0)

            def both(a, f):
                norm2.pool_rstd(pool, f[1], 0)
                add_bias(*a)
                if has_next(a[0]):
                    norm1.pool_rstd(pool, a[1] + 1, 0)

            layers(pool, A, lambda n, done: norm2.pool_rstd(pool, done, 0), both,
                   layer_starts=lambda d: pool.wait_ge(s_attn_w, d * 16 + 16))

        @block.tensor
        def _(pe):
            def turn(Y, bank, s_from, s_to, done):
                pe.wait_ge(s_from, done + 1)
                for t in range(TPC):
                    last = pe.transpose(psum[:, bank, t * P:(t + 1) * P], Y[:, t], ident)
                last.then_inc(s_to, 1)

            def project(done, before=None):
                pe.wait_ge(s_hT1, done + 1)
                for bank, weight in ((1, wq), (3, wv)):
                    for t in range(TPC):
                        last = pe.matmul(psum[:, bank, t * P:(t + 1) * P], hT1[:, t * P:(t + 1) * P], weight,
                                         start=True, stop=True)
                    last.then_inc(s_proj, 1)
                if before is not None:
                    pe.wait_ge(s_mid, before + 1)
                pe.matmul(psum[:, 2], wk, hT1[:], start=True, stop=True).then_inc(s_proj, 1)

            def turn_soft(n, done):
                src, bank, s_to = ((k, 0, s_k_turn), (q, 2, s_q_turn))[n]
                pe.wait_ge(s_soft, done * 2 + n + 1)
                for t in range(TPC):
                    last = pe.transpose(psum[:, bank, t * P:(t + 1) * P], src[:, t * P:(t + 1) * P], ident)
                last.then_inc(s_to, 1)

            def context(t, done):
                if t == 0:
                    pe.wait_ge(s_v, done + 1)
                    pe.wait_ge(s_k_tok, done + 1)
                    pe.wait_ge(s_less, done * 2 + 2)
                if t >= 2:
                    pe.wait_ge(s_own, done * TPC + t - 1)
                pe.matmul(psum[:, 1 + 2 * (t % 2)], k_tok[:, t * P:(t + 1) * P], v_own[:, t].rearrange("p b c -> p (b c)"),
                          start=True, stop=True).then_inc(s_ctx, 1)

            def attend(t, done):
                pe.wait_ge(s_own, done * TPC + t + 1)
                if t == 0:
                    pe.wait_ge(s_qT, done + 1)
                for b in range(BPT):
                    sl = slice(t * P + b * S, t * P + (b + 1) * S)
                    last = pe.matmul(psum[:, 0, sl], ctx[:, t % 2, b], qT[:, sl], start=True, stop=True)
                last.then_inc(s_a, 1)

            def attn_out(done):
                pe.wait_ge(s_aT, done + 1)
                for t in range(TPC):
                    last = pe.matmul(psum[:, 2, t * P:(t + 1) * P], aT[:, t * P:(t + 1) * P], wo, start=True, stop=True)
                last.then_inc(s_wo, 1)

            def up(done):
                pe.wait_ge(s_hT2, done + 1)
                for f in range(NF):
                    pe.matmul(psum[:, 5 + f if f < 3 else 4], ffn_w[:, f * P:(f + 1) * P], hT2[:], start=True,
                              stop=True).then_inc(s_up, 1)

            def down(t, done):
                if t == 0:
                    pe.wait_ge(s_hidden, done * NF + NF)
                for f in range(NF):
                    last = pe.matmul(psum[:, 5, t * P:(t + 1) * P], hidden[:, f, t * P:(t + 1) * P],
                                     ffn_w[:, (NF + f) * P:(NF + f + 1) * P], start=(f == 0), stop=(f == NF - 1))
                if t == TPC - 1:
                    last.then_inc(s_down, 1)

            def A(n, done):
                turn(Y1, 0, s_norm1, s_turn1, done)
                project(done)
                turn_soft(0, done)
                context(0, done)
                context(1, done)
                turn_soft(1, done)
                for t in range(TPC):
                    attend(t, done)
                    if t + 2 < TPC:
                        context(t + 2, done)
                attn_out(done)

            def F(n, done):
                turn(Y2, 4, s_norm2, s_turn2, done)
                up(done)
                for t in range(TPC):
                    down(t, done)

            def both(a, f):
                a, f = a[1], f[1]
                turn(Y1, 0, s_norm1, s_turn1, a)
                project(a, before=f)
                turn(Y2, 4, s_norm2, s_turn2, f)
                up(f)
                turn_soft(0, a)
                context(0, a)
                context(1, a)
                turn_soft(1, a)
                for t in range(TPC):
                    down(t, f)
                    attend(t, a)
                    if t + 2 < TPC:
                        context(t + 2, a)
                attn_out(a)

            def weights_in(d):
                pe.wait_ge(s_attn_w, d * 16 + 16)
                pe.wait_ge(s_ffn_w, d * 16 + 16)

            layers(pe, A, F, both, layer_starts=weights_in)

        @block.scalar
        def _(act):
            act.wait_ge(s_zero, 1)

            def features(bank, out, ln, s_from, s_to, done):
                act.wait_ge(s_from, done + 1)
                act.activation(out, psum[:, bank], ACT.Identity, bias=ln[:, 1:2], scale=ln[:, 0:1]).then_inc(s_to, 1)

            def values_out(done):
                act.wait_ge(s_proj, done * 3 + 2)
                for b in range(BPT):
                    rows = slice(b * S, (b + 1) * S)
                    last = act.activation(v_own[rows, :, b], tiles(psum[:, 3])[rows], ACT.Copy)
                last.then_inc(s_v, 1)

            def exponential(n, done):
                act.wait_ge(s_less, done * 2 + n + 1)
                x = (k, q)[n][:]
                act.activation(x, x, ACT.Exp).then_inc(s_exp, 1)

            def slope(f, done):
                act.wait_ge(s_up, done * NF + f + 1)
                act.activation(hidden[:, f], psum[:, 5 + f if f < 3 else 4], ACT.Copy, scale=0.01).then_inc(s_slope, 1)

            def turned(bank, out, s_from, s_to, done):
                act.wait_ge(s_from, done + 1)
                act.activation(out, psum[:, bank], ACT.Copy).then_inc(s_to, 1)

            def rest(done):
                turned(0, k_tok[:], s_k_turn, s_k_tok, done)
                turned(2, qT[:], s_q_turn, s_qT, done)
                act.wait_ge(s_a, done * TPC + TPC)
                act.activation(aT[:], psum[:, 0], ACT.Copy).then_inc(s_aT, 1)

            def A(n, done):
                features(0, hT1[:], ln1, s_turn1, s_hT1, done)
                values_out(done)
                exponential(0, done)
                exponential(1, done)
                rest(done)

            def F(n, done):
                features(4, hT2[:], ln2, s_turn2, s_hT2, done)
                for f in range(NF):
                    slope(f, done)

            def both(a, f):
                a, f = a[1], f[1]
                features(0, hT1[:], ln1, s_turn1, s_hT1, a)
                values_out(a)
                features(4, hT2[:], ln2, s_turn2, s_hT2, f)
                exponential(0, a)
                slope(0, f)
                exponential(1, a)
                for m in range(1, NF):
                    slope(m, f)
                rest(a)

            def weights_in(d):
                act.wait_ge(s_attn_w, d * 16 + 16)
                act.wait_ge(s_ffn_w, d * 16 + 16)

            layers(act, A, F, both, layer_starts=weights_in)

        @block.vector
        def _(dve):
            with dve.Fori(0, CHUNKS // 2) as i:
                x_of = lambda u: (lambda t: X[:, bass.ds(i * 8 + u * 4 + t, 1)])
                for u in range(2):
                    norm0.dve_stats(dve, x_of(u), i * 2 + u, u)
                for u in range(2):
                    norm0.dve_apply(dve, lambda t: stream[:, bass.ds(i * 8 + u * 4 + t, 1)], x_of(u), i * 2 + u, u, s_norm0)
            dve.wait_ge(s_norm0, CHUNKS)
            dve.engine_nop()

            def part(n, t, count=1):
                at = n * TPC + t
                return stream[:, at:at + count] if isinstance(at, int) else stream[:, bass.ds(at, count)]

            def soften(m, done):
                bank, x, stat, width = ((2, k, k_stat, S), (1, q, q_stat, DH))[m]
                groups = x[:].rearrange("p (g w) -> p g w", w=width)
                source = psum[:, bank].rearrange("p (g w) -> p g w", w=width)
                dve.wait_ge(s_proj, done * 3 + (3, 1)[m])
                dve.tensor_reduce(stat[:, 0], source, AX.X, ALU.max).then_inc(s_soft_link, 1)
                dve.wait_ge(s_soft_link, done * 6 + m + 1)
                dve.tensor_tensor(groups, source, spread(stat[:, 0], width, 2), ALU.subtract).then_inc(s_less, 1)

            def normalise(m, done):
                x, stat, width = ((k, k_stat, S), (q, q_stat, DH))[m]
                groups = x[:].rearrange("p (g w) -> p g w", w=width)
                dve.wait_ge(s_exp, done * 2 + m + 1)
                dve.tensor_reduce(stat[:, 1], groups, AX.X, ALU.add).then_inc(s_soft_link, 1)
                dve.wait_ge(s_soft_link, done * 6 + 2 * m + 3)
                dve.reciprocal(stat[:, 2], stat[:, 1]).then_inc(s_soft_link, 1)
                dve.wait_ge(s_soft_link, done * 6 + 2 * m + 4)
                dve.tensor_tensor(groups, groups, spread(stat[:, 2], width, 2), ALU.mult).then_inc(s_soft, 1)

            def leaky(f, done):
                dve.wait_ge(s_slope, done * NF + f + 1)
                dve.tensor_tensor(hidden[:, f], psum[:, 5 + f if f < 3 else 4], hidden[:, f], ALU.max).then_inc(s_hidden, 1)

            def attention(n, done, ffn=None):
                soften(0, done)
                soften(1, done)
                if ffn is not None:
                    leaky(0, ffn)
                normalise(0, done)
                if ffn is not None:
                    leaky(1, ffn)
                normalise(1, done)
                if ffn is not None:
                    leaky(2, ffn)
                    leaky(3, ffn)
                for t in range(TPC):
                    if t in (1, 2) and has_next(n):
                        (next_stats if t == 1 else next_apply)(n + 1, done + 1)
                    dve.wait_ge(s_ctx, done * TPC + t + 1)
                    dve.tensor_tensor(ctx[:, t % 2], psum[:, 1 + 2 * (t % 2)].rearrange("p (b c) -> p b c", b=BPT),
                                      spread(core.const("same16"), BPT, 1), ALU.mult).then_inc(s_own, 1)

            def attention_added(n, done):
                dve.wait_ge(s_wo, done + 1)
                dve.wait_ge(s_bo, done + 1)
                dve.tensor_tensor(part(n, 0, TPC), tiles(psum[:, 2]), part(n, 0, TPC), ALU.add).then_inc(s_mid, 1)
                gate(dve, s_mid, done + 1, passed_dve)

            def ffn_added(n, done):
                dve.wait_ge(s_down, done + 1)
                dve.tensor_tensor(part(n, 0, TPC), tiles(psum[:, 5]), part(n, 0, TPC), ALU.add).then_inc(s_layer, 1)

            def stats(norm, n, done):
                norm.dve_stats(dve, lambda t: part(n, t), done, 0)

            def apply(norm, Y, s_norm, n, done):
                norm.dve_apply(dve, lambda t: Y[:, t:t + 1], lambda t: part(n, t), done, 0, s_norm)

            def next_stats(n, done):
                stats(norm1, n, done)

            def next_apply(n, done):
                apply(norm1, Y1, s_norm1, n, done)

            def A(n, done):
                next_stats(n, done)
                next_apply(n, done)
                attention(n, done)

            def F(n, done):
                attention_added(n, done)
                stats(norm2, n, done)
                apply(norm2, Y2, s_norm2, n, done)
                for f in range(NF):
                    leaky(f, done)
                ffn_added(n, done)

            def both(a, f):
                attention_added(*f)
                stats(norm2, *f)
                apply(norm2, Y2, s_norm2, *f)
                attention(*a, f[1])
                ffn_added(*f)

            layers(dve, A, F, both, layer_ends=lambda d: gate(dve, s_layer, d * CHUNKS + CHUNKS, passed_dve))
            dve.tensor_tensor(X[:], X[:], stream[:], ALU.add)
        sc.close_block()


def program(nc, x, out, const, packs, context, context32, mask):
    tiles_of = lambda a: a.rearrange("(t b) s d -> (b s) t d", b=BPT)
    with ExitStack() as ctx:
        X = ctx.enter_context(nc.sbuf_tensor("X", [P, TILES, P], F32))
        inner = ctx.enter_context(nc.sbuf_tensor("inner", [P, TILES, P], F32))
        const_sb = ctx.enter_context(nc.sbuf_tensor("const_sb", [P, CONST_WIDTH], F32))
        s_loaded = ctx.enter_context(nc.semaphore("loaded"))
        s_stored = ctx.enter_context(nc.semaphore("stored"))
        core = Core(nc, packs, X, const_sb)
        with nc.Block() as block:
            @block.sync
            def _(sp):
                sp.dma_start(const_sb[:], const).then_inc(s_loaded, 16)
                sp.dma_start(X[:], tiles_of(x)).then_inc(s_loaded, 16)
                sp.wait_ge(s_loaded, 32)
        r8 = 8 ** -0.5
        hT_all = core.hT_all = ctx.enter_context(nc.sbuf_tensor("hT_all", [P, TOK], F32))
        logits = ctx.enter_context(nc.sbuf_tensor("logits", [P, TILES, 8], F32))
        comb = ctx.enter_context(nc.sbuf_tensor("comb", [P, TILES, 8], F32))

        def moe(name, router, kind, gate_kind, E, nf, capacity=None, **more):
            with Scope(core, name + "_all") as sc:
                w, arrived, fetch = sc.weights(name)
                front(core, name + "_front", router, hT_all, logits=logits, prefetch=fetch, **more.pop("front", {}))
                gates(core, name + "_gates", logits, comb, gate_kind, capacity)
                experts(core, name, (w, arrived), hT_all, comb, E, nf, kind, **more)
                sc.clear()

        generated = ctx.enter_context(nc.sbuf_tensor("generated", [P, GEN_WIDTH + 4], F32))

        def generated_as(names):
            def at(name):
                start, width = names[name]
                return generated[:, start:start + width]
            return at

        def cross(name, scale, mask=None):
            front(core, name + "_front", lambda n: None, hT_all)
            cross_attention(core, name, name, hT_all, context, scale, mask)

        def quantised():
            front(core, "q_front", lambda n: None, hT_all)
            quantised_ffn(core, "q_ffn", "q_ffn", hT_all)

        def third_self():
            at = {n: a for n, (a, _) in GENERATED.items()}
            generate(core, "t_gen", "t_gen", generated)
            small_attention(core, "t_self", generated_as(dict(
                wq=(at["ca"], P), wk=(at["ca"] + P, P), wv=(at["ca"] + 2 * P, P), wo=(at["cp"], P), bq=(at["ca_b"], 1),
                bk=(at["ca_b"] + 1, 1), bv=(at["ca_b"] + 2, 1), bo=(at["cp_b"], P),
                ln_w=(GEN_WIDTH, 1), ln_b=(GEN_WIDTH + 1, 1))), 16, r8, mask="fill", second=("eps5", False), keep=inner)
            source = generated_as(dict(up=(at["cf"], 512), down=(at["cm"], 512), b1=(at["cf_b"], 4), bo=(at["cm_b"], P),
                                       ln_w=(GEN_WIDTH + 2, 1), ln_b=(GEN_WIDTH + 3, 1)))
            front(core, "t_front", source, hT_all, second=("eps5", False), keep=(inner, "source"))
            experts(core, "t_mlp", source, hT_all, None, 1, 4, "gelu_tanh", base=inner, out_bias=True)

        def fourth():
            small_attention(core, "u_self", "u_self", 16, r8, mask="causal", second=("eps6", True), keep=inner,
                            rotate=("rcos", "rsin", "rcos", "rsin"), qk_norm=True, post="gate")
            moe("u_moe", "u_router", "glu", "top1", 8, 2, base=inner, b2=True,
                front=dict(second=("eps6", True), keep=(inner, "source")))

        steps = {
            1: lambda: cross("a_cross", r8),
            7: lambda: cross("e_cross", r8),
            9: quantised,
            10: lambda: cross("t_cross", r8, mask),
            11: third_self,
            12: fourth,
            2: lambda: linear_transformer(core, "l", inner),
            3: lambda: moe("a_moe", "a_router", "silu", "probs", 8, 3, shared=True, front=dict(second=("eps5", False))),
            6: lambda: moe("c_moe", "c_router", "gelu", "capacity", 8, 4, capacity=1280),
            4: lambda: small_attention(core, "c_cross", "c_cross", 16, r8, context=context32, mask="causal"),
            5: lambda: small_attention(core, "c_self", "c_self", 16, r8),
            8: lambda: small_attention(core, "retention", "retention", 8, 1.0, mask="decay", softmax=False,
                                       rotate=("xcos_q", "xsin_q", "xcos_k", "xsin_k"), post="group_norm"),
        }
        for n in SUBLAYERS:
            steps[n]()
        with nc.Block() as block:
            @block.sync
            def _(sp):
                sp.dma_start(tiles_of(out), X[:]).then_inc(s_stored, 16)
                sp.wait_ge(s_stored, 16)



def column(v):
    return np.ascontiguousarray(v.reshape(-1, P).T)


def row(v):
    return np.broadcast_to(v[None], (P, v.shape[-1]))


def block_diagonal(w):
    h, d, _ = w.shape
    out = np.zeros((h * d, h * d), w.dtype)
    for n in range(h):
        out[n * d:(n + 1) * d, n * d:(n + 1) * d] = w[n]
    return out


ZERO_COLUMN, ZERO_ROW = np.zeros((P, 1), np.float32), np.zeros((P, P), np.float32)


def pack_inputs(v):
    neighbours = np.arange(P) ^ 1
    qkv, b_qkv = v["L1_attn_w_qkv"].T, column(v["L1_attn_b_qkv"])
    packs = {
        "c_cross": dict(wq=v["L1_xattn_q_w"], wk=v["L1_xattn_k_w"], wv=v["L1_xattn_v_w"], wo=v["L1_xattn_o_w"],
                        bq=column(v["L1_xattn_q_b"]), bk=column(v["L1_xattn_k_b"]), bv=column(v["L1_xattn_v_b"]),
                        bo=row(v["L1_xattn_o_b"])),
        "c_self": dict(wq=qkv[:, 0:P], wk=qkv[:, P:2 * P], wv=qkv[:, 2 * P:], wo=v["L1_attn_w_out"].T,
                       bq=b_qkv[:, 0:1], bk=b_qkv[:, 1:2], bv=b_qkv[:, 2:3], bo=row(v["L1_attn_b_out"])),
        "retention": dict(wq=block_diagonal(v["L2_attn_W_Q"]), wk=block_diagonal(v["L2_attn_W_K"]),
                          wv=block_diagonal(v["L2_attn_W_V"]), wg=v["L2_attn_W_G"], wo=v["L2_attn_W_O"],
                          wq_swap=block_diagonal(v["L2_attn_W_Q"])[:, neighbours],
                          wk_swap=block_diagonal(v["L2_attn_W_K"])[:, neighbours],
                          gn_w=column(v["L2_attn_gn_weight"]), gn_b=column(v["L2_attn_gn_bias"]),
                          bq=ZERO_COLUMN, bk=ZERO_COLUMN, bq_swap=ZERO_COLUMN, bk_swap=ZERO_COLUMN,
                          bv=ZERO_COLUMN, bo=ZERO_ROW),
    }
    packs["a_cross"] = dict(wq=v["L0_xattn_Wq"].T, wk=v["L0_xattn_Wkv"][0:P].T, wv=v["L0_xattn_Wkv"][P:].T,
                            wo=v["L0_xattn_Wout"].T, bq=ZERO_COLUMN, bk=ZERO_COLUMN, bv=ZERO_COLUMN,
                            bo=row(v["L0_xattn_bout"]))
    heads_side = lambda a: a.transpose(1, 0, 2).reshape(P, P)
    packs["e_cross"] = dict(wq=heads_side(v["L2_xattn_Wq"]), wk=heads_side(v["L2_xattn_Wk"]),
                            wv=heads_side(v["L2_xattn_Wv"]), wo=v["L2_xattn_Wo"].T, bq=ZERO_COLUMN, bk=ZERO_COLUMN,
                            bv=ZERO_COLUMN, bo=ZERO_ROW)
    packs["t_cross"] = dict(wq=v["L3_xattn_wq"].T, wk=v["L3_xattn_wk"].T, wv=v["L3_xattn_wv"].T, wo=v["L3_xattn_wo"].T,
                            bq=column(v["L3_xattn_bq"]), bk=column(v["L3_xattn_bk"]), bv=column(v["L3_xattn_bv"]),
                            bo=row(v["L3_xattn_bo"]))
    get = lambda kind, d: v["L0_attn_" + kind][d]
    packs["l_attn"] = {str(d): np.concatenate([get(kind, d) for kind in ("wq", "wk", "wv", "wo")] + [
        row(get("bo", d)), column(get("ln1_w", d)), column(get("ln1_b", d))], axis=1) for d in range(DEPTH)}
    packs["l_ffn"] = {str(d): np.concatenate([get("w1", d)] + [get("w2", d)[n * P:(n + 1) * P] for n in range(4)] + [
        column(get("ln2_w", d)), column(get("ln2_b", d))], axis=1) for d in range(DEPTH)}
    w1 = v["L2_ffn_w1"].reshape(4, P, P).transpose(1, 0, 2).reshape(P, 4 * P)
    packs["q_ffn"] = dict(w1=w1, w2=v["L2_ffn_w2"], b=np.concatenate([column(v["L2_ffn_b1"]), column(v["L2_ffn_b2"])], axis=1))
    gen = {}
    halves = lambda a: np.concatenate([a[:, n * P:(n + 1) * P].T for n in range(a.shape[1] // P)], axis=1)
    for part in ("sub0", "sub1", "W", "B"):
        get = lambda name, kind: (v[f"L3_attn_{name}_{part}_{kind}"] if part in "WB" else
                                  v[f"L3_attn_{name}_sub_{kind}"][int(part[3])])
        gen[part] = np.concatenate([get("ca", "w").T, get("cp", "w").T, get("cf", "w").T, halves(get("cm", "w")),
                                    column(get("ca", "b")), row(get("cp", "b")), column(get("cf", "b")),
                                    row(get("cm", "b"))], axis=1)
    gen["wl"] = np.concatenate([row(v[f"L3_attn_{n}_Wl_{k}"][0]) for k in "wb" for n in ("ca", "cp", "cf", "cm")], axis=1)
    gen["norms"] = np.stack([v["L3_attn_" + n] for n in ("ln1_g", "ln1_b", "ln2_g", "ln2_b")], axis=1)
    packs["t_gen"] = gen
    across, kv = np.arange(P) ^ 4, (np.arange(P) // 32) * 8 + np.arange(P) % 8
    f = lambda name: v["L3_ffn_" + name]
    packs["u_self"] = dict(wq=f("Wq"), wk=f("Wk")[:, kv], wv=f("Wv")[:, kv], wo=f("Wo"), wq_swap=f("Wq")[:, across],
                           wk_swap=f("Wk")[:, kv][:, across], bq=column(f("bq")), bk=column(f("bk")[kv]),
                           bv=column(f("bv")[kv]), bq_swap=column(f("bq")[across]), bk_swap=column(f("bk")[kv][across]),
                           bo=row(f("bo")), qn=column(np.tile(f("qn_w"), 16)), kn=column(np.tile(f("kn_w"), 16)),
                           wg=block_diagonal(np.broadcast_to(f("Wg"), (16, 8, 8))), bg=column(np.tile(f("bg"), 16)),
                           ln_w=column(f("ln1_w")), ln_b=ZERO_COLUMN)
    packs["u_router"] = dict(ln_w=column(f("ln2_w")), ln_b=ZERO_COLUMN, router=f("Wr"), router_b=row(f("br")))
    order = [(e, n, h) for e in range(8) for n in range(2) for h in range(2)]
    b2 = np.zeros((P, P), np.float32)
    b2[0:8] = f("b2")
    packs["u_moe"] = dict(up=np.concatenate([f("W1")[e][:, h * 256 + n * P:h * 256 + (n + 1) * P] for e, n, h in order], axis=1),
                          b1=np.stack([f("b1")[e, h * 256 + n * P:h * 256 + (n + 1) * P] for e, n, h in order], axis=1),
                          down=np.concatenate([f("W2")[e, n * P:(n + 1) * P] for e in range(8) for n in range(2)], axis=1), b2=b2)
    gu, sgu = v["L0_ffn_gate_up_w"], v["L0_ffn_shared_gate_up_w"]
    blocks = [gu[e, half * 384 + f * P:half * 384 + (f + 1) * P].T for e in range(8) for f in range(3) for half in range(2)]
    packs["a_router"] = dict(ln_w=column(v["L0_ffn_ln_gamma"]), ln_b=column(v["L0_ffn_ln_beta"]),
                             router=v["L0_ffn_router_w"].T, router_b=ZERO_ROW[:, 0:8])
    packs["a_moe"] = dict(up=np.concatenate(blocks + [sgu[0:P].T, sgu[P:].T], axis=1),
                          down=np.concatenate([v["L0_ffn_down_w"][e][:, f * P:(f + 1) * P].T for e in range(8) for f in range(3)]
                                              + [v["L0_ffn_shared_down_w"].T], axis=1))
    packs["c_router"] = dict(router=v["L1_ffn_w_g"], router_b=ZERO_ROW[:, 0:8])
    packs["c_moe"] = dict(up=np.concatenate(list(v["L1_ffn_c_fc"]), axis=1),
                          down=np.concatenate([v["L1_ffn_c_proj"][e, f * P:(f + 1) * P] for e in range(8) for f in range(4)], axis=1))
    return packs


def kernel(**inputs):
    import concourse.bacc as bacc
    from concourse.bass_utils import run_bass_kernel_spmd

    v = {name: np.asarray(a) for name, a in inputs.items()}
    nc = bacc.Bacc("TRN2", target_bir_lowering=False, num_devices=1)
    arrays = {}

    def dram(name, array):
        arrays[name] = np.ascontiguousarray(array)
        return nc.dram_tensor(name, arrays[name].shape, mybir.dt.from_np(arrays[name].dtype), kind="ExternalInput").ap()

    packs = {}
    for name, parts in pack_inputs(v).items():
        at, places = 0, {}
        for part, array in parts.items():
            places[part] = (at, array.shape[1])
            at += array.shape[1]
        packs[name] = (dram("pack_" + name, np.concatenate(list(parts.values()), axis=1)), places)
    x = dram("x", v["x"])
    const = dram("const", np.concatenate(list(CONSTANTS.values()), axis=1))
    context = v["ctx_1024"].transpose(2, 0, 1)
    context32 = dram("context32", context[:, :, 0:S].reshape(P, TOK))
    out = nc.dram_tensor("out", v["x"].shape, F32, kind="ExternalOutput").ap()
    program(nc, x, out, const, packs, dram("context", context), context32,
            dram("mask", v["mask_1x1xSxS2_ik0"][0, 0]))
    return run_bass_kernel_spmd(nc, [arrays], core_ids=[0]).results[0]["out"]
```
